# Optimizing a Trainium2 kernel written in Bass

```python
import numpy as np
import jax
import jax.numpy as jnp

def _softmax(x, axis=-1):
    return jax.nn.softmax(x, axis=axis)

def _gelu(x):
    return jax.nn.gelu(x, approximate=True)

def _silu(x):
    return jax.nn.silu(x)

def _sigmoid(x):
    return jax.nn.sigmoid(x)

def _layernorm(x, axis=-1, eps=1e-05):
    m = jnp.mean(x, axis=axis, keepdims=True)
    v = jnp.var(x, axis=axis, keepdims=True)
    return (x - m) / jnp.sqrt(v + eps)

def _scatter_add(tgt, idx, src, axis=0):
    return tgt.at[idx].add(src)

def _segment_sum(src, seg, n):
    return jax.ops.segment_sum(src, seg, n)
kernel_name = 'mk_gps_d1_gnn_r8_dc9ed9'

def setup_inputs(seed: int=0):
    np.random.seed(seed)
    _w = jnp.asarray

    def _rec_inputs():
        import jax
        import jax.numpy as jnp
        _gk = jax.random.key(seed)
        x = -0.0003713 + 1 * jax.random.normal(jax.random.fold_in(_gk, 1), (6250, 256), jnp.float32)
        src = jax.random.randint(jax.random.fold_in(_gk, 2), (100000,), 0, 6250, jnp.int32)
        dst = jnp.minimum((6250 * jax.random.uniform(jax.random.fold_in(_gk, 3), (100000,)) ** 2.0).astype(jnp.int32), 49999)
        _o = jnp.argsort(dst, stable=True)
        src = src[_o]
        dst = dst[_o]
        return (x, src, dst)
    x, src, dst = _rec_inputs()

    def _L0_gnn_setup():
        import jax, jax.numpy as jnp
        import numpy as np
        N_NODES = 6250
        N_EDGES = 100000
        IN_SIZE = 256
        OUT_SIZE = 256
        key = jax.random.key(seed)
        k1, k2, k3, k4, k5 = jax.random.split(key, 5)
        x = jax.random.normal(k1, (N_NODES, IN_SIZE), dtype=jnp.float32)
        bound = 1.0 / np.sqrt(IN_SIZE)
        W = jax.random.uniform(k2, (IN_SIZE, OUT_SIZE), minval=-bound, maxval=bound, dtype=jnp.float32)
        b = jax.random.uniform(k3, (OUT_SIZE,), minval=-bound, maxval=bound, dtype=jnp.float32)
        edge_src = jax.random.randint(k4, (N_EDGES,), 0, N_NODES, dtype=jnp.int32)
        edge_dst = jax.random.randint(k5, (N_EDGES,), 0, N_NODES, dtype=jnp.int32)
        return {'x': x, 'W': W, 'b': b, 'edge_src': edge_src, 'edge_dst': edge_dst}
    _L0_gnn_all = _L0_gnn_setup()
    _L0_gnn_in = {k: v for k, v in _L0_gnn_all.items() if k in ('W', 'b')}
    del _L0_gnn_all

    def _L0_mix_setup():
        import jax, jax.numpy as jnp
        import numpy as np
        D_MODEL = 256
        NUM_HEADS = 8
        DEPTH = D_MODEL // NUM_HEADS
        B, L = (32, 512)

        def _feature_map(x):
            return jax.nn.elu(x) + 1.0
        key = jax.random.key(seed)
        ks = jax.random.split(key, 9)
        sc = 1.0 / np.sqrt(D_MODEL)
        return {'x': jax.random.normal(ks[0], (B, L, D_MODEL), dtype=jnp.float32), 'wq': jax.random.normal(ks[1], (D_MODEL, D_MODEL), dtype=jnp.float32) * sc, 'bq': jnp.zeros((D_MODEL,), dtype=jnp.float32), 'wk': jax.random.normal(ks[2], (D_MODEL, D_MODEL), dtype=jnp.float32) * sc, 'bk': jnp.zeros((D_MODEL,), dtype=jnp.float32), 'wv': jax.random.normal(ks[3], (D_MODEL, D_MODEL), dtype=jnp.float32) * sc, 'bv': jnp.zeros((D_MODEL,), dtype=jnp.float32), 'wo': jax.random.normal(ks[4], (D_MODEL, D_MODEL), dtype=jnp.float32) * sc, 'bo': jnp.zeros((D_MODEL,), dtype=jnp.float32)}
    _L0_mix_all = _L0_mix_setup()
    _L0_mix_in = {k: v for k, v in _L0_mix_all.items() if k in ('wq', 'bq', 'wk', 'bk', 'wv', 'bv', 'wo', 'bo')}
    del _L0_mix_all

    def _L0_ffn_setup():
        import math
        import jax, jax.numpy as jnp
        import numpy as np
        CAPACITY_FACTOR = 1.25
        key = jax.random.key(seed)
        ks = jax.random.split(key, 5)
        B, L, D, F, E = (8, 1024, 256, 1024, 8)
        h = jax.random.normal(ks[0], (B, L, D), dtype=jnp.float32)
        gate_w = jax.random.normal(ks[1], (D, E), dtype=jnp.float32) * 0.02
        gate_b = jnp.zeros((E,), dtype=jnp.float32)
        w1 = jax.random.normal(ks[2], (E, D, F), dtype=jnp.float32) * (1.0 / math.sqrt(D))
        b1 = jnp.zeros((E, F), dtype=jnp.float32)
        w2 = jax.random.normal(ks[3], (E, F, D), dtype=jnp.float32) * (1.0 / math.sqrt(F))
        b2 = jnp.zeros((E, D), dtype=jnp.float32)
        return {'h': h, 'gate_w': gate_w, 'gate_b': gate_b, 'w1': w1, 'b1': b1, 'w2': w2, 'b2': b2}
    _L0_ffn_all = _L0_ffn_setup()
    _L0_ffn_in = {k: v for k, v in _L0_ffn_all.items() if k in ('gate_w', 'gate_b', 'w1', 'b1', 'w2', 'b2')}
    del _L0_ffn_all
    return {'x': x, 'src': src, 'dst': dst, 'L0_gnn_W': _L0_gnn_in['W'], 'L0_gnn_b': _L0_gnn_in['b'], 'L0_mix_wq': _L0_mix_in['wq'], 'L0_mix_bq': _L0_mix_in['bq'], 'L0_mix_wk': _L0_mix_in['wk'], 'L0_mix_bk': _L0_mix_in['bk'], 'L0_mix_wv': _L0_mix_in['wv'], 'L0_mix_bv': _L0_mix_in['bv'], 'L0_mix_wo': _L0_mix_in['wo'], 'L0_mix_bo': _L0_mix_in['bo'], 'L0_ffn_gate_w': _L0_ffn_in['gate_w'], 'L0_ffn_gate_b': _L0_ffn_in['gate_b'], 'L0_ffn_w1': _L0_ffn_in['w1'], 'L0_ffn_b1': _L0_ffn_in['b1'], 'L0_ffn_w2': _L0_ffn_in['w2'], 'L0_ffn_b2': _L0_ffn_in['b2']}

def reference(x, src, dst, L0_gnn_W, L0_gnn_b, L0_mix_wq, L0_mix_bq, L0_mix_wk, L0_mix_bk, L0_mix_wv, L0_mix_bv, L0_mix_wo, L0_mix_bo, L0_ffn_gate_w, L0_ffn_gate_b, L0_ffn_w1, L0_ffn_b1, L0_ffn_w2, L0_ffn_b2):
    import jax
    import jax.numpy as jnp

    def _L0_gnn_ref(x, W, b, edge_src, edge_dst):
        import jax, jax.numpy as jnp
        import numpy as np
        N_NODES = 6250
        N_EDGES = 100000
        IN_SIZE = 256
        OUT_SIZE = 256
        Wh = x @ W + b
        m = Wh[edge_src]
        summed = jax.ops.segment_sum(m, edge_dst, num_segments=N_NODES)
        deg = jax.ops.segment_sum(jnp.ones((edge_dst.shape[0],), dtype=x.dtype), edge_dst, num_segments=N_NODES)
        h = summed / jnp.maximum(deg, 1.0)[:, None]
        return h

    def _L0_mix_ref(x, wq, bq, wk, bk, wv, bv, wo, bo):
        import jax, jax.numpy as jnp
        import numpy as np
        D_MODEL = 256
        NUM_HEADS = 8
        DEPTH = D_MODEL // NUM_HEADS
        B, L = (32, 512)

        def _feature_map(x):
            return jax.nn.elu(x) + 1.0
        b, l, _ = x.shape
        q = (x @ wq + bq).reshape(b, l, NUM_HEADS, DEPTH)
        k = (x @ wk + bk).reshape(b, l, NUM_HEADS, DEPTH)
        v = (x @ wv + bv).reshape(b, l, NUM_HEADS, DEPTH)
        q = _feature_map(q)
        k = _feature_map(k)
        kv = jnp.einsum('blhd,blhe->bhde', k, v)
        k_sum = jnp.sum(k, axis=1)
        qkv = jnp.einsum('blhd,bhde->blhe', q, kv)
        normalizer = jnp.einsum('blhd,bhd->blh', q, k_sum) + 1e-06
        out = qkv / normalizer[..., None]
        out = out.reshape(b, l, D_MODEL)
        return out @ wo + bo

    def _L0_ffn_ref(h, gate_w, gate_b, w1, b1, w2, b2):
        import math
        import jax, jax.numpy as jnp
        import numpy as np
        CAPACITY_FACTOR = 1.25
        B, L, D = h.shape
        E = gate_w.shape[1]
        T = B * L
        C = max(1, math.ceil(CAPACITY_FACTOR * T / E))
        x = h.reshape(T, D)
        logits = x @ gate_w + gate_b
        probs = jax.nn.softmax(logits, axis=-1)
        idx = jnp.argmax(probs, axis=-1)
        prb = jnp.take_along_axis(probs, idx[:, None], axis=1)[:, 0]
        one_hot = jax.nn.one_hot(idx, E, dtype=jnp.float32)
        pos = (jnp.cumsum(one_hot, axis=0) * one_hot).sum(-1).astype(jnp.int32) - 1
        kept = pos < C
        pos_safe = jnp.where(kept, pos, C)
        buf = jnp.zeros((E, C, D), dtype=h.dtype).at[idx, pos_safe].set(x, mode='drop')
        hmid = jax.nn.relu(jnp.einsum('ecd,edf->ecf', buf, w1) + b1[:, None, :])
        ybuf = jnp.einsum('ecf,efd->ecd', hmid, w2) + b2[:, None, :]
        pos_g = jnp.minimum(pos, C - 1)
        y_tok = ybuf[idx, pos_g] * (prb * kept)[:, None]
        y = y_tok.reshape(B, L, D)
        y = jnp.nan_to_num(y, nan=0.0, posinf=10000.0, neginf=-10000.0)
        return y
    xn = _layernorm(x, axis=-1)
    x = x + _L0_gnn_ref(xn, L0_gnn_W, L0_gnn_b, src, dst) + _L0_mix_ref(xn[None], L0_mix_wq, L0_mix_bq, L0_mix_wk, L0_mix_bk, L0_mix_wv, L0_mix_bv, L0_mix_wo, L0_mix_bo)[0]
    x = x + _L0_ffn_ref(_layernorm(x, axis=-1)[None], L0_ffn_gate_w, L0_ffn_gate_b, L0_ffn_w1, L0_ffn_b1, L0_ffn_w2, L0_ffn_b2)[0]
    return x

_drawn_inputs = setup_inputs


def setup_inputs(seed=0):
    import zlib

    import numpy as np

    out = dict(_drawn_inputs(seed))
    spreads = {'L0_mix_bq': (0.0, 0.8),
     'L0_mix_bk': (0.0, 0.8),
     'L0_mix_bv': (0.0, 0.1),
     'L0_mix_bo': (0.0, 0.1),
     'L0_ffn_gate_b': (0.0, 0.1),
     'L0_ffn_b1': (0.0, 0.617),
     'L0_ffn_b2': (0.0, 0.438)}
    factors = {'L0_mix_wq': 5.956, 'L0_mix_wk': 3.626, 'L0_mix_wv': 2.972}
    for name, (base, spread) in spreads.items():
        noise = np.random.default_rng([zlib.crc32(name.encode()), seed]).standard_normal(out[name].shape)
        drawn = base * np.exp(spread * noise) if base else spread * noise
        out[name] = jnp.asarray(drawn.astype(out[name].dtype))
    for name, factor in factors.items():
        out[name] = (out[name] * factor).astype(out[name].dtype)
    return out
```

```python
from contextlib import ExitStack

import concourse.bass as bass
from concourse import mybir

F32 = mybir.dt.float32
F16 = mybir.dt.float16
I32 = mybir.dt.int32
ALU = mybir.AluOpType
ACT = mybir.ActivationFunctionType
AX = mybir.AxisListType.X

P = 128
D = 256
DK = D // P
HEADS = 8
HD = D // HEADS
HB = P // HD
N = 6250
NT = -(-N // P)
LAST = N - (NT - 1) * P
E = 100000
EC = -(-E // P)
RING = 16
EB = -(-EC // RING)
ECP = EB * RING
EBLK = -(-ECP // P)
OH = 8
NB = 4
NX = 8
F = 1024
FC = F // P
CAP = 977
SLOTS = 1024
JOBS = SLOTS // P
LO = 2048.0
ROW = D + 4
C_RSTD, C_NMR, C_PRB, C_TOK = D, D + 1, D + 2, D + 3
LAG = 4
BIG = 1.0e6
EPS = 1e-5
PAD_DST = 100000.0


def gps_block(nc, x, src, dst, gnn_w, gnn_b, wq, bq, wk, bk, wv, bv, wo, bo,
              gate_w, gate_b, w1, b1, w2, b2, out):
    table = nc.dram_tensor("table", [NT * P, 2 * D], F16).ap()
    normed_t = nc.dram_tensor("normed_t", [NT, P, DK * P], F32).ap()
    rows = nc.dram_tensor("rows", [NX * SLOTS, ROW], F32).ap()
    rows_t = rows.rearrange("(s p) d -> s p d", p=P)
    x_t = x[0:(NT - 1) * P, :].rearrange("(t p) d -> t p d", p=P)
    out_t = out[0:(NT - 1) * P, :].rearrange("(t p) d -> t p d", p=P)

    with ExitStack() as ctx:
        def sb(name, shape, dt=F32):
            return ctx.enter_context(nc.sbuf_tensor(name, shape, dt))

        def bank(name):
            return ctx.enter_context(nc.psum_tensor(name, [P, 512], F32))

        def sem(name):
            return ctx.enter_context(nc.semaphore(name))

        w1s = sb("w1s", [P, NX, DK, F])
        w2s = sb("w2s", [P, NX, FC, D])
        b1s = sb("b1s", [P, NX * FC])
        b2s = sb("b2s", [P, NX, D])
        wkv = sb("wkv", [P, DK, 2 * D])
        wqs = sb("wqs", [P, DK, D])
        wos = sb("wos", [P, DK, D])
        wgs = sb("wgs", [P, DK, D])
        gws = sb("gws", [P, DK, NX])
        hs = sb("hs", [P, FC, P])
        bks = hs[:, 0:2, :].rearrange("p a b -> p (a b)")
        bvs = hs[:, 2:4, :].rearrange("p a b -> p (a b)")
        bos = sb("bos", [P, D])
        bgs = sb("bgs", [P, D])
        bqs = sb("bqs", [P, DK])
        gbs = sb("gbs", [P, NX])
        ident = sb("ident", [P, P])
        tri = sb("tri", [P, P])
        tri16 = sb("tri16", [P, P], F16)
        ones16 = sb("ones16", [P, P], F16)
        zero16 = sb("zero16", [P, 512], F16)
        iota_row = sb("iota_row", [P, P])
        iota_i = sb("iota_i", [P, P], I32)
        expert_m8 = sb("expert_m8", [P, NX])
        eps = sb("eps", [P, 1])

        src_t = sb("src_t", [P, EBLK * P], I32)
        dst_t = sb("dst_t", [P, EBLK * P])
        cmin = sb("cmin", [P, EBLK])
        cmax = sb("cmax", [P, EBLK])
        chunk_id = sb("chunk_id", [P, EBLK])
        chunk_i = sb("chunk_i", [P, EBLK], I32)
        bounds = sb("bounds", [P, 2, NT])
        lohi = sb("lohi", [NT, 2])
        lh_row = sb("lh_row", [1, 2, 64])
        new_row = sb("new_row", [1, 64])
        new_col = sb("new_col", [NT, 1])
        base_row = sb("base_row", [1, 64])
        spans = sb("spans", [1, 5, 64], I32)
        idx = sb("idx", [P, RING], I32)
        gathered = sb("gathered", [P, RING, 2 * D], F16)
        onehot = sb("onehot", [P, OH, P], F16)
        tile_iota = sb("tile_iota", [P, P])

        ring32 = gathered[:, :, :].rearrange("p a b -> p (a b)").bitcast(F32)
        xin = ring32[:, 0:2 * NB * D].rearrange("p (a b c) -> p a b c", a=2, b=NB)
        stats = sb("stats", [P, NB, 6])
        mv = sb("mv", [P, NB, 2])
        std = sb("std", [P, NB])
        rstd = sb("rstd", [P, NB])
        xn = sb("xn", [P, NB, D])
        trow = ring32[:, 2 * NB * D:3 * NB * D].bitcast(F16).rearrange("p (b d) -> p b d", b=NB)
        xt = ring32[:, 3 * NB * D:4 * NB * D].rearrange("p (b d) -> p b d", b=NB)
        dif = sb("dif", [P, NB, D])
        kvw = sb("kvw", [P, 4, D])
        kb, km, kr, ke = kvw[:, 0, :], kvw[:, 1, :], kvw[:, 2, :], kvw[:, 3, :]
        kk = sb("kk", [P, D])
        vv = sb("vv", [P, DK, P + 1])
        kvm = sb("kvm", [P, DK, P + HB])

        xtin = dif[:, 0:2, :]
        xres = dif[:, 2:4, :]
        qr, qm, qe, qt = xn[:, 0, :], xn[:, 1, :], xn[:, 2, :], xn[:, 3, :]
        rden = sb("rden", [P, HEADS])
        o_sb, ot = kvw[:, 0, :], kvw[:, 1, :]
        deg = sb("deg", [P, 4])
        agg, agt = kvw[:, 2, :], kvw[:, 3, :]
        xb = kk[:, :]
        rows_sb = sb("rows_sb", [P, 2, ROW])
        slot2 = sb("slot2", [P, 2], I32)
        x2 = wkv[:, 0, 0:D]
        x2t = wkv[:, 0, D:2 * D]
        lg = sb("lg", [P, 6, NX])
        sc = sb("sc", [P, 12])
        oh16 = sb("oh16", [P, NX], F16)
        cnt16 = sb("cnt16", [P, NX], F16)
        tok = sb("tok", [P, 1])

        jrow = sb("jrow", [P, 2, ROW])
        xj, xjt = xn[:, 0, :], xn[:, 1, :]
        y = sb("y", [P, 3, D])
        fin = wkv[:, 1, :].rearrange("p (a d) -> p a d", a=2)
        jtok = sb("jtok", [P, 2], I32)

        pA = bank("pA")
        pD = bank("pD")
        pT = bank("pT")
        pQ = bank("pQ")
        pH0 = bank("pH0")
        pH1 = bank("pH1")
        pY = bank("pY")
        pS = bank("pS")

        names = """w_edge w_qkv w_big consts iota_ok ident_ok
          e_src e_dst e_padded e_f32 e_ps e_copied e_bound e_bt e_lohi e_rowps e_row e_newps e_new e_baseps spans_ok idx_ok row_stored row_free fin_free
          x_in x_out ln_stats ln_std ln_xn ln_hi ln_dif ln_lo tab_st tab_free xt_ps xt_sb xt_st xt_free kv_ps kb_ok v_ok kr_ok km_ok ke_ok kk_ok
          kv_used kv_sum kvm_ok kvm_z rows_z rows_init
          slots passed relayed oh_slots oh_ready agg_done agg_used
          p2_in p2_free q_ps qr_ok qm_ok qe_ok qt_ok att_ps o_ok ot_ps ot_sb s_ok agg_ok agt_ps agt_sb x1_ps x1_ok
          st_ok sd_ok x2_ok x2t_ps x2t_sb lg_ps nmx_ok ex_ok oh_ok pos_ps row_ok row_st scat_done out_st
          j_in j_free xj_ok xjt_ps xjt_sb h0_ps h1_ps h0_sb h1_sb y_ps fin_ok fin_sc dve_c
          sp_hold act_hold dve_hold pool_hold pe_hold""".split()
        S = {n: sem(n) for n in names}
        landed = [sem(f"landed{j}") for j in range(RING)]
        block = ctx.enter_context(nc.Block())

        class Chain:
            def __init__(self, eng, s, at=0):
                self.eng, self.s, self.n, self.at = eng, s, 0, at

            def __call__(self, ins):
                ins.then_inc(self.s, 1)
                self.n += 1
                self.eng.wait_ge(self.s, self.at + self.n)

            def mark(self, ins):
                ins.then_inc(self.s, 1)
                self.n += 1

            def wait(self):
                self.eng.wait_ge(self.s, self.at + self.n)

        def hold(eng, name):
            eng.sem_inc(S[name], 1)

        def xin_f(a):
            g = ring32[:, 2 * NB * D:4 * NB * D]
            return g[:, a * EBLK * P:(a + 1) * EBLK * P].rearrange("p (b e) -> p b e", e=P)

        @block.sync
        def _(sp):
            full = (E // P // P) * P * P
            mid = E // P * P
            sp.wait_ge(S["e_padded"], 2)
            for a, name in ((0, "e_dst"), (1, "e_src")):
                v = dst if a == 0 else src
                t = xin[:, :, :, :].rearrange("p a b c -> p (a b c)").bitcast(I32)[:, a * 1024:a * 1024 + EBLK * P]
                t = t.rearrange("p (b e) -> p b e", e=P)
                sp.dma_start(t[:, 0:full // P // P, :], v[0:full].rearrange("(b r e) -> r b e", r=P, e=P)).then_inc(S[name], 16)
                sp.dma_start(t[0:(mid - full) // P, EBLK - 1, :], v[full:mid].rearrange("(r e) -> r e", e=P)).then_inc(S[name], 16)
                sp.dma_start(t[(mid - full) // P:(mid - full) // P + 1, EBLK - 1, 0:E - mid],
                             v[mid:E].rearrange("(a e) -> a e", a=1)).then_inc(S[name], 16)
            sp.dma_start(wkv[:, :, 0:D], wk.rearrange("(k p) n -> p k n", p=P)).then_inc(S["w_qkv"], 16)
            sp.dma_start(wkv[:, :, D:2 * D], wv.rearrange("(k p) n -> p k n", p=P)).then_inc(S["w_qkv"], 16)
            for t, v in ((wqs, wq), (wos, wo), (wgs, gnn_w)):
                sp.dma_start(t[:, :, :], v.rearrange("(k p) n -> p k n", p=P)).then_inc(S["w_qkv"], 16)
            sp.dma_start(gws[:, :, :], gate_w.rearrange("(k p) n -> p k n", p=P)).then_inc(S["w_qkv"], 16)
            for t, v in ((bks, bk), (bvs, bv), (bos, bo), (bgs, gnn_b), (gbs, gate_b)):
                sp.dma_start(t[:, :], v.partition_broadcast(P)).then_inc(S["w_qkv"], 16)
            with nc.allow_non_contiguous_dma(reason="per-partition bias columns"):
                sp.dma_start(bqs[:, :], bq.rearrange("(k p) -> p k", p=P)).then_inc(S["w_qkv"], 16)

            def load(i, nb, rows_n):
                t0 = i * NB
                if nb == NB:
                    sp.dma_start(xin[:, i % 2, :, :], x_t[bass.ds(t0, NB), :, :].rearrange("t p d -> p t d")).then_inc(S["x_in"], 16)
                else:
                    sp.dma_start(xin[0:rows_n, i % 2, 0, :], x[(NT - 1) * P:N, :]).then_inc(S["x_in"], 16)

            tab_v = table.rearrange("(t p) d -> t p d", p=P)
            nbat = NT // NB
            sp.sem_inc(S["xt_free"], 1)
            sp.sem_inc(S["tab_free"], 1)
            sp.wait_ge(S["e_copied"], 2)
            load(0, NB, P)
            sp.wait_ge(S["x_in"], 16)

            def batch(i, more):
                sp.wait_ge(S["x_out"], i + 1)
                hold(sp, "sp_hold")
                if more:
                    load(i + 1, NB, P)
                else:
                    load(i + 1, 1, LAST)
                sp.wait_ge(S["xt_sb"], i * NB + NB)
                sp.dma_start(normed_t[bass.ds(i * NB, NB), :, :].rearrange("t p n -> p t n"), xt[:, :, :]).then_inc(S["xt_st"], 16)
                sp.wait_ge(S["ln_lo"], i * NB + NB)
                sp.dma_start(tab_v[bass.ds(i * NB, NB), :, :].rearrange("t p d -> p t d"), trow[:, :, :]).then_inc(S["tab_st"], 16)
                sp.wait_ge(S["xt_st"], i * 16 + 16)
                sp.sem_inc(S["xt_free"], 1)
                sp.wait_ge(S["tab_st"], i * 16 + 16)
                sp.sem_inc(S["tab_free"], 1)
                sp.wait_ge(S["x_in"], i * 16 + 32)
                hold(sp, "sp_hold")

            with sp.Fori(0, nbat - 1) as i:
                batch(i, True)
            batch(nbat - 1, False)
            sp.wait_ge(S["xt_sb"], NT)
            sp.dma_start(normed_t[NT - 1, :, :], xt[:, 0, :]).then_inc(S["xt_st"], 16)
            sp.wait_ge(S["ln_lo"], NT)
            sp.dma_start(tab_v[NT - 1, :, :], trow[:, 0, :]).then_inc(S["tab_st"], 16)
            sp.wait_ge(S["xt_st"], 16 * (nbat + 1))

            sp.wait_ge(S["kk_ok"], NT)
            sp.dma_start(xtin[:, 0, :], normed_t[0, :, :]).then_inc(S["p2_in"], 16)
            sp.dma_start(xres[:, 0, :], x_t[0, :, :]).then_inc(S["p2_in"], 16)

            def node_io(t, more):
                sp.wait_ge(S["p2_in"], t * 32 + 32)
                hold(sp, "sp_hold")
                sp.wait_ge(S["p2_free"], t + 1)
                hold(sp, "sp_hold")
                sp.dma_start(xtin[:, (t + 1) % 2, :], normed_t[bass.ds(t + 1, 1), :, :].rearrange("t p n -> p (t n)")).then_inc(S["p2_in"], 16)
                if more:
                    sp.dma_start(xres[:, (t + 1) % 2, :], x_t[bass.ds(t + 1, 1), :, :].rearrange("t p d -> p (t d)")).then_inc(S["p2_in"], 16)
                else:
                    sp.dma_start(xres[0:LAST, (t + 1) % 2, :], x[(NT - 1) * P:N, :]).then_inc(S["p2_in"], 16)
                sp.wait_ge(S["x1_ok"], t + 1)
                sp.dma_start(out_t[bass.ds(t, 1), :, :].rearrange("t p d -> p (t d)"), rows_sb[:, t % 2, 0:D]).then_inc(S["row_st"], 16)
                sp.wait_ge(S["row_st"], t * 16 + 16)
                sp.sem_inc(S["row_stored"], 1)

            with sp.Fori(0, NT - 2) as t:
                node_io(t, True)
            node_io(NT - 2, False)
            sp.wait_ge(S["x1_ok"], NT)
            sp.dma_start(out[(NT - 1) * P:N, :], rows_sb[0:LAST, (NT - 1) % 2, 0:D]).then_inc(S["row_st"], 16)
            sp.wait_ge(S["row_st"], 16 * NT)

            sp.wait_ge(S["scat_done"], 16 * NT)
            with sp.Fori(0, NX * JOBS) as j:
                sp.wait_ge(S["j_free"], j + 1)
                sp.dma_start(jrow[:, j % 2, :], rows_t[bass.ds(j, 1), :, :].rearrange("t p d -> p (t d)")).then_inc(S["j_in"], 16)
                sp.wait_ge(S["j_in"], j * 16 + 16)
                hold(sp, "sp_hold")
            sp.wait_ge(S["fin_sc"], 16 * NX * JOBS)
            sp.wait_ge(S["tab_st"], 16 * (nbat + 1))

        @block.gpsimd
        def _(g):
            edges = xin[:, :, :, :].rearrange("p a b c -> p (a b c)").bitcast(I32)
            g.memset(edges[:, 0:1024], int(PAD_DST)).then_inc(S["e_padded"], 1)
            g.memset(edges[:, 1024:2048], 0).then_inc(S["e_padded"], 1)
            g.iota(iota_i[:, :], [[1, P]], base=0, channel_multiplier=0).then_inc(S["iota_ok"], 1)
            g.iota(chunk_i[:, :], [[P, EBLK]], base=0, channel_multiplier=1).then_inc(S["iota_ok"], 1)
            g.memset(ident[:, :], 0.0).then_inc(S["consts"], 1)
            g.memset(tri[:, :], 1.0).then_inc(S["consts"], 1)
            g.memset(ones16[:, :], 1.0).then_inc(S["consts"], 1)
            g.memset(zero16[:, :], 0.0).then_inc(S["consts"], 1)
            g.memset(eps[:, :], EPS).then_inc(S["consts"], 1)
            g.memset(vv[:, :, :], 1.0).then_inc(S["consts"], 1)
            g.wait_ge(S["consts"], 6)
            g.affine_select(out=ident[:, :], in_=ident[:, :], compare_op=ALU.not_equal, fill=1.0, base=0,
                            pattern=[[-1, P]], channel_multiplier=1).then_inc(S["ident_ok"], 1)
            g.affine_select(out=tri[:, :], in_=tri[:, :], compare_op=ALU.is_ge, fill=0.0, base=0,
                            pattern=[[1, P]], channel_multiplier=-1).then_inc(S["ident_ok"], 1)

            def keys(t, j):
                g.wait_ge(S["ln_hi"], t + 1)
                g.tensor_tensor(dif[:, j, :], xn[:, j, :], trow[:, j, 0:D], ALU.subtract).then_inc(S["ln_dif"], 1)

            def keys2(t):
                g.wait_ge(S["kv_used"], t + 1)
                hold(g, "pool_hold")
                g.wait_ge(S["ke_ok"], t + 1)
                g.tensor_tensor(kk[:, :], kr, ke, ALU.add).then_inc(S["kk_ok"], 1)

            with g.Fori(0, NT // NB) as i:
                for j in range(NB):
                    keys(i * NB + j, j)
                for j in range(NB):
                    keys2(i * NB + j)
            keys(NT - 1, 0)
            keys2(NT - 1)

            g.wait_ge(S["rows_z"], 1)
            g.dma_start(rows_t.rearrange("s p d -> p s d"), jrow[:, 0:1, :].broadcast_to([P, NX * JOBS, ROW])).then_inc(S["rows_init"], 16)
            g.wait_ge(S["rows_init"], 16)

            def scatter(t):
                g.wait_ge(S["row_ok"], t + 1)
                hold(g, "pool_hold")

                def send(b):
                    g.indirect_dma_start(rows[:, :], bass.IndirectOffsetOnAxis(ap=slot2[:, b:b + 1], axis=0), rows_sb[:, b, :], None,
                                         bounds_check=NX * SLOTS - 1, oob_is_err=False).then_inc(S["scat_done"], 16)
                with g.If(t % 2 < 1):
                    send(0)
                with g.Else():
                    send(1)
                g.wait_ge(S["scat_done"], t * 16 + 16)
                g.sem_inc(S["row_free"], 1)

            g.wait_ge(S["tab_st"], 16 * (NT // NB + 1))
            g.wait_ge(S["xt_st"], 16 * (NT // NB + 1))
            g.wait_ge(S["spans_ok"], 1)
            ends = [g.value_load(spans[0:1, 4, 0:1], min_val=EB, max_val=EB * NT)]

            def events(tile, tend, f):
                with g.While(lambda: g.snap(tend) < f - (RING - LAG)):
                    scatter(g.snap(tile))
                    g.reg_add(tile, tile, 1)
                    g.load(tend, spans[0:1, 1, bass.ds(g.snap(tile), 1)])
                g.sem_inc(S["pool_hold"], 1)

            def round_(i, first, tile=None, tend=None):
                half = RING // 2
                for j in range(RING):
                    if j % half == 0:
                        g.tensor_copy(idx[:, j:j + half], src_t[:, bass.ds((i % EB) * RING + j, half)]).then_inc(S["idx_ok"], 1)
                        g.wait_ge(S["idx_ok"], i * 2 + j // half + 1)
                        hold(g, "pool_hold")
                    if j % LAG == 0 and not first:
                        events(tile, tend, i * RING + j)
                    g.wait_ge(S["slots"], i * RING + j + 1)
                    hold(g, "pool_hold")
                    g.indirect_dma_start(gathered[:, j, :], None, table[:, :],
                                         bass.IndirectOffsetOnAxis(ap=idx[:, j:j + 1], axis=0)).then_inc(landed[j], 16)
                    if not (first and j < LAG):
                        g.wait_ge(landed[(j - LAG) % RING], (i + 1) * 16 if j >= LAG else i * 16)
                    g.sem_inc(S["relayed"], 1)

            round_(0, True)
            with g.register("tile_no") as tile, g.register("tile_end") as tend:
                g.reg_mov(tile, 0)
                g.load(tend, spans[0:1, 1, 0:1])
                with g.Fori(1, ends[0]) as i:
                    round_(i, False, tile, tend)
                for j in range(RING - LAG, RING):
                    g.wait_ge(landed[j], ends[0] * 16)
                    g.sem_inc(S["relayed"], 1)
                with g.Fori(g.snap(tile), NT) as t:
                    scatter(t)

            with g.Fori(0, NX * JOBS // 2) as i:
                for b in range(2):
                    g.wait_ge(S["fin_ok"], i * 2 + b + 1)
                    hold(g, "pool_hold")
                    g.indirect_dma_start(out[:, :], bass.IndirectOffsetOnAxis(ap=jtok[:, b:b + 1], axis=0),
                                         fin[:, b, :], None,
                                         bounds_check=N - 1, oob_is_err=False).then_inc(S["fin_sc"], 16)
                    g.wait_ge(S["fin_sc"], i * 32 + b * 16 + 16)
                    g.sem_inc(S["fin_free"], 1)

        @block.scalar
        def _(a):
            for e in range(NX):
                a.dma_start(w1s[:, e, :, :], w1[e, :, :].rearrange("(k p) f -> p k f", p=P)).then_inc(S["w_big"], 16)
                a.dma_start(w2s[:, e, :, :], w2[e, :, :].rearrange("(c p) d -> p c d", p=P)).then_inc(S["w_big"], 16)
            with nc.allow_non_contiguous_dma(reason="hidden bias to columns"):
                a.dma_start(b1s[:, :], b1.rearrange("e (c p) -> p (e c)", p=P)).then_inc(S["w_big"], 16)
            a.dma_start(b2s[:, :, :].rearrange("p e d -> p (e d)"), b2.rearrange("e d -> (e d)").partition_broadcast(P)).then_inc(S["w_big"], 16)

            a.wait_ge(S["consts"], 6)

            def norm(i, nb):
                t0 = i * NB
                a.wait_ge(S["ln_stats"], i + 1)
                a.activation(std[:, 0:nb], mv[:, 0:nb, 1], ACT.Sqrt, bias=eps[:, 0:1]).then_inc(S["ln_std"], 1)
                for j in range(nb):
                    if j == 0:
                        a.wait_ge(S["tab_free"], i + 1)
                        a.sem_inc(S["act_hold"], 1)
                    a.wait_ge(S["ln_xn"], t0 + j + 1)
                    a.activation(trow[:, j, 0:D], xn[:, j, :], ACT.Copy).then_inc(S["ln_hi"], 1)
                for j in range(nb):
                    a.wait_ge(S["ln_dif"], t0 + j + 1)
                    a.activation(trow[:, j, D:2 * D], dif[:, j, :], ACT.Copy, scale=LO).then_inc(S["ln_lo"], 1)
                for j in range(nb):
                    t = t0 + j
                    a.wait_ge(S["kv_used"], t + 1)
                    a.sem_inc(S["act_hold"], 1)
                    a.wait_ge(S["kb_ok"], t + 1)
                    a.activation(vv[:, :, 0:P], pQ[:, D:2 * D].rearrange("p (k n) -> p k n", k=DK), ACT.Copy).then_inc(S["v_ok"], 1)
                    a.activation(kr, kb, ACT.Relu).then_inc(S["kr_ok"], 1)
                    a.wait_ge(S["km_ok"], t + 1)
                    a.activation(ke, km, ACT.Exp).then_inc(S["ke_ok"], 1)

            with a.Fori(0, NT // NB) as i:
                norm(i, NB)
            norm(NT // NB, 1)

            with a.Fori(0, NT) as t:
                a.wait_ge(S["q_ps"], t + 1)
                for k in range(DK):
                    ins = a.activation(qr[:, k * P:(k + 1) * P], pQ[:, k * P:(k + 1) * P], ACT.Relu, bias=bqs[:, k:k + 1])
                ins.then_inc(S["qr_ok"], 1)
                a.wait_ge(S["qm_ok"], t + 1)
                a.activation(qe, qm, ACT.Exp).then_inc(S["qe_ok"], 1)
                a.wait_ge(S["ot_ps"], t + 1)
                a.activation(ot, pT[:, 0:D], ACT.Copy).then_inc(S["ot_sb"], 1)
                a.wait_ge(S["s_ok"], t + 1)
                a.activation(agg, agg, ACT.Copy, scale=deg[:, 1:2]).then_inc(S["agg_ok"], 1)
                a.wait_ge(S["agt_ps"], t + 1)
                a.activation(agt, pS[:, 0:D], ACT.Copy).then_inc(S["agt_sb"], 1)
                a.wait_ge(S["st_ok"], t + 1)
                a.activation(sc[:, 2:3], sc[:, 1:2], ACT.Sqrt, bias=eps[:, 0:1]).then_inc(S["sd_ok"], 1)
                a.wait_ge(S["x2t_ps"], t + 1)
                a.activation(x2t, pT[:, 0:D], ACT.Copy).then_inc(S["x2t_sb"], 1)
                a.wait_ge(S["nmx_ok"], t + 1)
                a.activation(lg[:, 1, :], lg[:, 0, :], ACT.Exp, bias=sc[:, 4:5], accum_out=sc[:, 5:6]).then_inc(S["ex_ok"], 1)

            with a.Fori(0, NX) as e:
                with a.Fori(0, JOBS) as i:
                    j = e * JOBS + i
                    a.wait_ge(S["xjt_ps"], j + 1)
                    a.activation(xjt, pT[:, 0:D], ACT.Copy).then_inc(S["xjt_sb"], 1)
                    a.wait_ge(S["h0_ps"], j + 1)
                    for c in range(FC // 2):
                        ins = a.activation(hs[:, c, :], pH0[:, c * P:(c + 1) * P], ACT.Relu, bias=b1s[:, bass.ds(e * FC + c, 1)])
                    ins.then_inc(S["h0_sb"], 1)

        @block.tensor
        def _(pe):
            pe.wait_ge(S["ident_ok"], 2)
            for a, (b0, b1_) in enumerate(((pT, pQ), (pS, pY))):
                pe.wait_ge(S["e_f32"], a + 1)
                for b in range(EBLK):
                    o = (b0, b1_)[b // 4][:, (b % 4) * P:(b % 4 + 1) * P]
                    ins = pe.transpose(o, xin_f(a)[:, b, :], ident[:, :])
                ins.then_inc(S["e_ps"], 1)
            pe.wait_ge(S["e_copied"], 2)
            pe.wait_ge(S["e_bound"], 1)
            for a in range(2):
                ins = pe.transpose(pS[0:NT, a * P:(a + 1) * P], bounds[:, a, :], ident[:, :])
            ins.then_inc(S["e_bt"], 1)
            pe.wait_ge(S["e_lohi"], 1)
            for a in range(2):
                ins = pe.matmul(pT[0:1, a * 64:a * 64 + NT], lohi[:, a:a + 1], ident[0:NT, 0:NT], start=True, stop=True)
            ins.then_inc(S["e_rowps"], 1)
            pe.wait_ge(S["e_row"], 1)
            pe.matmul(pS[0:NT, 0:1], new_row[0:1, 0:NT], ident[0:1, 0:1], start=True, stop=True).then_inc(S["e_newps"], 1)
            pe.wait_ge(S["e_new"], 1)
            pe.matmul(pT[0:1, 0:NT], new_col[:, :], tri[0:NT, 0:NT], start=True, stop=True).then_inc(S["e_baseps"], 1)

            kvp = (pH0, pH1)
            for k in range(DK):
                pe.matmul(kvp[k][:, 0:P + 1], zero16[:, 0:P], zero16[:, 0:P + 1], start=True, stop=False)
            pe.wait_ge(S["w_qkv"], 16 * 12)
            pe.wait_ge(S["spans_ok"], 1)

            def keys(t, j, rows_n, last):
                pe.wait_ge(S["ln_xn"], t + 1)
                if j >= 0:
                    pe.sem_inc(S["pe_hold"], 1)
                for k in range(DK):
                    ins = pe.transpose(pT[:, k * P:(k + 1) * P], xn[:, j, k * P:(k + 1) * P], ident[:, :])
                ins.then_inc(S["xt_ps"], 1)
                pe.wait_ge(S["xt_sb"], t + 1)
                for k in range(DK):
                    ins = pe.matmul(pQ[:, :], xt[:, j, k * P:(k + 1) * P], wkv[:, k, :], start=(k == 0), stop=(k == DK - 1))
                ins.then_inc(S["kv_ps"], 1)
                pe.wait_ge(S["kk_ok"], t + 1)
                pe.sem_inc(S["pe_hold"], 1)
                pe.wait_ge(S["v_ok"], t + 1)
                for k in range(DK):
                    ins = pe.matmul(kvp[k][:, 0:P + 1], kk[0:rows_n, k * P:(k + 1) * P], vv[0:rows_n, k, :], start=False, stop=last)
                ins.then_inc(S["kv_used"], 1)

            pe.sem_inc(S["kv_used"], 1)
            with pe.Fori(0, NT // NB) as i:
                for j in range(NB):
                    keys(i * NB + j, j, P, False)
            keys(NT - 1, 0, LAST, True)

            pe.wait_ge(S["kvm_ok"], 1)
            pe.sem_inc(S["slots"], RING)
            pe.sem_inc(S["oh_slots"], OH)
            with pe.register("held") as at_r, pe.register("pair") as pair_r:
                pe.reg_mov(at_r, 0)
                pe.reg_mov(pair_r, 1)
                with pe.Fori(0, NT) as t:
                    pe.wait_ge(S["p2_in"], t * 32 + 32)
                    for m in range(DK):
                        for k in range(DK):
                            ins = pe.matmul(pQ[:, m * P:(m + 1) * P], wqs[:, k, m * P:(m + 1) * P], xtin[:, t % 2, k * P:(k + 1) * P],
                                            start=(k == 0), stop=(k == DK - 1))
                    ins.then_inc(S["q_ps"], 1)
                    pe.wait_ge(S["qt_ok"], t + 1)
                    for k in range(DK):
                        ins = pe.matmul(pQ[:, k * (P + HB):(k + 1) * (P + HB)], qt[:, k * P:(k + 1) * P], kvm[:, k, :], start=True, stop=True)
                    ins.then_inc(S["att_ps"], 1)
                    pe.wait_ge(S["o_ok"], t + 1)
                    for k in range(DK):
                        ins = pe.transpose(pT[:, k * P:(k + 1) * P], o_sb[:, k * P:(k + 1) * P], ident[:, :])
                    ins.then_inc(S["ot_ps"], 1)

                    lo = pe.value_load(spans[0:1, 0, bass.ds(t, 1)], min_val=0, max_val=ECP * NT)
                    last = pe.value_load(spans[0:1, 1, bass.ds(t, 1)], min_val=0, max_val=ECP * NT)
                    at = pe.snap(at_r)
                    with pe.If(at < lo):
                        with pe.Fori(at, lo) as f:
                            pe.wait_ge(S["relayed"], f + 1 + LAG)
                            pe.sem_inc(S["slots"], 1)
                        pe.sem_inc(S["pe_hold"], 1)
                    pe.wait_ge(S["agg_used"], t + 1)
                    pe.matmul(pA[:, :], zero16[:, 0:P], zero16[:, :], start=True, stop=False)
                    pe.matmul(pD[:, 0:1], zero16[:, 0:P], zero16[:, 0:1], start=True, stop=False)

                    def add(f, final):
                        n = pe.snap(pair_r)
                        pe.wait_ge(S["relayed"], f + 1 + LAG)
                        pe.sem_inc(S["pe_hold"], 1)
                        pe.wait_ge(S["oh_ready"], n)
                        a = pe.matmul(pA[:, :], onehot[:, n % OH, :], gathered[:, f % RING, :], start=False, stop=final)
                        if not final:
                            a.then_inc(S["slots"], 1)
                        pe.matmul(pD[:, 0:1], onehot[:, n % OH, :], ones16[:, 0:1], start=False, stop=final).then_inc(S["oh_slots"], 1)
                        pe.reg_add(pair_r, pair_r, 1)

                    with pe.If(lo < last):
                        with pe.Fori(lo, last) as f:
                            add(f, False)
                        pe.sem_inc(S["pe_hold"], 1)
                    add(last, True)
                    pe.matmul(pS[:, 0:1], zero16[:, 0:P], zero16[:, 0:1], start=True, stop=True).then_inc(S["agg_done"], 1)
                    pe.reg_mov(at_r, last)

                    pe.wait_ge(S["agg_ok"], t + 1)
                    for k in range(DK):
                        ins = pe.transpose(pS[:, k * P:(k + 1) * P], agg[:, k * P:(k + 1) * P], ident[:, :])
                    ins.then_inc(S["agt_ps"], 1)
                    pe.wait_ge(S["ot_sb"], t + 1)
                    for k in range(DK):
                        pe.matmul(pQ[:, 0:D], ot[:, k * P:(k + 1) * P], wos[:, k, :], start=(k == 0), stop=False)
                    pe.wait_ge(S["agt_sb"], t + 1)
                    for k in range(DK):
                        ins = pe.matmul(pQ[:, 0:D], agt[:, k * P:(k + 1) * P], wgs[:, k, :], start=False, stop=(k == DK - 1))
                    ins.then_inc(S["x1_ps"], 1)
                    pe.wait_ge(S["x2_ok"], t + 1)
                    for k in range(DK):
                        ins = pe.transpose(pT[:, k * P:(k + 1) * P], x2[:, k * P:(k + 1) * P], ident[:, :])
                    ins.then_inc(S["x2t_ps"], 1)
                    pe.wait_ge(S["x2t_sb"], t + 1)
                    for k in range(DK):
                        ins = pe.matmul(pS[:, 0:NX], x2t[:, k * P:(k + 1) * P], gws[:, k, :], start=(k == 0), stop=(k == DK - 1))
                    ins.then_inc(S["lg_ps"], 1)
                    pe.wait_ge(S["oh_ok"], t + 1)
                    pe.matmul(pS[:, NX:2 * NX], tri16[:, :], oh16[:, :], start=True, stop=False)
                    pe.matmul(pS[:, NX:2 * NX], ones16[:, :], cnt16[:, :], start=False, stop=True).then_inc(S["pos_ps"], 1)

            pe.wait_ge(S["w_big"], 16 * 18)
            for e in range(NX):
                with pe.Fori(0, JOBS) as i:
                    j = e * JOBS + i
                    pe.wait_ge(S["xj_ok"], j + 1)
                    for k in range(DK):
                        ins = pe.transpose(pT[:, k * P:(k + 1) * P], xj[:, k * P:(k + 1) * P], ident[:, :])
                    ins.then_inc(S["xjt_ps"], 1)
                    pe.wait_ge(S["xjt_sb"], j + 1)
                    for c in range(FC):
                        ph = (pH0, pH1)[c // 4]
                        for k in range(DK):
                            ins = pe.matmul(ph[:, (c % 4) * P:(c % 4 + 1) * P], w1s[:, e, k, c * P:(c + 1) * P],
                                            xjt[:, k * P:(k + 1) * P], start=(k == 0), stop=(k == DK - 1))
                        if c % 4 == 3:
                            ins.then_inc(S["h0_ps" if c == 3 else "h1_ps"], 1)
                    for c in range(FC):
                        if c % 4 == 0:
                            pe.wait_ge(S["h0_sb" if c == 0 else "h1_sb"], j + 1)
                        ins = pe.matmul(pY[:, 0:D], hs[:, c, :], w2s[:, e, c, :],
                                        start=(c == 0), stop=(c == FC - 1))
                    ins.then_inc(S["y_ps"], 1)

        @block.vector
        def _(v):
            c = Chain(v, S["dve_c"])
            v.wait_ge(S["iota_ok"], 2)
            c.mark(v.tensor_copy(iota_row[:, :], iota_i[:, :]))
            c.mark(v.tensor_scalar(expert_m8[:, :], iota_i[:, 0:NX], float(-NX), None, ALU.add))
            c.mark(v.tensor_copy(chunk_id[:, :], chunk_i[:, :]))
            c.mark(v.memset(cnt16[:, :], 0.0))
            v.wait_ge(S["ident_ok"], 2)
            c.mark(v.tensor_copy(tri16[:, :], tri[:, :]))
            c.mark(v.memset(kvm[:, :, :], 0.0))
            c.mark(v.memset(new_row[:, :], 0.0))
            c.mark(v.memset(spans[:, :, :], 1 << 30))
            edges = xin[:, :, :, :].rearrange("p a b c -> p (a b c)").bitcast(I32)
            for a, name in ((0, "e_dst"), (1, "e_src")):
                v.wait_ge(S[name], 48)
                v.tensor_copy(xin_f(a).rearrange("p b e -> p (b e)"), edges[:, a * 1024:a * 1024 + EBLK * P]).then_inc(S["e_f32"], 1)
            v.wait_ge(S["e_f32"], 2)
            c.mark(v.tensor_reduce(cmin[:, :], xin_f(0), AX, ALU.min))
            c(v.tensor_reduce(cmax[:, :], xin_f(0), AX, ALU.max))
            for a, (b0, b1_) in enumerate(((pT, pQ), (pS, pY))):
                v.wait_ge(S["e_ps"], a + 1)
                t = (dst_t, src_t)[a]
                v.tensor_copy(t[:, 0:512], b0[:, :])
                v.tensor_copy(t[:, 512:EBLK * P], b1_[:, 0:EBLK * P - 512]).then_inc(S["e_copied"], 1)
            sel = xn[:, :, :].rearrange("p a b -> p (a b)")
            m0 = sel[:, 0:NT * EBLK].rearrange("p (t b) -> p t b", b=EBLK)
            m1 = sel[:, 512:512 + NT * EBLK].rearrange("p (t b) -> p t b", b=EBLK)
            thr = tile_iota[:, 0:NT]
            c(v.tensor_scalar(thr, iota_row[:, 0:NT], float(P), None, ALU.mult))

            def wide(ap):
                return ap.rearrange("p (a b) -> p a b", a=1).broadcast_to([P, NT, EBLK])
            thr_w = thr.rearrange("p (t a) -> p t a", a=1).broadcast_to([P, NT, EBLK])
            c(v.tensor_tensor(m0, wide(cmax[:, :]), thr_w, ALU.is_ge))
            ids_lo, ids_hi = lg[:, 0, 0:EBLK], lg[:, 1, 0:EBLK]
            c.mark(v.tensor_scalar(ids_lo, chunk_id[:, :], -BIG, None, ALU.add))
            c.mark(v.tensor_scalar(ids_hi, chunk_id[:, :], 1.0, None, ALU.add))
            c(v.tensor_scalar(thr, thr, float(P), None, ALU.add))
            c(v.tensor_tensor(m1, wide(cmin[:, :]), thr_w, ALU.is_lt))
            c(v.tensor_tensor(m0, m0, wide(ids_lo), ALU.mult))
            c(v.tensor_tensor(m1, m1, wide(ids_hi), ALU.mult))
            c.mark(v.tensor_reduce(bounds[:, 0, :], m0, AX, ALU.min))
            c(v.tensor_reduce(bounds[:, 1, :], m1, AX, ALU.max))
            v.sem_inc(S["e_bound"], 1)
            v.wait_ge(S["e_bt"], 1)
            c.mark(v.tensor_reduce(lohi[:, 0:1], pS[0:NT, 0:P], AX, ALU.min))
            c(v.tensor_reduce(lohi[:, 1:2], pS[0:NT, P:2 * P], AX, ALU.max))
            c(v.tensor_scalar(lohi[:, 0:1], lohi[:, 0:1], BIG, float(EC - 1), ALU.add, ALU.min))
            c(v.tensor_scalar(new_col[:, :], lohi[:, 0:1], 1.0, None, ALU.add))
            c(v.tensor_tensor(lohi[:, 1:2], lohi[:, 1:2], new_col[:, :], ALU.max))
            v.sem_inc(S["e_lohi"], 1)
            v.wait_ge(S["e_rowps"], 1)
            c(v.tensor_copy(lh_row[0:1, :, 0:NT], pT[0:1, 0:2 * 64].rearrange("p (a t) -> p a t", a=2)[:, :, 0:NT]))
            c(v.scalar_tensor_tensor(new_row[0:1, 1:NT], lh_row[0:1, 1, 0:NT - 1], -1.0, lh_row[0:1, 0, 1:NT], ALU.add, ALU.is_gt))
            v.sem_inc(S["e_row"], 1)
            v.wait_ge(S["e_newps"], 1)
            c(v.tensor_copy(new_col[:, :], pS[0:NT, 0:1]))
            v.sem_inc(S["e_new"], 1)
            v.wait_ge(S["e_baseps"], 1)
            c(v.tensor_scalar(base_row[0:1, 0:NT], pT[0:1, 0:NT], float(ECP), None, ALU.mult))
            c.mark(v.tensor_copy(spans[0:1, 2:4, 0:NT], lh_row[0:1, :, 0:NT]))
            c.mark(v.tensor_tensor(spans[0:1, 0, 0:NT], lh_row[0:1, 0, 0:NT], base_row[0:1, 0:NT], ALU.add))
            c.mark(v.scalar_tensor_tensor(spans[0:1, 1, 0:NT], lh_row[0:1, 1, 0:NT], -1.0, base_row[0:1, 0:NT], ALU.add, ALU.add))
            c(v.tensor_scalar(spans[0:1, 4, 0:1], base_row[0:1, NT - 1:NT], 1.0 / RING, float(EB), ALU.mult, ALU.add))
            v.sem_inc(S["spans_ok"], 1)
            c0 = c.n

            K1 = 3
            v.sem_inc(S["x_out"], 1)

            def keys(i, nb):
                t0 = i * NB
                k = Chain(v, S["dve_c"], c0 + i * K1)
                v.wait_ge(S["x_in"], i * 16 + 16)
                hold(v, "dve_hold")
                for j in range(nb):
                    ins = v.bn_stats(stats[:, j, :], xin[:, i % 2, j, :])
                k(ins)
                hold(v, "dve_hold")
                for j in range(nb):
                    ins = v.bn_aggr(mv[:, j, :], stats[:, j, :])
                ins.then_inc(S["ln_stats"], 1)
                v.wait_ge(S["ln_std"], i + 1)
                k(v.reciprocal(rstd[:, 0:nb], std[:, 0:nb]))
                for j in range(nb):
                    ins = v.tensor_scalar(xn[:, j, :], xin[:, i % 2, j, :], mv[:, j, 0:1], rstd[:, j:j + 1], ALU.subtract, ALU.mult)
                    ins.then_inc(S["ln_xn"], 1)
                k(v.memset(sc[:, 11:12], 0.0))
                v.sem_inc(S["x_out"], 1)
                assert k.n == K1
                for j in range(nb):
                    t = t0 + j
                    if j == 0:
                        v.wait_ge(S["xt_free"], i + 1)
                        v.sem_inc(S["dve_hold"], 1)
                    v.wait_ge(S["xt_ps"], t + 1)
                    v.tensor_copy(xt[:, j, :], pT[:, 0:D]).then_inc(S["xt_sb"], 1)
                    v.wait_ge(S["kv_ps"], t + 1)
                    v.tensor_tensor(kb, pQ[:, 0:D], bks[:, :], ALU.add).then_inc(S["kb_ok"], 1)
                    v.wait_ge(S["kb_ok"], t + 1)
                    v.tensor_scalar(km, kb, 0.0, None, ALU.min).then_inc(S["km_ok"], 1)
                v.wait_ge(S["ln_dif"], t0 + nb)
                v.sem_inc(S["dve_hold"], 1)

            with v.Fori(0, NT // NB) as i:
                keys(i, NB)
            keys(NT // NB, 1)
            c1 = c0 + (NT // NB + 1) * K1

            c = Chain(v, S["dve_c"], c1)
            v.wait_ge(S["kv_used"], NT + 1)
            for k in range(DK):
                ps = (pH0, pH1)[k]
                for h in range(HB):
                    r = slice(h * HD, (h + 1) * HD)
                    c.mark(v.tensor_copy(kvm[r, k, P + h:P + h + 1], ps[r, P:P + 1]))
            c.wait()
            for k in range(DK):
                ps = (pH0, pH1)[k]
                for h in range(HB):
                    r = slice(h * HD, (h + 1) * HD)
                    c.mark(v.scalar_tensor_tensor(kvm[r, k, h * HD:(h + 1) * HD], bvs[r, k * P + h * HD:k * P + (h + 1) * HD],
                                                  kvm[r, k, P + h:P + h + 1], ps[r, h * HD:(h + 1) * HD], ALU.mult, ALU.add))
            c.mark(v.memset(jrow[:, 0, 0:C_TOK], 0.0))
            c.mark(v.memset(jrow[:, 0, C_TOK:ROW].bitcast(I32), N))
            c(v.tensor_scalar(tok[:, :], chunk_id[:, 0:1], float(-P), None, ALU.add))
            v.sem_inc(S["rows_z"], 1)
            v.sem_inc(S["kvm_ok"], 1)
            v.sem_inc(S["agg_used"], 1)
            v.sem_inc(S["p2_free"], 1)
            for n in ("row_stored", "row_free", "fin_free", "j_free"):
                v.sem_inc(S[n], 2)
            c2 = c1 + c.n

            K2 = 29
            with v.register("pair_v") as pair_r:
                v.reg_mov(pair_r, 1)
                with v.Fori(0, NT) as t:
                    k = Chain(v, S["dve_c"], c2 + t * K2)
                    v.wait_ge(S["qr_ok"], t + 1)
                    for m in range(DK):
                        ins = v.tensor_scalar(qm[:, m * P:(m + 1) * P], pQ[:, m * P:(m + 1) * P], bqs[:, m:m + 1], 0.0, ALU.add, ALU.min)
                    ins.then_inc(S["qm_ok"], 1)
                    v.wait_ge(S["qe_ok"], t + 1)
                    v.tensor_tensor(qt, qr, qe, ALU.add).then_inc(S["qt_ok"], 1)
                    v.wait_ge(S["att_ps"], t + 1)
                    att = pQ[:, 0:DK * (P + HB)].rearrange("p (k n) -> p k n", k=DK)
                    k(v.tensor_scalar(rden[:, :].rearrange("p (k h) -> p k h", k=DK), att[:, :, P:P + HB], 1e-6, None, ALU.add))
                    k(v.reciprocal(rden[:, :], rden[:, :]))
                    for m in range(DK):
                        ins = v.tensor_tensor(o_sb[:, m * P:(m + 1) * P].rearrange("p (h d) -> p h d", d=HD),
                                              att[:, m, 0:P].rearrange("p (h d) -> p h d", d=HD),
                                              rden[:, m * HB:(m + 1) * HB].rearrange("p (h a) -> p h a", a=1).broadcast_to([P, HB, HD]), ALU.mult)
                    ins.then_inc(S["o_ok"], 1)
                    v.wait_ge(S["p2_in"], t * 32 + 32)
                    k(v.tensor_tensor(xb, xres[:, t % 2, :], bos[:, :], ALU.add))
                    v.sem_inc(S["p2_free"], 1)

                    lo = v.value_load(spans[0:1, 2, bass.ds(t, 1)], min_val=0, max_val=EC - 1)
                    hi = v.value_load(spans[0:1, 3, bass.ds(t, 1)], min_val=1, max_val=EC)
                    k(v.tensor_scalar(tok[:, :], tok[:, :], float(P), None, ALU.add))
                    k(v.tensor_scalar(sc[:, 0:1], chunk_id[:, 0:1], -1.0, tok[:, 0:1], ALU.mult, ALU.add))
                    k(v.tensor_scalar(tile_iota[:, :], iota_row[:, :], sc[:, 0:1], None, ALU.add))
                    hold(v, "dve_hold")
                    with v.Fori(lo, hi) as ch:
                        n = v.snap(pair_r)
                        v.wait_ge(S["oh_slots"], n)
                        v.tensor_scalar(onehot[:, n % OH, :], tile_iota[:, :], dst_t[:, bass.ds(ch, 1)], None, ALU.is_equal).then_inc(S["oh_ready"], 1)
                        v.reg_add(pair_r, pair_r, 1)

                    v.wait_ge(S["agg_done"], t + 1)
                    k.mark(v.tensor_scalar(deg[:, 0:1], pD[:, 0:1], 1.0, None, ALU.max))
                    k.mark(v.tensor_scalar(deg[:, 2:3], pD[:, 0:1], 1.0, None, ALU.min))
                    k(v.tensor_copy(agg, pA[:, 0:D]))
                    k(v.reciprocal(deg[:, 1:2], deg[:, 0:1]))
                    k(v.scalar_tensor_tensor(agg, pA[:, D:2 * D], 1.0 / LO, agg, ALU.mult, ALU.add))
                    v.sem_inc(S["s_ok"], 1)
                    v.sem_inc(S["agg_used"], 1)
                    k(v.scalar_tensor_tensor(xb, bgs[:, :], deg[:, 2:3], xb, ALU.mult, ALU.add))
                    v.wait_ge(S["row_stored"], t + 1)
                    v.sem_inc(S["dve_hold"], 1)
                    v.wait_ge(S["row_free"], t + 1)
                    v.sem_inc(S["dve_hold"], 1)
                    v.wait_ge(S["x1_ps"], t + 1)
                    v.tensor_tensor(rows_sb[:, t % 2, 0:D], pQ[:, 0:D], xb, ALU.add).then_inc(S["x1_ok"], 1)
                    v.wait_ge(S["x1_ok"], t + 1)
                    hold(v, "dve_hold")
                    k(v.bn_stats(stats[:, 0, :], rows_sb[:, t % 2, 0:D]))
                    hold(v, "dve_hold")
                    k(v.bn_aggr(sc[:, 0:2], stats[:, 0, :]))
                    v.sem_inc(S["st_ok"], 1)
                    v.wait_ge(S["sd_ok"], t + 1)
                    k(v.reciprocal(rows_sb[:, t % 2, C_RSTD:C_RSTD + 1], sc[:, 2:3]))
                    k(v.scalar_tensor_tensor(rows_sb[:, t % 2, C_NMR:C_NMR + 1], sc[:, 0:1], -1.0, rows_sb[:, t % 2, C_RSTD:C_RSTD + 1], ALU.mult, ALU.mult))
                    v.tensor_scalar(x2, rows_sb[:, t % 2, 0:D], rows_sb[:, t % 2, C_RSTD:C_RSTD + 1], rows_sb[:, t % 2, C_NMR:C_NMR + 1], ALU.mult, ALU.add).then_inc(S["x2_ok"], 1)
                    v.wait_ge(S["lg_ps"], t + 1)
                    k(v.tensor_tensor(lg[:, 0, :], pS[:, 0:NX], gbs[:, :], ALU.add))
                    k(v.tensor_reduce(sc[:, 3:4], lg[:, 0, :], AX, ALU.max))
                    v.tensor_scalar(sc[:, 4:5], sc[:, 3:4], -1.0, None, ALU.mult).then_inc(S["nmx_ok"], 1)
                    k(v.scalar_tensor_tensor(lg[:, 2, :], lg[:, 0, :], sc[:, 3:4], expert_m8[:, :], ALU.is_ge, ALU.mult))
                    k(v.tensor_reduce(sc[:, 6:7], lg[:, 2, :], AX, ALU.min))
                    v.tensor_scalar(oh16[:, :], expert_m8[:, :], sc[:, 6:7], None, ALU.is_equal).then_inc(S["oh_ok"], 1)
                    v.wait_ge(S["ex_ok"], t + 1)
                    k.mark(v.reciprocal(rows_sb[:, t % 2, C_PRB:C_PRB + 1], sc[:, 5:6]))
                    v.wait_ge(S["pos_ps"], t + 1)
                    k(v.tensor_tensor(lg[:, 3, :], pS[:, NX:2 * NX], oh16[:, :], ALU.mult))
                    k(v.tensor_reduce(sc[:, 7:8], lg[:, 3, :], AX, ALU.add))
                    k.mark(v.tensor_tensor(cnt16[:, :], cnt16[:, :], oh16[:, :], ALU.add))
                    k.mark(v.tensor_scalar(sc[:, 8:9], sc[:, 6:7], float(SLOTS), float(NX * SLOTS - 1), ALU.mult, ALU.add))
                    k(v.tensor_scalar(sc[:, 9:10], sc[:, 7:8], float(CAP), BIG, ALU.is_gt, ALU.mult))
                    k(v.tensor_tensor(sc[:, 8:9], sc[:, 8:9], sc[:, 7:8], ALU.add))
                    k.mark(v.tensor_tensor(slot2[:, bass.ds(t % 2, 1)], sc[:, 8:9], sc[:, 9:10], ALU.add))
                    k(v.tensor_copy(rows_sb[:, t % 2, C_TOK:C_TOK + 1].bitcast(I32), tok[:, :]))
                    v.sem_inc(S["row_ok"], 1)
                    assert k.n == K2, k.n
                v.sem_inc(S["dve_hold"], 1)
            c3 = c2 + NT * K2

            K3 = 8
            with v.Fori(0, NX) as e:
                with v.Fori(0, JOBS) as i:
                    j = e * JOBS + i
                    k = Chain(v, S["dve_c"], c3 + j * K3)
                    v.wait_ge(S["j_in"], j * 16 + 16)
                    v.tensor_scalar(xj, jrow[:, j % 2, 0:D], jrow[:, j % 2, C_RSTD:C_RSTD + 1], jrow[:, j % 2, C_NMR:C_NMR + 1],
                                    ALU.mult, ALU.add).then_inc(S["xj_ok"], 1)
                    v.wait_ge(S["h1_ps"], j + 1)
                    for q in range(FC // 2, FC):
                        ins = v.tensor_scalar(hs[:, q, :], pH1[:, (q - FC // 2) * P:(q - FC // 2 + 1) * P],
                                              b1s[:, bass.ds(e * FC + q, 1)], 0.0, ALU.add, ALU.max)
                    ins.then_inc(S["h1_sb"], 1)
                    v.wait_ge(S["y_ps"], j + 1)
                    k(v.tensor_tensor(y[:, 0, :], pY[:, 0:D], b2s[:, bass.ds(e, 1), :].rearrange("p a d -> p (a d)"), ALU.add))
                    k(v.tensor_scalar(y[:, 1, :], y[:, 0, :], jrow[:, j % 2, C_PRB:C_PRB + 1], None, ALU.mult))
                    k.mark(v.tensor_scalar(y[:, 2, :].bitcast(I32), y[:, 1, :], 0.0, 0.0, ALU.mult, ALU.is_equal))
                    v.wait_ge(S["fin_free"], j + 1)
                    v.sem_inc(S["dve_hold"], 1)
                    k.mark(v.tensor_scalar(fin[:, j % 2, :], y[:, 1, :], 1.0e4, -1.0e4, ALU.min, ALU.max))
                    k(v.tensor_tensor(y[:, 0, :], y[:, 1, :], y[:, 1, :], ALU.is_equal))
                    k(v.tensor_tensor(y[:, 0, :], fin[:, j % 2, :], y[:, 0, :], ALU.mult))
                    hold(v, "dve_hold")
                    k(v.copy_predicated(y[:, 0, :], y[:, 2, :].bitcast(I32), y[:, 1, :]))
                    v.tensor_copy(jtok[:, bass.ds(j % 2, 1)], jrow[:, j % 2, C_TOK:C_TOK + 1].bitcast(I32))
                    k(v.tensor_tensor(fin[:, j % 2, :], y[:, 0, :], jrow[:, j % 2, 0:D], ALU.add))
                    assert k.n == K3, k.n
                    v.sem_inc(S["fin_ok"], 1)
                    v.sem_inc(S["j_free"], 1)


_INS = ["x", "src", "dst", "L0_gnn_W", "L0_gnn_b", "L0_mix_wq", "L0_mix_bq", "L0_mix_wk", "L0_mix_bk", "L0_mix_wv", "L0_mix_bv",
        "L0_mix_wo", "L0_mix_bo", "L0_ffn_gate_w", "L0_ffn_gate_b", "L0_ffn_w1", "L0_ffn_b1", "L0_ffn_w2", "L0_ffn_b2"]
_OUTS = [((N, D), "float32")]


def kernel(**inputs):
    import numpy as _np
    import concourse.bacc as _bacc
    from concourse import mybir as _mybir
    from concourse.bass_utils import run_bass_kernel_spmd as _run

    nc = _bacc.Bacc("TRN2", target_bir_lowering=False, num_devices=1)
    arrays, args = {}, []
    for name in _INS:
        a = _np.ascontiguousarray(inputs[name])
        arrays[f"in_{name}_dram"] = a
        args.append(nc.dram_tensor(f"in_{name}_dram", a.shape, _mybir.dt.from_np(a.dtype), kind="ExternalInput").ap())
    for i, (shape, dtype) in enumerate(_OUTS):
        dt = _mybir.dt.from_np(_np.dtype(dtype))
        args.append(nc.dram_tensor(f"out_{i}_dram", shape, dt, kind="ExternalOutput").ap())
    gps_block(nc, *args)
    r = _run(nc, [arrays], core_ids=[0])
    got = tuple(r.results[0][f"out_{i}_dram"] for i in range(len(_OUTS)))
    return got[0]
```

```python
from contextlib import ExitStack

import concourse.bass as bass
from concourse import mybir

F32 = mybir.dt.float32
F16 = mybir.dt.float16
I32 = mybir.dt.int32
ALU = mybir.AluOpType
ACT = mybir.ActivationFunctionType
AX = mybir.AxisListType.X

P = 128
D = 256
DK = D // P
HEADS = 8
HD = D // HEADS
HB = P // HD
N = 6250
NT = -(-N // P)
LAST = N - (NT - 1) * P
E = 100000
EC = -(-E // P)
G = 4
RQ = 4
RING = RQ * G
EB = -(-EC // RING)
EQ = EB * RQ
ECP = EB * RING
EBLK = -(-ECP // P)
OQ = 4
EARLY = 2
NB = 4
NX = 8
F = 1024
FC = F // P
CAP = 977
SLOTS = 1024
JOBS = SLOTS // P
LO = 2048.0
ROW = D + 4
C_RSTD, C_NMR, C_PRB, C_TOK = D, D + 1, D + 2, D + 3
RB = 4
AFTER = 2
JB = 4
BIG = 1.0e6
EPS = 1e-5
PAD_DST = 100000.0


def gps_block(nc, x, src, dst, gnn_w, gnn_b, wq, bq, wk, bk, wv, bv, wo, bo,
              gate_w, gate_b, w1, b1, w2, b2, out):
    table = nc.dram_tensor("table", [NT * P, 2 * D], F16).ap()
    normed_t = nc.dram_tensor("normed_t", [NT, P, DK * P], F32).ap()
    rows = nc.dram_tensor("rows", [NX * SLOTS, ROW], F32).ap()
    rows_t = rows.rearrange("(s p) d -> s p d", p=P)
    x_t = x[0:(NT - 1) * P, :].rearrange("(t p) d -> t p d", p=P)
    out_t = out[0:(NT - 1) * P, :].rearrange("(t p) d -> t p d", p=P)

    with ExitStack() as ctx:
        def sb(name, shape, dt=F32):
            return ctx.enter_context(nc.sbuf_tensor(name, shape, dt))

        def bank(name):
            return ctx.enter_context(nc.psum_tensor(name, [P, 512], F32))

        def sem(name):
            return ctx.enter_context(nc.semaphore(name))

        w1s = sb("w1s", [P, NX, DK, F])
        w2s = sb("w2s", [P, NX, FC, D])
        b1s = sb("b1s", [P, NX * FC])
        b2s = sb("b2s", [P, NX, D])
        wkv = sb("wkv", [P, DK, 2 * D])
        wqs = sb("wqs", [P, DK, D])
        wos = sb("wos", [P, DK, D])
        wgs = sb("wgs", [P, DK, D])
        gws = sb("gws", [P, DK, NX])
        hs = sb("hs", [P, FC, P])
        bks = hs[:, 0:2, :].rearrange("p a b -> p (a b)")
        bvs = hs[:, 2:4, :].rearrange("p a b -> p (a b)")
        bos = sb("bos", [P, D])
        bgs = sb("bgs", [P, D])
        bqs = sb("bqs", [P, DK])
        gbs = sb("gbs", [P, NX])
        ident = sb("ident", [P, P])
        tri = sb("tri", [P, P])
        c16 = sb("c16", [P, 4, P], F16)
        zero16, ones16, tri16 = c16[:, 0, :], c16[:, 1, :], c16[:, 2, :]
        any16 = c16[:, :, :].rearrange("p a b -> p (a b)")
        iota_row = sb("iota_row", [P, P])
        iota_i = sb("iota_i", [P, P], I32)
        expert_m8 = sb("expert_m8", [P, NX])
        eps = sb("eps", [P, 1])

        src_t = sb("src_t", [P, ECP], I32)
        dst_t = sb("dst_t", [P, ECP])
        cmin = sb("cmin", [P, EBLK])
        cmax = sb("cmax", [P, EBLK])
        chunk_id = sb("chunk_id", [P, EBLK])
        chunk_i = sb("chunk_i", [P, EBLK], I32)
        bounds = sb("bounds", [P, 2, NT])
        lohi = sb("lohi", [NT, 2])
        lh_row = sb("lh_row", [1, 2, 64])
        new_row = sb("new_row", [1, 64])
        new_col = sb("new_col", [NT, 1])
        base_row = sb("base_row", [1, 64])
        spans = sb("spans", [1, 6, 64], I32)
        idx = sb("idx", [P, RING], I32)
        gathered = sb("gathered", [P, RING, 2 * D], F16)
        onehot = sb("onehot", [P, OQ, G, P], F16)
        tile_iota = sb("tile_iota", [P, P])

        ring32 = gathered[:, :, :].rearrange("p a b -> p (a b)").bitcast(F32)
        xin = ring32[:, 0:2 * NB * D].rearrange("p (a b c) -> p a b c", a=2, b=NB)
        stats = sb("stats", [P, NB, 6])
        mv = sb("mv", [P, NB, 2])
        std = sb("std", [P, NB])
        rstd = sb("rstd", [P, NB])
        xn = sb("xn", [P, NB, D])
        trow = ring32[:, 2 * NB * D:3 * NB * D].bitcast(F16).rearrange("p (b d) -> p b d", b=NB)
        xt = ring32[:, 3 * NB * D:4 * NB * D].rearrange("p (b d) -> p b d", b=NB)
        dif = sb("dif", [P, NB, D])
        kvw = sb("kvw", [P, 4, D])
        kb, km, kr, ke = kvw[:, 0, :], kvw[:, 1, :], kvw[:, 2, :], kvw[:, 3, :]
        kk = sb("kk", [P, D])
        vv = sb("vv", [P, DK, P + 1])
        kvm = sb("kvm", [P, DK, P + HB])

        xtin = dif[:, 0:2, :]
        xres = dif[:, 2:4, :]
        qr, qe, qt, ahi = xn[:, 0, :], xn[:, 1, :], xn[:, 2, :], xn[:, 3, :]
        rden = sb("rden", [P, HEADS])
        o_sb, ot = kvw[:, 0, :], kvw[:, 1, :]
        deg = sb("deg", [P, 4])
        agg, agt = kvw[:, 2, :], kvw[:, 3, :]
        xb = kk[:, :]
        rows_sb = sb("rows_sb", [P, RB, ROW])
        row_at = sb("row_at", [P, RB], I32)
        x2 = wkv[:, 0, 0:D]
        x2t = wkv[:, 0, D:2 * D]
        lg = sb("lg", [P, 6, NX])
        sc = sb("sc", [P, 12])
        oh16 = sb("oh16", [P, NX], F16)
        cnt16 = sb("cnt16", [P, NX], F16)
        rn = sb("rn", [P, 2])
        tok = sb("tok", [P, 1])

        jrow = ring32[:, 0:JB * ROW].rearrange("p (a d) -> p a d", a=JB)
        y = ring32[:, JB * ROW:JB * ROW + 3 * D].rearrange("p (a d) -> p a d", a=3)
        empty = ring32[:, 0:ROW]
        xj, xjt = xn[:, 0, :], xn[:, 1, :]
        fin = wkv[:, 1, :].rearrange("p (a d) -> p a d", a=2)
        jtok = sb("jtok", [P, 2], I32)

        pA = bank("pA")
        pD = bank("pD")
        pT = bank("pT")
        pQ = bank("pQ")
        pH0 = bank("pH0")
        pH1 = bank("pH1")
        pY = bank("pY")
        pS = bank("pS")

        names = """w_edge w_qkv w_big consts iota_ok ident_ok
          e_src e_dst e_padded e_f32 e_ps e_copied e_bound e_bt e_lohi e_rowps e_row e_newps e_new e_baseps spans_ok idx_ok row_stored row_free fin_free
          x_in x_out ln_stats ln_std ln_xn ln_hi ln_dif ln_lo tab_st tab_free xt_ps xt_sb xt_st xt_free kv_ps kb_ok v_ok kr_ok km_ok ke_ok kk_ok
          kv_used kv_sum kvm_ok kvm_z rows_z rows_init
          slots relayed oh_slots oh_ready agg_done
          xt_in xr_in xb_ok q_ps qe_ok qt_ok att_ps o_ok ot_ps ot_sb dg_ok ahi_ok agg_ok agt_ps agt_sb x1_ps x1_ok
          st_ok sd_ok nm_ok x2_ok x2t_ps x2t_sb lg_ps nmx_ok ex_ok oh_ok pos_ps row_ok row_st scat_done
          tile_c y_used j_ready j_free xj_ok xjt_ps xjt_sb h0_ps h1_ps h0_sb h1_sb y_ps fin_ok fin_sc dve_c
          place_c agg_c att_c x1_c route_c route2_c
          sp_hold act_hold dve_hold pool_hold pe_hold""".split()
        S = {n: sem(n) for n in names}
        landed = [sem(f"landed{j}") for j in range(RQ)]
        j_in = [sem(f"j_in{b}") for b in range(JB)]
        block = ctx.enter_context(nc.Block())

        class Chain:
            def __init__(self, eng, s, at=0):
                self.eng, self.s, self.n, self.at = eng, s, 0, at

            def __call__(self, ins):
                ins.then_inc(self.s, 1)
                self.n += 1
                self.eng.wait_ge(self.s, self.at + self.n)

            def mark(self, ins):
                ins.then_inc(self.s, 1)
                self.n += 1

            def wait(self):
                self.eng.wait_ge(self.s, self.at + self.n)

        def hold(eng, name):
            eng.sem_inc(S[name], 1)

        def xin_f(a):
            g = ring32[:, 2 * NB * D:4 * NB * D]
            return g[:, a * EBLK * P:(a + 1) * EBLK * P].rearrange("p (b e) -> p b e", e=P)

        @block.sync
        def _(sp):
            full = (E // P // P) * P * P
            mid = E // P * P
            sp.wait_ge(S["e_padded"], 2)
            for a, name in ((0, "e_dst"), (1, "e_src")):
                v = dst if a == 0 else src
                t = xin[:, :, :, :].rearrange("p a b c -> p (a b c)").bitcast(I32)[:, a * 1024:a * 1024 + EBLK * P]
                t = t.rearrange("p (b e) -> p b e", e=P)
                sp.dma_start(t[:, 0:full // P // P, :], v[0:full].rearrange("(b r e) -> r b e", r=P, e=P)).then_inc(S[name], 16)
                sp.dma_start(t[0:(mid - full) // P, EBLK - 1, :], v[full:mid].rearrange("(r e) -> r e", e=P)).then_inc(S[name], 16)
                sp.dma_start(t[(mid - full) // P:(mid - full) // P + 1, EBLK - 1, 0:E - mid],
                             v[mid:E].rearrange("(a e) -> a e", a=1)).then_inc(S[name], 16)
            sp.dma_start(wkv[:, :, 0:D], wk.rearrange("(k p) n -> p k n", p=P)).then_inc(S["w_qkv"], 16)
            sp.dma_start(wkv[:, :, D:2 * D], wv.rearrange("(k p) n -> p k n", p=P)).then_inc(S["w_qkv"], 16)
            for t, v in ((wqs, wq), (wos, wo), (wgs, gnn_w)):
                sp.dma_start(t[:, :, :], v.rearrange("(k p) n -> p k n", p=P)).then_inc(S["w_qkv"], 16)
            sp.dma_start(gws[:, :, :], gate_w.rearrange("(k p) n -> p k n", p=P)).then_inc(S["w_qkv"], 16)
            for t, v in ((bks, bk), (bvs, bv), (bos, bo), (bgs, gnn_b), (gbs, gate_b)):
                sp.dma_start(t[:, :], v.partition_broadcast(P)).then_inc(S["w_qkv"], 16)
            with nc.allow_non_contiguous_dma(reason="per-partition bias columns"):
                sp.dma_start(bqs[:, :], bq.rearrange("(k p) -> p k", p=P)).then_inc(S["w_qkv"], 16)

            def load(i, nb, rows_n):
                t0 = i * NB
                if nb == NB:
                    sp.dma_start(xin[:, i % 2, :, :], x_t[bass.ds(t0, NB), :, :].rearrange("t p d -> p t d")).then_inc(S["x_in"], 16)
                else:
                    sp.dma_start(xin[0:rows_n, i % 2, 0, :], x[(NT - 1) * P:N, :]).then_inc(S["x_in"], 16)

            tab_v = table.rearrange("(t p) d -> t p d", p=P)
            nbat = NT // NB
            sp.sem_inc(S["xt_free"], 1)
            sp.sem_inc(S["tab_free"], 1)
            sp.wait_ge(S["e_copied"], 2)
            load(0, NB, P)
            sp.wait_ge(S["x_in"], 16)

            def batch(i, more):
                sp.wait_ge(S["x_out"], i + 1)
                hold(sp, "sp_hold")
                if more:
                    load(i + 1, NB, P)
                else:
                    load(i + 1, 1, LAST)
                sp.wait_ge(S["xt_sb"], i * NB + NB)
                sp.dma_start(normed_t[bass.ds(i * NB, NB), :, :].rearrange("t p n -> p t n"), xt[:, :, :]).then_inc(S["xt_st"], 16)
                sp.wait_ge(S["ln_lo"], i * NB + NB)
                sp.dma_start(tab_v[bass.ds(i * NB, NB), :, :].rearrange("t p d -> p t d"), trow[:, :, :]).then_inc(S["tab_st"], 16)
                sp.wait_ge(S["xt_st"], i * 16 + 16)
                sp.sem_inc(S["xt_free"], 1)
                sp.wait_ge(S["tab_st"], i * 16 + 16)
                sp.sem_inc(S["tab_free"], 1)
                sp.wait_ge(S["x_in"], i * 16 + 32)
                hold(sp, "sp_hold")

            with sp.Fori(0, nbat - 1) as i:
                batch(i, True)
            batch(nbat - 1, False)
            sp.wait_ge(S["xt_sb"], NT)
            sp.dma_start(normed_t[NT - 1, :, :], xt[:, 0, :]).then_inc(S["xt_st"], 16)
            sp.wait_ge(S["ln_lo"], NT)
            sp.dma_start(tab_v[NT - 1, :, :], trow[:, 0, :]).then_inc(S["tab_st"], 16)
            sp.wait_ge(S["xt_st"], 16 * (nbat + 1))

            sp.wait_ge(S["kk_ok"], NT)
            for t in range(2):
                sp.dma_start(xtin[:, t, :], normed_t[t, :, :]).then_inc(S["xt_in"], 16)
                sp.wait_ge(S["xt_in"], 16 * (t + 1))
            sp.dma_start(xres[:, 0, :], x_t[0, :, :]).then_inc(S["xr_in"], 16)
            sp.wait_ge(S["xr_in"], 16)

            def node_io(t, ahead):
                if ahead >= 1:
                    sp.wait_ge(S["q_ps"], t + 1)
                    hold(sp, "sp_hold")
                    sp.dma_start(xtin[:, t % 2, :], normed_t[bass.ds(t + 2, 1), :, :].rearrange("t p n -> p (t n)")).then_inc(S["xt_in"], 16)
                    hold(sp, "sp_hold")
                sp.wait_ge(S["xb_ok"], t + 1)
                hold(sp, "sp_hold")
                if ahead >= 1:
                    sp.dma_start(xres[:, (t + 1) % 2, :], x_t[bass.ds(t + 1, 1), :, :].rearrange("t p d -> p (t d)")).then_inc(S["xr_in"], 16)
                else:
                    sp.dma_start(xres[0:LAST, (t + 1) % 2, :], x[(NT - 1) * P:N, :]).then_inc(S["xr_in"], 16)
                sp.wait_ge(S["x1_ok"], t + 1)
                hold(sp, "sp_hold")
                sp.dma_start(out_t[bass.ds(t, 1), :, :].rearrange("t p d -> p (t d)"), rows_sb[:, t % RB, 0:D]).then_inc(S["row_st"], 16)
                sp.wait_ge(S["row_st"], t * 16 + 16)
                sp.sem_inc(S["row_stored"], 1)
                if ahead >= 1:
                    sp.wait_ge(S["xt_in"], t * 16 + 48)
                    hold(sp, "sp_hold")
                sp.wait_ge(S["xr_in"], t * 16 + 32)
                hold(sp, "sp_hold")

            with sp.Fori(0, NT - 2) as t:
                node_io(t, 2)
            node_io(NT - 2, 0)
            sp.wait_ge(S["x1_ok"], NT)
            sp.dma_start(out[(NT - 1) * P:N, :], rows_sb[0:LAST, (NT - 1) % RB, 0:D]).then_inc(S["row_st"], 16)
            sp.wait_ge(S["row_st"], 16 * NT)

            sp.wait_ge(S["scat_done"], 16 * (NT + 1))

            def load_rows(j, b):
                sp.dma_start(jrow[:, b, :], rows_t[bass.ds(j, 1), :, :].rearrange("t p d -> p (t d)")).then_inc(j_in[b], 16)
            def report(i, b):
                sp.wait_ge(j_in[b], i * 16 + 16)
                hold(sp, "sp_hold")
                sp.sem_inc(S["j_ready"], 1)
            for b in range(JB):
                load_rows(b, b)
            for b in range(JB - 1):
                report(0, b)
            with sp.Fori(0, NX * JOBS // JB - 1) as i:
                for b in range(JB):
                    sp.wait_ge(S["j_free"], i * JB + b + 1)
                    hold(sp, "sp_hold")
                    load_rows(i * JB + b + JB, b)
                    if b == 0:
                        report(i, JB - 1)
                    else:
                        report(i + 1, b - 1)
            report(NX * JOBS // JB - 1, JB - 1)
            sp.wait_ge(S["fin_sc"], 16 * NX * JOBS)
            sp.wait_ge(S["tab_st"], 16 * (nbat + 1))

        @block.gpsimd
        def _(g):
            edges = xin[:, :, :, :].rearrange("p a b c -> p (a b c)").bitcast(I32)
            g.memset(edges[:, 0:1024], int(PAD_DST)).then_inc(S["e_padded"], 1)
            g.memset(edges[:, 1024:2048], 0).then_inc(S["e_padded"], 1)
            g.iota(iota_i[:, :], [[1, P]], base=0, channel_multiplier=0).then_inc(S["iota_ok"], 1)
            g.iota(chunk_i[:, :], [[P, EBLK]], base=0, channel_multiplier=1).then_inc(S["iota_ok"], 1)
            g.memset(ident[:, :], 0.0).then_inc(S["consts"], 1)
            g.memset(tri[:, :], 1.0).then_inc(S["consts"], 1)
            g.memset(c16[:, 1:4, :], 1.0).then_inc(S["consts"], 1)
            g.memset(zero16, 0.0).then_inc(S["consts"], 1)
            g.memset(eps[:, :], EPS).then_inc(S["consts"], 1)
            g.memset(vv[:, :, :], 1.0).then_inc(S["consts"], 1)
            g.wait_ge(S["consts"], 6)
            g.affine_select(out=ident[:, :], in_=ident[:, :], compare_op=ALU.not_equal, fill=1.0, base=0,
                            pattern=[[-1, P]], channel_multiplier=1).then_inc(S["ident_ok"], 1)
            g.affine_select(out=tri[:, :], in_=tri[:, :], compare_op=ALU.is_ge, fill=0.0, base=0,
                            pattern=[[1, P]], channel_multiplier=-1).then_inc(S["ident_ok"], 1)

            def keys(t, j):
                g.wait_ge(S["ln_hi"], t + 1)
                g.tensor_tensor(dif[:, j, :], xn[:, j, :], trow[:, j, 0:D], ALU.subtract).then_inc(S["ln_dif"], 1)

            def keys2(t):
                g.wait_ge(S["kv_used"], t + 1)
                hold(g, "pool_hold")
                g.wait_ge(S["ke_ok"], t + 1)
                g.tensor_tensor(kk[:, :], kr, ke, ALU.add).then_inc(S["kk_ok"], 1)

            with g.Fori(0, NT // NB) as i:
                for j in range(NB):
                    keys(i * NB + j, j)
                for j in range(NB):
                    keys2(i * NB + j)
            keys(NT - 1, 0)
            keys2(NT - 1)

            g.wait_ge(S["rows_z"], 1)
            g.dma_start(rows_t.rearrange("s p d -> p s d"), empty.rearrange("p (a d) -> p a d", a=1).broadcast_to([P, NX * JOBS, ROW])).then_inc(S["scat_done"], 16)
            g.wait_ge(S["scat_done"], 16)

            def scatter(t):
                g.wait_ge(S["scat_done"], t * 16 + 16)
                g.sem_inc(S["row_free"], 1)
                g.wait_ge(S["row_ok"], t + 1)
                hold(g, "pool_hold")

                def send(b):
                    g.indirect_dma_start(rows[:, :], bass.IndirectOffsetOnAxis(ap=row_at[:, b:b + 1], axis=0), rows_sb[:, b, :], None,
                                         bounds_check=NX * SLOTS - 1, oob_is_err=False).then_inc(S["scat_done"], 16)
                with g.If(t % RB < RB // 2):
                    with g.If(t % RB < 1):
                        send(0)
                    with g.Else():
                        send(1)
                    g.sem_inc(S["pool_hold"], 1)
                with g.Else():
                    with g.If(t % RB < RB - 1):
                        send(2)
                    with g.Else():
                        send(3)
                    g.sem_inc(S["pool_hold"], 1)
                g.sem_inc(S["pool_hold"], 1)

            g.wait_ge(S["tab_st"], 16 * (NT // NB + 1))
            g.wait_ge(S["xt_st"], 16 * (NT // NB + 1))
            g.wait_ge(S["spans_ok"], 1)
            ends = [g.value_load(spans[0:1, 4, 0:1], min_val=EB, max_val=EB * NT)]

            def events(tile, tend, f):
                with g.While(lambda: g.snap(tend) < f - (RQ - 1)):
                    scatter(g.snap(tile))
                    g.reg_add(tile, tile, 1)
                    g.load(tend, spans[0:1, 1, bass.ds(g.snap(tile) + AFTER, 1)])
                g.sem_inc(S["pool_hold"], 1)

            def gather(i, s, tile=None, tend=None):
                first = isinstance(i, int) and i == 0
                f = i * RQ + s
                if s % 2 == 0:
                    g.tensor_copy(idx[:, s * G:(s + 2) * G], src_t[:, bass.ds((i % EB) * RING + s * G, 2 * G)]).then_inc(S["idx_ok"], 1)
                    g.wait_ge(S["idx_ok"], i * 2 + s // 2 + 1)
                    hold(g, "pool_hold")
                if not first:
                    events(tile, tend, f)
                g.wait_ge(S["slots"], f + 1)
                hold(g, "pool_hold")
                for j in range(s * G, (s + 1) * G):
                    g.indirect_dma_start(gathered[:, j, :], None, table[:, :],
                                         bass.IndirectOffsetOnAxis(ap=idx[:, j:j + 1], axis=0)).then_inc(landed[s], 16)
                if not (first and s == 0):
                    g.wait_ge(landed[(s - 1) % RQ], (i + 1) * 16 * G if s > 0 else i * 16 * G)
                    g.sem_inc(S["relayed"], 1)

            for s in range(RQ):
                gather(0, s)
            with g.register("tile_no") as tile, g.register("tile_end") as tend:
                g.reg_mov(tile, 0)
                g.load(tend, spans[0:1, 1, AFTER:AFTER + 1])
                with g.Fori(1, ends[0]) as i:
                    for s in range(RQ):
                        gather(i, s, tile, tend)
                g.wait_ge(landed[RQ - 1], ends[0] * 16 * G)
                g.sem_inc(S["relayed"], 1)
                with g.Fori(g.snap(tile), NT) as t:
                    scatter(t)

            with g.Fori(0, NX * JOBS // 2) as i:
                for b in range(2):
                    g.wait_ge(S["fin_ok"], i * 2 + b + 1)
                    hold(g, "pool_hold")
                    g.indirect_dma_start(out[:, :], bass.IndirectOffsetOnAxis(ap=jtok[:, b:b + 1], axis=0),
                                         fin[:, b, :], None,
                                         bounds_check=N - 1, oob_is_err=False).then_inc(S["fin_sc"], 16)
                    g.wait_ge(S["fin_sc"], i * 32 + b * 16 + 16)
                    g.sem_inc(S["fin_free"], 1)

        @block.scalar
        def _(a):
            for e in range(NX):
                a.dma_start(w1s[:, e, :, :], w1[e, :, :].rearrange("(k p) f -> p k f", p=P)).then_inc(S["w_big"], 16)
                a.dma_start(w2s[:, e, :, :], w2[e, :, :].rearrange("(c p) d -> p c d", p=P)).then_inc(S["w_big"], 16)
            with nc.allow_non_contiguous_dma(reason="hidden bias to columns"):
                a.dma_start(b1s[:, :], b1.rearrange("e (c p) -> p (e c)", p=P)).then_inc(S["w_big"], 16)
            a.dma_start(b2s[:, :, :].rearrange("p e d -> p (e d)"), b2.rearrange("e d -> (e d)").partition_broadcast(P)).then_inc(S["w_big"], 16)

            a.wait_ge(S["consts"], 6)

            def norm(i, nb):
                t0 = i * NB
                a.wait_ge(S["ln_stats"], i + 1)
                a.activation(std[:, 0:nb], mv[:, 0:nb, 1], ACT.Sqrt, bias=eps[:, 0:1]).then_inc(S["ln_std"], 1)
                for j in range(nb):
                    if j == 0:
                        a.wait_ge(S["tab_free"], i + 1)
                        a.sem_inc(S["act_hold"], 1)
                    a.wait_ge(S["ln_xn"], t0 + j + 1)
                    a.activation(trow[:, j, 0:D], xn[:, j, :], ACT.Copy).then_inc(S["ln_hi"], 1)
                for j in range(nb):
                    a.wait_ge(S["ln_dif"], t0 + j + 1)
                    a.activation(trow[:, j, D:2 * D], dif[:, j, :], ACT.Copy, scale=LO).then_inc(S["ln_lo"], 1)
                for j in range(nb):
                    t = t0 + j
                    a.wait_ge(S["kv_used"], t + 1)
                    a.sem_inc(S["act_hold"], 1)
                    a.wait_ge(S["kb_ok"], t + 1)
                    a.activation(vv[:, :, 0:P], pQ[:, D:2 * D].rearrange("p (k n) -> p k n", k=DK), ACT.Copy).then_inc(S["v_ok"], 1)
                    a.activation(kr, kb, ACT.Relu).then_inc(S["kr_ok"], 1)
                    a.wait_ge(S["km_ok"], t + 1)
                    a.activation(ke, km, ACT.Exp).then_inc(S["ke_ok"], 1)

            with a.Fori(0, NT // NB) as i:
                norm(i, NB)
            norm(NT // NB, 1)

            def query(t):
                a.wait_ge(S["q_ps"], t + 1)
                for out_, f in ((qr, ACT.Relu), (qe, ACT.Exp)):
                    for k in range(DK):
                        ins = a.activation(out_[:, k * P:(k + 1) * P], pQ[:, k * P:(k + 1) * P], f, bias=bqs[:, k:k + 1])
                ins.then_inc(S["qe_ok"], 1)

            def gate_in(t):
                a.wait_ge(S["x2t_ps"], t + 1)
                a.activation(x2t, pH0[:, 0:D], ACT.Copy).then_inc(S["x2t_sb"], 1)

            def softmax(t):
                a.wait_ge(S["nmx_ok"], t + 1)
                a.activation(lg[:, 1, :], lg[:, 0, :], ACT.Exp, bias=sc[:, 4:5], accum_out=sc[:, 5:6]).then_inc(S["ex_ok"], 1)

            def node(t, first=False, final=False):
                a.wait_ge(S["dg_ok"], t + 1)
                a.activation(ahi, pA[:, 0:D], ACT.Copy, scale=deg[:, 1:2]).then_inc(S["ahi_ok"], 1)
                a.wait_ge(S["ot_ps"], t + 1)
                a.activation(ot, pH1[:, 0:D], ACT.Copy).then_inc(S["ot_sb"], 1)
                if not first:
                    gate_in(t - 1)
                if not final:
                    query(t + 1)
                a.wait_ge(S["agt_ps"], t + 1)
                a.activation(agt, pT[:, 0:D], ACT.Copy).then_inc(S["agt_sb"], 1)
                if not first:
                    softmax(t - 1)
                a.wait_ge(S["st_ok"], t + 1)
                a.activation(sc[:, 2:3], sc[:, 1:2], ACT.Sqrt, bias=eps[:, 0:1]).then_inc(S["sd_ok"], 1)
                a.wait_ge(S["nm_ok"], t + 1)
                a.sem_inc(S["act_hold"], 1)
                a.activation(x2, rows_sb[:, t % RB, 0:D], ACT.Identity, scale=rn[:, 0:1], bias=rn[:, 1:2]).then_inc(S["x2_ok"], 1)

            query(0)
            node(0, first=True)
            with a.Fori(1, NT - 1) as t:
                node(t)
            node(NT - 1, final=True)
            gate_in(NT - 1)
            softmax(NT - 1)

            def columns(j):
                a.wait_ge(S["xjt_ps"], j + 1)
                a.activation(xjt, pT[:, 0:D], ACT.Copy).then_inc(S["xjt_sb"], 1)
            columns(0)

            def job(e, i, more=True):
                j = e * JOBS + i
                a.wait_ge(S["h0_ps"], j + 1)
                for c in range(FC // 2):
                    ins = a.activation(hs[:, c, :], pH0[:, c * P:(c + 1) * P], ACT.Relu, bias=b1s[:, bass.ds(e * FC + c, 1)])
                ins.then_inc(S["h0_sb"], 1)
                if more:
                    columns(j + 1)
            with a.Fori(0, NX - 1) as e:
                with a.Fori(0, JOBS) as i:
                    job(e, i)
            with a.Fori(0, JOBS - 1) as i:
                job(NX - 1, i)
            job(NX - 1, JOBS - 1, False)

        @block.tensor
        def _(pe):
            pe.wait_ge(S["ident_ok"], 2)
            for a, (b0, b1_) in enumerate(((pT, pQ), (pS, pY))):
                pe.wait_ge(S["e_f32"], a + 1)
                for b in range(EBLK):
                    o = (b0, b1_)[b // 4][:, (b % 4) * P:(b % 4 + 1) * P]
                    ins = pe.transpose(o, xin_f(a)[:, b, :], ident[:, :])
                ins.then_inc(S["e_ps"], 1)
            pe.wait_ge(S["e_copied"], 2)
            pe.wait_ge(S["e_bound"], 1)
            for a in range(2):
                ins = pe.transpose(pS[0:NT, a * P:(a + 1) * P], bounds[:, a, :], ident[:, :])
            ins.then_inc(S["e_bt"], 1)
            pe.wait_ge(S["e_lohi"], 1)
            for a in range(2):
                ins = pe.matmul(pT[0:1, a * 64:a * 64 + NT], lohi[:, a:a + 1], ident[0:NT, 0:NT], start=True, stop=True)
            ins.then_inc(S["e_rowps"], 1)
            pe.wait_ge(S["e_row"], 1)
            pe.matmul(pS[0:NT, 0:1], new_row[0:1, 0:NT], ident[0:1, 0:1], start=True, stop=True).then_inc(S["e_newps"], 1)
            pe.wait_ge(S["e_new"], 1)
            pe.matmul(pT[0:1, 0:NT], new_col[:, :], tri[0:NT, 0:NT], start=True, stop=True).then_inc(S["e_baseps"], 1)

            kvp = (pH0, pH1)
            for k in range(DK):
                pe.matmul(kvp[k][:, 0:P + 1], zero16, any16[:, 0:P + 1], start=True, stop=False)
            pe.wait_ge(S["w_qkv"], 16 * 12)
            pe.wait_ge(S["spans_ok"], 1)

            def keys(t, j, rows_n, last):
                pe.wait_ge(S["ln_xn"], t + 1)
                if j >= 0:
                    pe.sem_inc(S["pe_hold"], 1)
                for k in range(DK):
                    ins = pe.transpose(pT[:, k * P:(k + 1) * P], xn[:, j, k * P:(k + 1) * P], ident[:, :])
                ins.then_inc(S["xt_ps"], 1)
                pe.wait_ge(S["xt_sb"], t + 1)
                for k in range(DK):
                    ins = pe.matmul(pQ[:, :], xt[:, j, k * P:(k + 1) * P], wkv[:, k, :], start=(k == 0), stop=(k == DK - 1))
                ins.then_inc(S["kv_ps"], 1)
                pe.wait_ge(S["kk_ok"], t + 1)
                pe.sem_inc(S["pe_hold"], 1)
                pe.wait_ge(S["v_ok"], t + 1)
                for k in range(DK):
                    ins = pe.matmul(kvp[k][:, 0:P + 1], kk[0:rows_n, k * P:(k + 1) * P], vv[0:rows_n, k, :], start=False, stop=last)
                ins.then_inc(S["kv_used"], 1)

            pe.sem_inc(S["kv_used"], 1)
            with pe.Fori(0, NT // NB) as i:
                for j in range(NB):
                    keys(i * NB + j, j, P, False)
            keys(NT - 1, 0, LAST, True)

            pe.wait_ge(S["kvm_ok"], 1)
            pe.sem_inc(S["slots"], RQ)
            pe.sem_inc(S["oh_slots"], OQ)
            with pe.register("held") as at_r, pe.register("pair") as pair_r:
                pe.reg_mov(at_r, 0)
                pe.reg_mov(pair_r, 1)

                def query(t):
                    pe.wait_ge(S["xt_in"], t * 16 + 16)
                    for m in range(DK):
                        for k in range(DK):
                            ins = pe.matmul(pQ[:, m * P:(m + 1) * P], wqs[:, k, m * P:(m + 1) * P], xtin[:, t % 2, k * P:(k + 1) * P],
                                            start=(k == 0), stop=(k == DK - 1))
                    ins.then_inc(S["q_ps"], 1)

                def read_out(t):
                    pe.wait_ge(S["qt_ok"], t + 1)
                    for k in range(DK):
                        ins = pe.matmul(pQ[:, k * (P + HB):(k + 1) * (P + HB)], qt[:, k * P:(k + 1) * P], kvm[:, k, :], start=True, stop=True)
                    ins.then_inc(S["att_ps"], 1)

                def sum_rows(t):
                    lo = pe.value_load(spans[0:1, 0, bass.ds(t, 1)], min_val=0, max_val=EQ * NT)
                    last = pe.value_load(spans[0:1, 1, bass.ds(t, 1)], min_val=0, max_val=EQ * NT)
                    at = pe.snap(at_r)
                    with pe.If(at < lo):
                        with pe.Fori(at, lo) as f:
                            pe.wait_ge(S["relayed"], f + 1)
                            pe.sem_inc(S["slots"], 1)
                        pe.sem_inc(S["pe_hold"], 1)
                    pe.matmul(pA[:, :], zero16, any16, start=True, stop=False)
                    pe.matmul(pD[:, 0:1], zero16, any16[:, 0:1], start=True, stop=False)

                    def add(f, final):
                        n = pe.snap(pair_r)
                        pe.wait_ge(S["relayed"], f + 1)
                        pe.sem_inc(S["pe_hold"], 1)
                        pe.wait_ge(S["oh_ready"], n)
                        for j in range(G):
                            stop = final and j == G - 1
                            m = pe.matmul(pA[:, :], onehot[:, n % OQ, j, :], gathered[:, (f % RQ) * G + j, :], start=False, stop=stop)
                            if j == G - 1 and not final:
                                m.then_inc(S["slots"], 1)
                            m = pe.matmul(pD[:, 0:1], onehot[:, n % OQ, j, :], ones16[:, 0:1], start=False, stop=stop)
                        m.then_inc(S["oh_slots"], 1)
                        pe.reg_add(pair_r, pair_r, 1)

                    with pe.If(lo < last):
                        with pe.Fori(lo, last) as f:
                            add(f, False)
                        pe.sem_inc(S["pe_hold"], 1)
                    add(last, True)
                    pe.matmul(pD[:, 1:2], zero16, any16[:, 0:1], start=True, stop=True).then_inc(S["agg_done"], 1)
                    pe.reg_mov(at_r, last)

                def gate_in(t):
                    pe.wait_ge(S["x2_ok"], t + 1)
                    for k in range(DK):
                        ins = pe.transpose(pH0[:, k * P:(k + 1) * P], x2[:, k * P:(k + 1) * P], ident[:, :])
                    ins.then_inc(S["x2t_ps"], 1)

                def gate(t):
                    pe.wait_ge(S["x2t_sb"], t + 1)
                    for k in range(DK):
                        ins = pe.matmul(pS[:, 0:NX], x2t[:, k * P:(k + 1) * P], gws[:, k, :], start=(k == 0), stop=(k == DK - 1))
                    ins.then_inc(S["lg_ps"], 1)

                def count(t):
                    pe.wait_ge(S["oh_ok"], t + 1)
                    pe.matmul(pS[:, NX:2 * NX], tri16, oh16[:, :], start=True, stop=False)
                    pe.matmul(pS[:, NX:2 * NX], ones16, cnt16[:, :], start=False, stop=True).then_inc(S["pos_ps"], 1)

                def node(t, first=False, final=False):
                    sum_rows(t)
                    pe.wait_ge(S["o_ok"], t + 1)
                    for k in range(DK):
                        ins = pe.transpose(pH1[:, k * P:(k + 1) * P], o_sb[:, k * P:(k + 1) * P], ident[:, :])
                    ins.then_inc(S["ot_ps"], 1)
                    if not first:
                        gate_in(t - 1)
                    if not final:
                        query(t + 1)
                    pe.wait_ge(S["agg_ok"], t + 1)
                    for k in range(DK):
                        ins = pe.transpose(pT[:, k * P:(k + 1) * P], agg[:, k * P:(k + 1) * P], ident[:, :])
                    ins.then_inc(S["agt_ps"], 1)
                    if not first:
                        gate(t - 1)
                    pe.wait_ge(S["ot_sb"], t + 1)
                    for k in range(DK):
                        pe.matmul(pY[:, 0:D], ot[:, k * P:(k + 1) * P], wos[:, k, :], start=(k == 0), stop=False)
                    pe.wait_ge(S["agt_sb"], t + 1)
                    for k in range(DK):
                        ins = pe.matmul(pY[:, 0:D], agt[:, k * P:(k + 1) * P], wgs[:, k, :], start=False, stop=(k == DK - 1))
                    ins.then_inc(S["x1_ps"], 1)
                    if not final:
                        read_out(t + 1)
                    if not first:
                        count(t - 1)

                query(0)
                read_out(0)
                node(0, first=True)
                with pe.Fori(1, NT - 1) as t:
                    node(t)
                node(NT - 1, final=True)
                gate_in(NT - 1)
                pe.wait_ge(S["row_ok"], NT - 1)
                pe.sem_inc(S["pe_hold"], 1)
                gate(NT - 1)
                count(NT - 1)

            pe.wait_ge(S["w_big"], 16 * 18)

            def columns(j):
                pe.wait_ge(S["xj_ok"], j + 1)
                for k in range(DK):
                    ins = pe.transpose(pT[:, k * P:(k + 1) * P], xj[:, k * P:(k + 1) * P], ident[:, :])
                ins.then_inc(S["xjt_ps"], 1)
            columns(0)

            def job(e, i, more=True):
                j = e * JOBS + i
                pe.wait_ge(S["xjt_sb"], j + 1)
                for c in range(FC):
                    ph = (pH0, pH1)[c // 4]
                    for k in range(DK):
                        ins = pe.matmul(ph[:, (c % 4) * P:(c % 4 + 1) * P], w1s[:, e, k, c * P:(c + 1) * P],
                                        xjt[:, k * P:(k + 1) * P], start=(k == 0), stop=(k == DK - 1))
                    if c % 4 == 3:
                        ins.then_inc(S["h0_ps" if c == 3 else "h1_ps"], 1)
                if more:
                    columns(j + 1)
                pe.wait_ge(S["y_used"], j + 1)
                pe.sem_inc(S["pe_hold"], 1)
                for c in range(FC):
                    if c % 4 == 0:
                        pe.wait_ge(S["h0_sb" if c == 0 else "h1_sb"], j + 1)
                    ins = pe.matmul(pY[:, 0:D], hs[:, c, :], w2s[:, e, c, :], start=(c == 0), stop=(c == FC - 1))
                ins.then_inc(S["y_ps"], 1)
            for e in range(NX):
                with pe.Fori(0, JOBS if e < NX - 1 else JOBS - 1) as i:
                    job(e, i)
            job(NX - 1, JOBS - 1, False)

        @block.vector
        def _(v):
            c = Chain(v, S["dve_c"])
            v.wait_ge(S["iota_ok"], 2)
            c.mark(v.tensor_copy(iota_row[:, :], iota_i[:, :]))
            c.mark(v.tensor_scalar(expert_m8[:, :], iota_i[:, 0:NX], float(-NX), None, ALU.add))
            c.mark(v.tensor_copy(chunk_id[:, :], chunk_i[:, :]))
            c.mark(v.memset(cnt16[:, :], 0.0))
            v.wait_ge(S["ident_ok"], 2)
            c.mark(v.tensor_copy(tri16, tri[:, :]))
            c.mark(v.memset(kvm[:, :, :], 0.0))
            c.mark(v.memset(new_row[:, :], 0.0))
            c.mark(v.memset(spans[:, :, :], 1 << 30))
            edges = xin[:, :, :, :].rearrange("p a b c -> p (a b c)").bitcast(I32)
            for a, name in ((0, "e_dst"), (1, "e_src")):
                v.wait_ge(S[name], 48)
                v.tensor_copy(xin_f(a).rearrange("p b e -> p (b e)"), edges[:, a * 1024:a * 1024 + EBLK * P]).then_inc(S["e_f32"], 1)
            v.wait_ge(S["e_f32"], 2)
            c.mark(v.tensor_reduce(cmin[:, :], xin_f(0), AX, ALU.min))
            c(v.tensor_reduce(cmax[:, :], xin_f(0), AX, ALU.max))
            for a, (b0, b1_) in enumerate(((pT, pQ), (pS, pY))):
                v.wait_ge(S["e_ps"], a + 1)
                t = (dst_t, src_t)[a]
                v.tensor_copy(t[:, 0:512], b0[:, :])
                v.tensor_copy(t[:, 512:ECP], b1_[:, 0:ECP - 512]).then_inc(S["e_copied"], 1)
            sel = xn[:, :, :].rearrange("p a b -> p (a b)")
            m0 = sel[:, 0:NT * EBLK].rearrange("p (t b) -> p t b", b=EBLK)
            m1 = sel[:, 512:512 + NT * EBLK].rearrange("p (t b) -> p t b", b=EBLK)
            thr = kk[:, 0:NT]
            c(v.tensor_scalar(thr, iota_row[:, 0:NT], float(P), None, ALU.mult))

            def wide(ap):
                return ap.rearrange("p (a b) -> p a b", a=1).broadcast_to([P, NT, EBLK])
            thr_w = thr.rearrange("p (t a) -> p t a", a=1).broadcast_to([P, NT, EBLK])
            c(v.tensor_tensor(m0, wide(cmax[:, :]), thr_w, ALU.is_ge))
            ids_lo, ids_hi = lg[:, 0, 0:EBLK], lg[:, 1, 0:EBLK]
            c.mark(v.tensor_scalar(ids_lo, chunk_id[:, :], -BIG, None, ALU.add))
            c.mark(v.tensor_scalar(ids_hi, chunk_id[:, :], 1.0, None, ALU.add))
            c(v.tensor_scalar(thr, thr, float(P), None, ALU.add))
            c(v.tensor_tensor(m1, wide(cmin[:, :]), thr_w, ALU.is_lt))
            c(v.tensor_tensor(m0, m0, wide(ids_lo), ALU.mult))
            c(v.tensor_tensor(m1, m1, wide(ids_hi), ALU.mult))
            c.mark(v.tensor_reduce(bounds[:, 0, :], m0, AX, ALU.min))
            c(v.tensor_reduce(bounds[:, 1, :], m1, AX, ALU.max))
            v.sem_inc(S["e_bound"], 1)
            v.wait_ge(S["e_bt"], 1)
            c.mark(v.tensor_reduce(lohi[:, 0:1], pS[0:NT, 0:P], AX, ALU.min))
            c(v.tensor_reduce(lohi[:, 1:2], pS[0:NT, P:2 * P], AX, ALU.max))
            c(v.tensor_scalar(lohi[:, 0:1], lohi[:, 0:1], BIG, float(EC - 1), ALU.add, ALU.min))
            c(v.tensor_scalar(new_col[:, :], lohi[:, 0:1], 1.0, None, ALU.add))
            c(v.tensor_tensor(lohi[:, 1:2], lohi[:, 1:2], new_col[:, :], ALU.max))
            c.mark(v.tensor_scalar(lohi[:, 0:1], lohi[:, 0:1], 1.0 / G, -(G - 1) / (2.0 * G), ALU.mult, ALU.add))
            c(v.tensor_scalar(lohi[:, 1:2], lohi[:, 1:2], 1.0 / G, (G - 1) / (2.0 * G), ALU.mult, ALU.add))
            c(v.tensor_scalar(lohi[:, :], lohi[:, :], 2.0 ** 23, None, ALU.add))
            c(v.tensor_scalar(lohi[:, :], lohi[:, :], -2.0 ** 23, None, ALU.add))
            v.sem_inc(S["e_lohi"], 1)
            v.wait_ge(S["e_rowps"], 1)
            c(v.tensor_copy(lh_row[0:1, :, 0:NT], pT[0:1, 0:2 * 64].rearrange("p (a t) -> p a t", a=2)[:, :, 0:NT]))
            c(v.scalar_tensor_tensor(new_row[0:1, 1:NT], lh_row[0:1, 1, 0:NT - 1], -1.0, lh_row[0:1, 0, 1:NT], ALU.add, ALU.is_gt))
            v.sem_inc(S["e_row"], 1)
            v.wait_ge(S["e_newps"], 1)
            c(v.tensor_copy(new_col[:, :], pS[0:NT, 0:1]))
            v.sem_inc(S["e_new"], 1)
            v.wait_ge(S["e_baseps"], 1)
            c(v.tensor_scalar(base_row[0:1, 0:NT], pT[0:1, 0:NT], float(EQ), None, ALU.mult))
            c.mark(v.tensor_copy(spans[0:1, 2:4, 0:NT], lh_row[0:1, :, 0:NT]))
            c.mark(v.tensor_tensor(spans[0:1, 0, 0:NT], lh_row[0:1, 0, 0:NT], base_row[0:1, 0:NT], ALU.add))
            c.mark(v.scalar_tensor_tensor(spans[0:1, 1, 0:NT], lh_row[0:1, 1, 0:NT], -1.0, base_row[0:1, 0:NT], ALU.add, ALU.add))
            c(v.tensor_scalar(spans[0:1, 4, 0:1], base_row[0:1, NT - 1:NT], 1.0 / RQ, float(EB), ALU.mult, ALU.add))
            c.mark(v.tensor_scalar(new_row[0:1, 0:NT], lh_row[0:1, 0, 0:NT], float(EARLY), None, ALU.add))
            c.wait()
            c(v.tensor_tensor(spans[0:1, 5, 0:NT], new_row[0:1, 0:NT], lh_row[0:1, 1, 0:NT], ALU.min))
            v.sem_inc(S["spans_ok"], 1)
            c0 = c.n

            K1 = 3
            v.sem_inc(S["x_out"], 1)

            def keys(i, nb):
                t0 = i * NB
                k = Chain(v, S["dve_c"], c0 + i * K1)
                v.wait_ge(S["x_in"], i * 16 + 16)
                hold(v, "dve_hold")
                for j in range(nb):
                    ins = v.bn_stats(stats[:, j, :], xin[:, i % 2, j, :])
                k(ins)
                hold(v, "dve_hold")
                for j in range(nb):
                    ins = v.bn_aggr(mv[:, j, :], stats[:, j, :])
                ins.then_inc(S["ln_stats"], 1)
                v.wait_ge(S["ln_std"], i + 1)
                k(v.reciprocal(rstd[:, 0:nb], std[:, 0:nb]))
                for j in range(nb):
                    ins = v.tensor_scalar(xn[:, j, :], xin[:, i % 2, j, :], mv[:, j, 0:1], rstd[:, j:j + 1], ALU.subtract, ALU.mult)
                    ins.then_inc(S["ln_xn"], 1)
                k(v.memset(sc[:, 11:12], 0.0))
                v.sem_inc(S["x_out"], 1)
                assert k.n == K1
                for j in range(nb):
                    t = t0 + j
                    if j == 0:
                        v.wait_ge(S["xt_free"], i + 1)
                        v.sem_inc(S["dve_hold"], 1)
                    v.wait_ge(S["xt_ps"], t + 1)
                    v.tensor_copy(xt[:, j, :], pT[:, 0:D]).then_inc(S["xt_sb"], 1)
                    v.wait_ge(S["kv_ps"], t + 1)
                    v.tensor_tensor(kb, pQ[:, 0:D], bks[:, :], ALU.add).then_inc(S["kb_ok"], 1)
                    v.wait_ge(S["kb_ok"], t + 1)
                    v.tensor_scalar(km, kb, 0.0, None, ALU.min).then_inc(S["km_ok"], 1)
                v.wait_ge(S["ln_dif"], t0 + nb)
                v.sem_inc(S["dve_hold"], 1)

            with v.Fori(0, NT // NB) as i:
                keys(i, NB)
            keys(NT // NB, 1)
            c1 = c0 + (NT // NB + 1) * K1

            c = Chain(v, S["dve_c"], c1)
            v.wait_ge(S["kv_used"], NT + 1)
            for k in range(DK):
                ps = (pH0, pH1)[k]
                for h in range(HB):
                    r = slice(h * HD, (h + 1) * HD)
                    c.mark(v.tensor_copy(kvm[r, k, P + h:P + h + 1], ps[r, P:P + 1]))
            c.wait()
            for k in range(DK):
                ps = (pH0, pH1)[k]
                for h in range(HB):
                    r = slice(h * HD, (h + 1) * HD)
                    c.mark(v.scalar_tensor_tensor(kvm[r, k, h * HD:(h + 1) * HD], bvs[r, k * P + h * HD:k * P + (h + 1) * HD],
                                                  kvm[r, k, P + h:P + h + 1], ps[r, h * HD:(h + 1) * HD], ALU.mult, ALU.add))
            c.mark(v.memset(empty[:, 0:C_TOK], 0.0))
            c.mark(v.memset(empty[:, C_TOK:ROW].bitcast(I32), N))
            c.mark(v.tensor_copy(tile_iota[:, :], iota_row[:, :]))
            c(v.tensor_copy(tok[:, :], chunk_id[:, 0:1]))
            v.sem_inc(S["rows_z"], 1)
            v.sem_inc(S["kvm_ok"], 1)
            v.sem_inc(S["xb_ok"], 1)
            v.sem_inc(S["row_stored"], RB)
            v.sem_inc(S["row_free"], RB - 1)
            v.sem_inc(S["fin_free"], 2)
            c2 = c1 + c.n

            K = {"place_c": 1, "agg_c": 5, "att_c": 2, "x1_c": 4, "route_c": 4, "route2_c": 9, "tile_c": 1}

            def part(name, t):
                return Chain(v, S[name], t * K[name])

            with v.register("pair_v") as pair_r:
                v.reg_mov(pair_r, 1)

                def one_hots(lo, hi):
                    with v.Fori(lo, hi) as ch:
                        n = v.snap(pair_r)
                        v.wait_ge(S["oh_slots"], n)
                        v.tensor_tensor(onehot[:, n % OQ, :, :],
                                        tile_iota[:, :].rearrange("p (a n) -> p a n", a=1).broadcast_to([P, G, P]),
                                        dst_t[:, bass.ds(ch * G, G)].rearrange("p (g a) -> p g a", a=1).broadcast_to([P, G, P]),
                                        ALU.is_equal).then_inc(S["oh_ready"], 1)
                        v.reg_add(pair_r, pair_r, 1)

                def span(row, t, **kw):
                    return v.value_load(spans[0:1, row, bass.ds(t, 1)], **kw)

                def early(t):
                    one_hots(span(2, t, min_val=0, max_val=EQ - 1), span(5, t, min_val=1, max_val=EQ))

                def late(t):
                    lo, hi = span(5, t, min_val=1, max_val=EQ), span(3, t, min_val=1, max_val=EQ)
                    with v.If(lo < hi):
                        one_hots(lo, hi)
                        v.sem_inc(S["dve_hold"], 1)

                def queries(t):
                    v.wait_ge(S["qe_ok"], t + 1)
                    v.scalar_tensor_tensor(qt, qe, 1.0, qr, ALU.min, ALU.add).then_inc(S["qt_ok"], 1)

                def attend(t):
                    k = part("att_c", t)
                    v.wait_ge(S["att_ps"], t + 1)
                    att = pQ[:, 0:DK * (P + HB)].rearrange("p (k n) -> p k n", k=DK)
                    k(v.tensor_scalar(rden[:, :].rearrange("p (k h) -> p k h", k=DK), att[:, :, P:P + HB], 1e-6, None, ALU.add))
                    k(v.reciprocal(rden[:, :], rden[:, :]))
                    for m in range(DK):
                        ins = v.tensor_tensor(o_sb[:, m * P:(m + 1) * P].rearrange("p (h d) -> p h d", d=HD),
                                              att[:, m, 0:P].rearrange("p (h d) -> p h d", d=HD),
                                              rden[:, m * HB:(m + 1) * HB].rearrange("p (h a) -> p h a", a=1).broadcast_to([P, HB, HD]), ALU.mult)
                    ins.then_inc(S["o_ok"], 1)
                    assert k.n == K["att_c"]

                def mean(t):
                    k = part("agg_c", t)
                    v.wait_ge(S["agg_done"], t + 1)
                    k.mark(v.tensor_scalar(deg[:, 2:3], pD[:, 0:1], 1.0, None, ALU.min))
                    k(v.tensor_scalar(deg[:, 0:1], pD[:, 0:1], 1.0, None, ALU.max))
                    v.reciprocal(deg[:, 1:2], deg[:, 0:1]).then_inc(S["dg_ok"], 1)
                    v.wait_ge(S["dg_ok"], t + 1)
                    k.mark(v.tensor_scalar(deg[:, 3:4], deg[:, 1:2], 1.0 / LO, None, ALU.mult))
                    v.wait_ge(S["xr_in"], t * 16 + 16)
                    k(v.tensor_tensor(xb, xres[:, t % 2, :], bos[:, :], ALU.add))
                    v.wait_ge(S["ahi_ok"], t + 1)
                    v.scalar_tensor_tensor(agg, pA[:, D:2 * D], deg[:, 3:4], ahi, ALU.mult, ALU.add).then_inc(S["agg_ok"], 1)
                    k(v.scalar_tensor_tensor(xb, bgs[:, :], deg[:, 2:3], xb, ALU.mult, ALU.add))
                    v.sem_inc(S["xb_ok"], 1)
                    assert k.n == K["agg_c"]

                def residual(t):
                    k = part("x1_c", t)
                    v.wait_ge(S["row_stored"], t + 1)
                    v.sem_inc(S["dve_hold"], 1)
                    v.wait_ge(S["row_free"], t + 1)
                    v.sem_inc(S["dve_hold"], 1)
                    v.wait_ge(S["x1_ps"], t + 1)
                    v.tensor_tensor(rows_sb[:, t % RB, 0:D], pY[:, 0:D], xb, ALU.add).then_inc(S["x1_ok"], 1)
                    v.wait_ge(S["x1_ok"], t + 1)
                    hold(v, "dve_hold")
                    k(v.bn_stats(stats[:, 0, :], rows_sb[:, t % RB, 0:D]))
                    hold(v, "dve_hold")
                    v.bn_aggr(sc[:, 0:2], stats[:, 0, :]).then_inc(S["st_ok"], 1)
                    v.wait_ge(S["sd_ok"], t + 1)
                    k(v.reciprocal(rn[:, 0:1], sc[:, 2:3]))
                    k(v.scalar_tensor_tensor(rn[:, 1:2], sc[:, 0:1], -1.0, rn[:, 0:1], ALU.mult, ALU.mult))
                    k(v.tensor_copy(rows_sb[:, t % RB, C_RSTD:C_NMR + 1], rn[:, :]))
                    v.sem_inc(S["nm_ok"], 1)
                    assert k.n == K["x1_c"]

                def route(t):
                    k = part("route_c", t)
                    v.wait_ge(S["lg_ps"], t + 1)
                    k(v.tensor_tensor(lg[:, 0, :], pS[:, 0:NX], gbs[:, :], ALU.add))
                    k(v.tensor_reduce(sc[:, 3:4], lg[:, 0, :], AX, ALU.max))
                    v.tensor_scalar(sc[:, 4:5], sc[:, 3:4], -1.0, None, ALU.mult).then_inc(S["nmx_ok"], 1)
                    k(v.scalar_tensor_tensor(lg[:, 2, :], lg[:, 0, :], sc[:, 3:4], expert_m8[:, :], ALU.is_ge, ALU.mult))
                    k(v.tensor_reduce(sc[:, 6:7], lg[:, 2, :], AX, ALU.min))
                    v.tensor_scalar(oh16[:, :], expert_m8[:, :], sc[:, 6:7], None, ALU.is_equal).then_inc(S["oh_ok"], 1)
                    assert k.n == K["route_c"]

                def place(t):
                    k = part("route2_c", t)
                    v.wait_ge(S["ex_ok"], t + 1)
                    k.mark(v.reciprocal(rows_sb[:, t % RB, C_PRB:C_PRB + 1], sc[:, 5:6]))
                    v.wait_ge(S["pos_ps"], t + 1)
                    k(v.tensor_tensor(lg[:, 3, :], pS[:, NX:2 * NX], oh16[:, :], ALU.mult))
                    k.mark(v.tensor_reduce(sc[:, 7:8], lg[:, 3, :], AX, ALU.add))
                    k.mark(v.tensor_tensor(cnt16[:, :], cnt16[:, :], oh16[:, :], ALU.add))
                    k(v.tensor_scalar(sc[:, 8:9], sc[:, 6:7], float(SLOTS), float(NX * SLOTS - 1), ALU.mult, ALU.add))
                    k.mark(v.tensor_copy(rows_sb[:, t % RB, C_TOK:C_TOK + 1].bitcast(I32), tok[:, :]))
                    k.mark(v.tensor_scalar(sc[:, 9:10], sc[:, 7:8], float(CAP), BIG, ALU.is_gt, ALU.mult))
                    k(v.tensor_tensor(sc[:, 8:9], sc[:, 8:9], sc[:, 7:8], ALU.add))
                    k(v.tensor_tensor(row_at[:, bass.ds(t % RB, 1)], sc[:, 8:9], sc[:, 9:10], ALU.add))
                    assert k.n == K["route2_c"], k.n
                    v.sem_inc(S["row_ok"], 1)
                    p = part("place_c", t)
                    p(v.tensor_scalar(tok[:, :], tok[:, :], float(P), None, ALU.add))

                def node(t, first=False, final=False):
                    late(t)
                    mean(t)
                    if not final:
                        p = part("tile_c", t)
                        p(v.tensor_scalar(tile_iota[:, :], tile_iota[:, :], float(P), None, ALU.add))
                        hold(v, "dve_hold")
                        early(t + 1)
                        queries(t + 1)
                    if not first:
                        route(t - 1)
                    residual(t)
                    if not final:
                        attend(t + 1)
                    if not first:
                        place(t - 1)

                early(0)
                queries(0)
                attend(0)
                node(0, first=True)
                with v.Fori(1, NT - 1) as t:
                    node(t)
                node(NT - 1, final=True)
                route(NT - 1)
                place(NT - 1)

            K3 = 7

            def columns(j):
                v.wait_ge(S["j_ready"], j + 1)
                v.sem_inc(S["dve_hold"], 1)
                v.tensor_scalar(xj, jrow[:, j % JB, 0:D], jrow[:, j % JB, C_RSTD:C_RSTD + 1], jrow[:, j % JB, C_NMR:C_NMR + 1],
                                ALU.mult, ALU.add).then_inc(S["xj_ok"], 1)

            def job(e, i, more=True):
                j = e * JOBS + i
                k = Chain(v, S["dve_c"], c2 + j * K3)
                v.wait_ge(S["h1_ps"], j + 1)
                for q in range(FC // 2, FC):
                    ins = v.tensor_scalar(hs[:, q, :], pH1[:, (q - FC // 2) * P:(q - FC // 2 + 1) * P],
                                          b1s[:, bass.ds(e * FC + q, 1)], 0.0, ALU.add, ALU.max)
                ins.then_inc(S["h1_sb"], 1)
                if more:
                    v.wait_ge(S["xjt_ps"], j + 2)
                    v.sem_inc(S["dve_hold"], 1)
                    columns(j + 2)
                v.wait_ge(S["y_ps"], j + 1)
                v.tensor_tensor(y[:, 0, :], pY[:, 0:D], b2s[:, bass.ds(e, 1), :].rearrange("p a d -> p (a d)"), ALU.add).then_inc(S["y_used"], 1)
                v.wait_ge(S["y_used"], j + 2)
                hold(v, "dve_hold")
                k(v.tensor_scalar(y[:, 1, :], y[:, 0, :], jrow[:, j % JB, C_PRB:C_PRB + 1], None, ALU.mult))
                k.mark(v.tensor_scalar(y[:, 2, :].bitcast(I32), y[:, 1, :], 0.0, 0.0, ALU.mult, ALU.is_equal))
                v.wait_ge(S["fin_free"], j + 1)
                v.sem_inc(S["dve_hold"], 1)
                k.mark(v.tensor_scalar(fin[:, j % 2, :], y[:, 1, :], 1.0e4, -1.0e4, ALU.min, ALU.max))
                k(v.tensor_tensor(y[:, 0, :], y[:, 1, :], y[:, 1, :], ALU.is_equal))
                k(v.tensor_tensor(y[:, 0, :], fin[:, j % 2, :], y[:, 0, :], ALU.mult))
                hold(v, "dve_hold")
                k(v.copy_predicated(y[:, 0, :], y[:, 2, :].bitcast(I32), y[:, 1, :]))
                v.tensor_copy(jtok[:, bass.ds(j % 2, 1)], jrow[:, j % JB, C_TOK:C_TOK + 1].bitcast(I32))
                k(v.tensor_tensor(fin[:, j % 2, :], y[:, 0, :], jrow[:, j % JB, 0:D], ALU.add))
                assert k.n == K3, k.n
                v.sem_inc(S["fin_ok"], 1)
                v.sem_inc(S["j_free"], 1)

            v.sem_inc(S["y_used"], 1)
            columns(0)
            v.wait_ge(S["xjt_ps"], 1)
            columns(1)
            with v.Fori(0, NX - 1) as e:
                with v.Fori(0, JOBS) as i:
                    job(e, i)
            with v.Fori(0, JOBS - 2) as i:
                job(NX - 1, i)
            for i in range(JOBS - 2, JOBS):
                job(NX - 1, i, False)


_INS = ["x", "src", "dst", "L0_gnn_W", "L0_gnn_b", "L0_mix_wq", "L0_mix_bq", "L0_mix_wk", "L0_mix_bk", "L0_mix_wv", "L0_mix_bv",
        "L0_mix_wo", "L0_mix_bo", "L0_ffn_gate_w", "L0_ffn_gate_b", "L0_ffn_w1", "L0_ffn_b1", "L0_ffn_w2", "L0_ffn_b2"]
_OUTS = [((N, D), "float32")]


def kernel(**inputs):
    import numpy as _np
    import concourse.bacc as _bacc
    from concourse import mybir as _mybir
    from concourse.bass_utils import run_bass_kernel_spmd as _run

    nc = _bacc.Bacc("TRN2", target_bir_lowering=False, num_devices=1)
    arrays, args = {}, []
    for name in _INS:
        a = _np.ascontiguousarray(inputs[name])
        arrays[f"in_{name}_dram"] = a
        args.append(nc.dram_tensor(f"in_{name}_dram", a.shape, _mybir.dt.from_np(a.dtype), kind="ExternalInput").ap())
    for i, (shape, dtype) in enumerate(_OUTS):
        dt = _mybir.dt.from_np(_np.dtype(dtype))
        args.append(nc.dram_tensor(f"out_{i}_dram", shape, dt, kind="ExternalOutput").ap())
    gps_block(nc, *args)
    r = _run(nc, [arrays], core_ids=[0])
    got = tuple(r.results[0][f"out_{i}_dram"] for i in range(len(_OUTS)))
    return got[0]
```

```python
from contextlib import ExitStack

import concourse.bass as bass
from concourse import mybir

F32 = mybir.dt.float32
F16 = mybir.dt.float16
I32 = mybir.dt.int32
ALU = mybir.AluOpType
ACT = mybir.ActivationFunctionType
AX = mybir.AxisListType.X

P = 128
D = 256
DK = D // P
HEADS = 8
HD = D // HEADS
HB = P // HD
N = 6250
NT = -(-N // P)
LAST = N - (NT - 1) * P
E = 100000
EC = -(-E // P)
G = 4
RQ = 4
RING = RQ * G
EB = -(-EC // RING)
EQ = EB * RQ
PACK = 256
ECP = EB * RING
EBLK = -(-ECP // P)
OQ = 4
EARLY = 4
NB = 4
NX = 8
F = 1024
FC = F // P
CAP = 977
SLOTS = 1024
JOBS = SLOTS // P
LO = 2048.0
ROW = D + 4
C_RSTD, C_NMR, C_PRB, C_TOK = D, D + 1, D + 2, D + 3
RB = 4
AFTER = 2
JB = 4
BIG = 1.0e6
EPS = 1e-5
PAD_DST = 100000.0


def gps_block(nc, x, src, dst, gnn_w, gnn_b, wq, bq, wk, bk, wv, bv, wo, bo,
              gate_w, gate_b, w1, b1, w2, b2, out):
    table = nc.dram_tensor("table", [NT * P, 2 * D], F16).ap()
    normed_t = nc.dram_tensor("normed_t", [NT, P, DK * P], F32).ap()
    rows = nc.dram_tensor("rows", [NX * SLOTS, ROW], F32).ap()
    rows_t = rows.rearrange("(s p) d -> s p d", p=P)
    x_t = x[0:(NT - 1) * P, :].rearrange("(t p) d -> t p d", p=P)
    out_t = out[0:(NT - 1) * P, :].rearrange("(t p) d -> t p d", p=P)

    with ExitStack() as ctx:
        def sb(name, shape, dt=F32):
            return ctx.enter_context(nc.sbuf_tensor(name, shape, dt))

        def bank(name):
            return ctx.enter_context(nc.psum_tensor(name, [P, 512], F32))

        def sem(name):
            return ctx.enter_context(nc.semaphore(name))

        w1s = sb("w1s", [P, NX, DK, F])
        w2s = sb("w2s", [P, NX, FC, D])
        b1s = sb("b1s", [P, NX * FC])
        b2s = sb("b2s", [P, NX, D])
        wkv = sb("wkv", [P, DK, 2 * D])
        wqs = sb("wqs", [P, DK, D])
        wos = sb("wos", [P, DK, D])
        wgs = sb("wgs", [P, DK, D])
        gws = sb("gws", [P, DK, NX])
        hs = sb("hs", [P, FC, P])
        bks = hs[:, 0:2, :].rearrange("p a b -> p (a b)")
        bvs = hs[:, 2:4, :].rearrange("p a b -> p (a b)")
        bos = sb("bos", [P, D])
        bgs = sb("bgs", [P, D])
        bqs = sb("bqs", [P, DK])
        gbs = sb("gbs", [P, NX])
        ident = sb("ident", [P, P])
        tri = sb("tri", [P, P])
        c16 = sb("c16", [P, 4, P], F16)
        zero16, ones16, tri16 = c16[:, 0, :], c16[:, 1, :], c16[:, 2, :]
        any16 = c16[:, :, :].rearrange("p a b -> p (a b)")
        iota_row = sb("iota_row", [P, P])
        iota_i = sb("iota_i", [P, P], I32)
        expert_m8 = sb("expert_m8", [P, NX])
        eps = sb("eps", [P, 1])

        src_t = sb("src_t", [P, ECP], I32)
        dst_t = sb("dst_t", [P, ECP])
        cmin = sb("cmin", [P, EBLK])
        cmax = sb("cmax", [P, EBLK])
        chunk_id = sb("chunk_id", [P, EBLK])
        chunk_i = sb("chunk_i", [P, EBLK], I32)
        bounds = sb("bounds", [P, 2, NT])
        lohi = sb("lohi", [NT, 2])
        lh_row = sb("lh_row", [1, 2, 64])
        new_row = sb("new_row", [1, 64])
        new_col = sb("new_col", [NT, 1])
        base_row = sb("base_row", [1, 64])
        spans = sb("spans", [1, 2, 64], I32)
        words = spans[0:1, 0, :]
        ends = sb("ends", [1, 3, NT], I32)
        rounds = spans[0:1, 1, 0:1]
        plan = spans[0:1, 1, NX:2 * NX]
        total = spans[0:1, 1, 2 * NX:2 * NX + 1]
        counts = spans[0:1, 1, 3 * NX:4 * NX]
        idx = sb("idx", [P, RING], I32)
        gathered = sb("gathered", [P, RING, 2 * D], F16)
        onehot = sb("onehot", [P, OQ, G, P], F16)
        tile_iota = sb("tile_iota", [P, P])

        ring32 = gathered[:, :, :].rearrange("p a b -> p (a b)").bitcast(F32)
        xin = ring32[:, 0:2 * NB * D].rearrange("p (a b c) -> p a b c", a=2, b=NB)
        stats = sb("stats", [P, NB, 6])
        mv = sb("mv", [P, NB, 2])
        std = sb("std", [P, NB])
        mean2 = sb("mean2", [P, 2 * NB])
        rstd2 = sb("rstd2", [P, 2 * NB])
        xn = sb("xn", [P, NB, D])
        trow = ring32[:, 2 * NB * D:3 * NB * D].bitcast(F16).rearrange("p (b d) -> p b d", b=NB)
        pTS, pQY = (lambda b: (pT, pS)[b]), (lambda b: (pQ, pY)[b])
        xt = ring32[:, 3 * NB * D:4 * NB * D].rearrange("p (b d) -> p b d", b=NB)
        dif = sb("dif", [P, NB, D])
        kvw = sb("kvw", [P, 4, D])
        kb, kr = kvw[:, 0:2, :], kvw[:, 2:4, :]
        kk = sb("kk", [P, D])
        vv = sb("vv", [P, 2, DK, P + 1])
        kvm = sb("kvm", [P, DK, P + HB])

        xtin = dif[:, 0:2, :]
        xres = dif[:, 2:4, :]
        qr, qe, qt, ahi = xn[:, 0, :], xn[:, 1, :], xn[:, 2, :], xn[:, 3, :]
        rden = sb("rden", [P, HEADS])
        o_sb, ot = kvw[:, 0, :], kvw[:, 1, :]
        rdeg = sb("rdeg", [P, 2])
        deg = sb("deg", [P, 3])
        agg, agt = kvw[:, 2, :], kvw[:, 3, :]
        xb = kk[:, :]
        gb = wkv[:, 1, 0:D]
        rows_sb = sb("rows_sb", [P, RB, ROW])
        row_at = sb("row_at", [P, RB], I32)
        x2 = wkv[:, 0, 0:D]
        x2t = wkv[:, 0, D:2 * D]
        lg = sb("lg", [P, 6, NX])
        sc = sb("sc", [P, 12])
        oh16 = sb("oh16", [P, NX], F16)
        cnt16 = sb("cnt16", [P, NX], F16)
        spare = sb("spare", [P, 1])
        rn = sb("rn", [P, 2])
        tok = sb("tok", [P, 1])

        jrow = ring32[:, 0:JB * ROW].rearrange("p (a d) -> p a d", a=JB)
        y = ring32[:, JB * ROW:JB * ROW + 3 * D].rearrange("p (a d) -> p a d", a=3)
        empty = rows_sb[:, 0, :]
        xj, xjt = xn[:, 0, :], xn[:, 1, :]
        fin = wkv[:, 1, :].rearrange("p (a d) -> p a d", a=2)
        jtok = sb("jtok", [P, 2], I32)

        pA = bank("pA")
        pD = bank("pD")
        pT = bank("pT")
        pQ = bank("pQ")
        pH0 = bank("pH0")
        pH1 = bank("pH1")
        pY = bank("pY")
        pS = bank("pS")

        names = """w_qkv w_big consts iota_ok ident_ok e_src e_dst e_padded e_f32 e_ps e_copied e_bound e_bt e_lohi
          e_rowps e_row e_newps e_new e_baseps spans_ok idx_ok row_stored row_free fin_free x_in ln_stats ln_std
          ln_xn ln_hi ln_dif ln_lo xt_ps xt_sb kv_ps kb_ok v_ok ke_ok kk_ok kv_used kvm_ok rows_z slots relayed
          oh_slots oh_ready agg_done xt_in xr_in xb_ok q_ps qe_ok qt_ok att_ps o_ok ot_ps ot_sb dg_ok ahi_ok
          gb_ok agg_ok agt_ps agt_sb x1_ps x1_ok st_ok sd_ok nm_ok x2_ok x2t_ps x2t_sb lg_ps nmx_ok ex_ok oh_ok
          pos_ps row_ok row_st scat_done tile_c y_used j_in j_free plan_ps plan_ok xj_ok xjt_ps xjt_sb h0_ps
          h1_ps h0_sb h1_sb y_ps fin_ok fin_sc dve_c agg_c att_c x1_c norm_c route_c route2_c sp_hold act_hold
          dve_hold pool_hold pe_hold""".split()
        S = {n: sem(n) for n in names}
        landed = [sem(f"landed{j}") for j in range(RING)]
        xt_st = [sem(f"xt_st{b}") for b in range(NB)]
        tab_st = [sem(f"tab_st{b}") for b in range(NB)]
        block = ctx.enter_context(nc.Block())

        class Chain:
            def __init__(self, eng, s, at=0):
                self.eng, self.s, self.n, self.at = eng, s, 0, at

            def __call__(self, ins):
                ins.then_inc(self.s, 1)
                self.n += 1
                self.eng.wait_ge(self.s, self.at + self.n)

            def mark(self, ins):
                ins.then_inc(self.s, 1)
                self.n += 1

            def wait(self):
                self.eng.wait_ge(self.s, self.at + self.n)

        def expert_jobs(eng, e):
            w = eng.value_load(plan[0:1, bass.ds(e, 1)], min_val=1, max_val=NX * JOBS * PACK)
            return eng.snap(w // PACK), eng.snap(w % PACK)

        def hold(eng, name):
            eng.sem_inc(S[name], 1)

        def xin_f(a):
            g = ring32[:, 2 * NB * D:4 * NB * D]
            return g[:, a * EBLK * P:(a + 1) * EBLK * P].rearrange("p (b e) -> p b e", e=P)

        @block.sync
        def _(sp):
            full = (E // P // P) * P * P
            mid = E // P * P
            sp.wait_ge(S["e_padded"], 2)
            for a, name in ((0, "e_dst"), (1, "e_src")):
                v = dst if a == 0 else src
                t = xin[:, :, :, :].rearrange("p a b c -> p (a b c)").bitcast(I32)[:, a * 1024:a * 1024 + EBLK * P]
                t = t.rearrange("p (b e) -> p b e", e=P)
                sp.dma_start(t[:, 0:full // P // P, :], v[0:full].rearrange("(b r e) -> r b e", r=P, e=P)).then_inc(S[name], 16)
                sp.dma_start(t[0:(mid - full) // P, EBLK - 1, :], v[full:mid].rearrange("(r e) -> r e", e=P)).then_inc(S[name], 16)
                sp.dma_start(t[(mid - full) // P:(mid - full) // P + 1, EBLK - 1, 0:E - mid],
                             v[mid:E].rearrange("(a e) -> a e", a=1)).then_inc(S[name], 16)
            sp.dma_start(wkv[:, :, 0:D], wk.rearrange("(k p) n -> p k n", p=P)).then_inc(S["w_qkv"], 16)
            sp.dma_start(wkv[:, :, D:2 * D], wv.rearrange("(k p) n -> p k n", p=P)).then_inc(S["w_qkv"], 16)
            for t, v in ((wqs, wq), (wos, wo), (wgs, gnn_w)):
                sp.dma_start(t[:, :, :], v.rearrange("(k p) n -> p k n", p=P)).then_inc(S["w_qkv"], 16)
            sp.dma_start(gws[:, :, :], gate_w.rearrange("(k p) n -> p k n", p=P)).then_inc(S["w_qkv"], 16)
            for t, v in ((bks, bk), (bvs, bv), (bos, bo), (bgs, gnn_b), (gbs, gate_b)):
                sp.dma_start(t[:, :], v.partition_broadcast(P)).then_inc(S["w_qkv"], 16)
            with nc.allow_non_contiguous_dma(reason="per-partition bias columns"):
                sp.dma_start(bqs[:, :], bq.rearrange("(k p) -> p k", p=P)).then_inc(S["w_qkv"], 16)

            def load(i, nb, rows_n):
                t0 = i * NB
                if nb == NB:
                    sp.dma_start(xin[:, i % 2, :, :], x_t[bass.ds(t0, NB), :, :].rearrange("t p d -> p t d")).then_inc(S["x_in"], 16)
                else:
                    sp.dma_start(xin[0:rows_n, i % 2, 0, :], x[(NT - 1) * P:N, :]).then_inc(S["x_in"], 16)

            tab_v = table.rearrange("(t p) d -> t p d", p=P)
            nbat = NT // NB
            sp.wait_ge(S["e_copied"], 2)
            load(0, NB, P)
            sp.wait_ge(S["x_in"], 16)
            load(1, NB, P)
            sp.wait_ge(S["x_in"], 32)

            def store_t(i, j):
                t = i * NB + j
                sp.wait_ge(S["xt_sb"], t + 1)
                hold(sp, "sp_hold")
                sp.dma_start(normed_t[bass.ds(t, 1), :, :].rearrange("t p n -> p (t n)"), xt[:, j, :]).then_inc(xt_st[j], 16)

            def store_tab(i, j):
                t = i * NB + j
                sp.wait_ge(S["ln_lo"], t + 1)
                hold(sp, "sp_hold")
                sp.dma_start(tab_v[bass.ds(t, 1), :, :].rearrange("t p d -> p (t d)"), trow[:, j, :]).then_inc(tab_st[j], 16)

            def batch(i, nb, ahead):
                for j in range(NB):
                    if j == NB - 1 and ahead:
                        sp.wait_ge(S["ln_xn"], i * NB + 2 * NB)
                        hold(sp, "sp_hold")
                        sp.wait_ge(S["x_in"], i * 16 + 48)
                        hold(sp, "sp_hold")
                        load(i + 3, ahead, LAST)
                    if j < NB - 1:
                        store_t(i, j + 1)
                    else:
                        store_t(i + 1, 0)
                    if j == 0:
                        store_tab(i, NB - 1)
                    elif j <= nb:
                        store_tab(i + 1, j - 1)

            store_t(0, 0)
            sp.wait_ge(S["ln_xn"], NB)
            load(2, NB, P)
            for j in range(NB - 1):
                store_tab(0, j)
            with sp.Fori(0, nbat - 3) as i:
                batch(i, NB, NB)
            batch(nbat - 3, NB, 1)
            batch(nbat - 2, NB, 0)
            batch(nbat - 1, 1, 0)
            for b in range(NB):
                sp.wait_ge(xt_st[b], 16 * len(range(b, NT, NB)))

            sp.wait_ge(S["kk_ok"], NT)
            for t in range(2):
                sp.dma_start(xtin[:, t, :], normed_t[t, :, :]).then_inc(S["xt_in"], 16)
                sp.wait_ge(S["xt_in"], 16 * (t + 1))
            sp.dma_start(xres[:, 0, :], x_t[0, :, :]).then_inc(S["xr_in"], 16)
            sp.wait_ge(S["xr_in"], 16)

            def node_io(t, ahead):
                if ahead >= 1:
                    sp.wait_ge(S["q_ps"], t + 1)
                    hold(sp, "sp_hold")
                    sp.dma_start(xtin[:, t % 2, :], normed_t[bass.ds(t + 2, 1), :, :].rearrange("t p n -> p (t n)")).then_inc(S["xt_in"], 16)
                    hold(sp, "sp_hold")
                sp.wait_ge(S["xb_ok"], t + 1)
                hold(sp, "sp_hold")
                if ahead >= 1:
                    sp.dma_start(xres[:, (t + 1) % 2, :], x_t[bass.ds(t + 1, 1), :, :].rearrange("t p d -> p (t d)")).then_inc(S["xr_in"], 16)
                else:
                    sp.dma_start(xres[0:LAST, (t + 1) % 2, :], x[(NT - 1) * P:N, :]).then_inc(S["xr_in"], 16)
                sp.wait_ge(S["x1_ok"], t + 1)
                hold(sp, "sp_hold")
                sp.dma_start(out_t[bass.ds(t, 1), :, :].rearrange("t p d -> p (t d)"), rows_sb[:, t % RB, 0:D]).then_inc(S["row_st"], 16)
                sp.wait_ge(S["row_st"], t * 16 + 16)
                sp.sem_inc(S["row_stored"], 1)
                if ahead >= 1:
                    sp.wait_ge(S["xt_in"], t * 16 + 48)
                    hold(sp, "sp_hold")
                sp.wait_ge(S["xr_in"], t * 16 + 32)
                hold(sp, "sp_hold")

            with sp.Fori(0, NT - 2) as t:
                node_io(t, 2)
            node_io(NT - 2, 0)
            sp.wait_ge(S["x1_ok"], NT)
            sp.dma_start(out[(NT - 1) * P:N, :], rows_sb[0:LAST, (NT - 1) % RB, 0:D]).then_inc(S["row_st"], 16)
            sp.wait_ge(S["row_st"], 16 * NT)

            sp.wait_ge(S["plan_ok"], 1)
            sp.wait_ge(S["scat_done"], 16 * (NT + NX))

            def load_rows(j, tile):
                sp.wait_ge(S["j_free"], j + 1)
                hold(sp, "sp_hold")
                sp.dma_start(jrow[:, bass.ds(j % JB, 1), :].rearrange("p a d -> p (a d)"),
                             rows_t[bass.ds(tile, 1), :, :].rearrange("t p d -> p (t d)")).then_inc(S["j_in"], 16)
                sp.wait_ge(S["j_in"], j * 16 + 16)
                hold(sp, "sp_hold")

            with sp.Fori(0, NX) as e:
                base, n = expert_jobs(sp, e)
                with sp.Fori(0, n) as i:
                    load_rows(base + i, e * JOBS + i % JOBS)
                hold(sp, "sp_hold")
            jobs = sp.value_load(total, min_val=NX, max_val=NX * JOBS)
            for b in range(2):
                load_rows(jobs + b, 0)
            sp.wait_ge(S["fin_sc"], jobs * 16)
            hold(sp, "sp_hold")

        @block.gpsimd
        def _(g):
            edges = xin[:, :, :, :].rearrange("p a b c -> p (a b c)").bitcast(I32)
            g.memset(edges[:, 0:1024], int(PAD_DST)).then_inc(S["e_padded"], 1)
            g.memset(edges[:, 1024:2048], 0).then_inc(S["e_padded"], 1)
            g.iota(iota_i[:, :], [[1, P]], base=0, channel_multiplier=0).then_inc(S["iota_ok"], 1)
            g.iota(chunk_i[:, :], [[P, EBLK]], base=0, channel_multiplier=1).then_inc(S["iota_ok"], 1)
            g.memset(ident[:, :], 0.0).then_inc(S["consts"], 1)
            g.memset(tri[:, :], 1.0).then_inc(S["consts"], 1)
            g.memset(c16[:, 1:4, :], 1.0).then_inc(S["consts"], 1)
            g.memset(zero16, 0.0).then_inc(S["consts"], 1)
            g.memset(empty[:, 0:C_TOK], 0.0).then_inc(S["rows_z"], 1)
            g.memset(empty[:, C_TOK:ROW].bitcast(I32), N).then_inc(S["rows_z"], 1)
            g.memset(eps[:, :], EPS).then_inc(S["consts"], 1)
            g.memset(vv[:, :, :, :], 1.0).then_inc(S["consts"], 1)
            g.wait_ge(S["consts"], 6)
            g.affine_select(out=ident[:, :], in_=ident[:, :], compare_op=ALU.not_equal, fill=1.0, base=0,
                            pattern=[[-1, P]], channel_multiplier=1).then_inc(S["ident_ok"], 1)
            g.affine_select(out=tri[:, :], in_=tri[:, :], compare_op=ALU.is_ge, fill=0.0, base=0,
                            pattern=[[1, P]], channel_multiplier=-1).then_inc(S["ident_ok"], 1)

            def remainder(t, j):
                g.wait_ge(S["ln_hi"], t + 1)
                g.tensor_tensor(dif[:, j, :], xn[:, j, :], trow[:, j, 0:D], ALU.subtract).then_inc(S["ln_dif"], 1)

            g.wait_ge(S["rows_z"], 2)
            with g.Fori(0, NX) as i:
                for j in range(NB):
                    remainder(i * NB + j, j)
                g.dma_start(rows_t[bass.ds(i * JOBS, JOBS), :, :].rearrange("s p d -> p s d"),
                            empty.rearrange("p (a d) -> p a d", a=1).broadcast_to([P, JOBS, ROW])).then_inc(S["scat_done"], 16)
            with g.Fori(NX, NT // NB) as i:
                for j in range(NB):
                    remainder(i * NB + j, j)
            remainder(NT - 1, 0)

            def scatter(t):
                g.wait_ge(S["scat_done"], t * 16 + 16 * NX)
                g.sem_inc(S["row_free"], 1)
                g.wait_ge(S["row_ok"], t + 1)
                hold(g, "pool_hold")

                def send(b):
                    g.indirect_dma_start(rows[:, :], bass.IndirectOffsetOnAxis(ap=row_at[:, b:b + 1], axis=0), rows_sb[:, b, :], None,
                                         bounds_check=NX * SLOTS - 1, oob_is_err=False).then_inc(S["scat_done"], 16)
                with g.If(t % RB < RB // 2):
                    with g.If(t % RB < 1):
                        send(0)
                    with g.Else():
                        send(1)
                    g.sem_inc(S["pool_hold"], 1)
                with g.Else():
                    with g.If(t % RB < RB - 1):
                        send(2)
                    with g.Else():
                        send(3)
                    g.sem_inc(S["pool_hold"], 1)
                g.sem_inc(S["pool_hold"], 1)

            for b in range(NB):
                g.wait_ge(tab_st[b], 16 * len(range(b, NT, NB)))
                g.wait_ge(xt_st[b], 16 * len(range(b, NT, NB)))
            g.wait_ge(S["scat_done"], 16 * NX)
            g.wait_ge(S["spans_ok"], 1)
            turns = g.value_load(rounds, min_val=EB, max_val=EB * NT)

            def load_end(reg, t):
                g.load(reg, words[0:1, bass.ds(t, 1)])
                w = g.snap(reg)
                g.reg_mov(reg, w // PACK + w % PACK)
                g.reg_add(reg, reg, -1)

            def events(tile, tend, f):
                with g.While(lambda: g.snap(tend) < f - (RQ - 1)):
                    scatter(g.snap(tile))
                    g.reg_add(tile, tile, 1)
                    load_end(tend, g.snap(tile) + AFTER)
                g.sem_inc(S["pool_hold"], 1)

            def report(s, count):
                for j in range(s * G, (s + 1) * G):
                    g.wait_ge(landed[j], count)
                g.sem_inc(S["relayed"], 1)

            def gather(i, s, tile=None, tend=None):
                first = isinstance(i, int) and i == 0
                f = i * RQ + s
                if s % 2 == 0:
                    g.tensor_copy(idx[:, s * G:(s + 2) * G], src_t[:, bass.ds((i % EB) * RING + s * G, 2 * G)]).then_inc(S["idx_ok"], 1)
                    g.wait_ge(S["idx_ok"], i * 2 + s // 2 + 1)
                    hold(g, "pool_hold")
                if not first:
                    events(tile, tend, f)
                g.wait_ge(S["slots"], f + 1)
                hold(g, "pool_hold")
                for j in range(s * G, (s + 1) * G):
                    g.indirect_dma_start(gathered[:, j, :], None, table[:, :],
                                         bass.IndirectOffsetOnAxis(ap=idx[:, j:j + 1], axis=0)).then_inc(landed[j], 16)
                if not (first and s == 0):
                    report((s - 1) % RQ, (i + 1) * 16 if s > 0 else i * 16)

            for s in range(RQ):
                gather(0, s)
            with g.register("tile_no") as tile, g.register("tile_end") as tend:
                g.reg_mov(tile, 0)
                load_end(tend, AFTER)
                with g.Fori(1, turns) as i:
                    for s in range(RQ):
                        gather(i, s, tile, tend)
                report(RQ - 1, turns * 16)
                with g.Fori(g.snap(tile), NT) as t:
                    scatter(t)

            g.wait_ge(S["plan_ok"], 1)
            jobs = g.value_load(total, min_val=NX, max_val=NX * JOBS)
            with g.Fori(0, jobs) as j:
                g.wait_ge(S["fin_ok"], j + 1)
                hold(g, "pool_hold")

                def finish(b):
                    g.indirect_dma_start(out[:, :], bass.IndirectOffsetOnAxis(ap=jtok[:, b:b + 1], axis=0),
                                         fin[:, b, :], None,
                                         bounds_check=N - 1, oob_is_err=False).then_inc(S["fin_sc"], 16)
                with g.If(j % 2 < 1):
                    finish(0)
                with g.Else():
                    finish(1)
                g.wait_ge(S["fin_sc"], j * 16 + 16)
                g.sem_inc(S["fin_free"], 1)

        @block.scalar
        def _(a):
            def load_expert(e):
                a.dma_start(w1s[:, bass.ds(e, 1), :, :].rearrange("p a k f -> p (a k) f"),
                            w1[bass.ds(e, 1), :, :].rearrange("a (k p) f -> p (a k) f", p=P)).then_inc(S["w_big"], 16)
                a.dma_start(w2s[:, bass.ds(e, 1), :, :].rearrange("p a c d -> p (a c) d"),
                            w2[bass.ds(e, 1), :, :].rearrange("a (c p) d -> p (a c) d", p=P)).then_inc(S["w_big"], 16)

            with nc.allow_non_contiguous_dma(reason="hidden bias to columns"):
                a.dma_start(b1s[:, :], b1.rearrange("e (c p) -> p (e c)", p=P)).then_inc(S["w_big"], 16)
            a.dma_start(b2s[:, :, :].rearrange("p e d -> p (e d)"), b2.rearrange("e d -> (e d)").partition_broadcast(P)).then_inc(S["w_big"], 16)

            a.wait_ge(S["consts"], 6)

            def std_(i, nb):
                a.wait_ge(S["ln_stats"], i + 1)
                a.activation(std[:, 0:nb], mv[:, 0:nb, 1], ACT.Sqrt, bias=eps[:, 0:1]).then_inc(S["ln_std"], 1)

            def high(i, j, fresh=False):
                a.wait_ge(S["ln_xn"], i * NB + j + 1)
                if not fresh:
                    a.sem_inc(S["act_hold"], 1)
                    a.wait_ge(tab_st[j], i * 16)
                a.activation(trow[:, j, 0:D], xn[:, j, :], ACT.Copy).then_inc(S["ln_hi"], 1)

            def low(i, j):
                a.wait_ge(S["ln_dif"], i * NB + j + 1)
                a.activation(trow[:, j, D:2 * D], dif[:, j, :], ACT.Copy, scale=LO).then_inc(S["ln_lo"], 1)

            def features(t, b):
                a.wait_ge(S["kv_used"], t + 1)
                a.sem_inc(S["act_hold"], 1)
                a.wait_ge(S["kb_ok"], t + 1)
                a.activation(vv[:, b, :, 0:P], pQY(b)[:, D:2 * D].rearrange("p (k n) -> p k n", k=DK), ACT.Copy).then_inc(S["v_ok"], 1)
                a.activation(kr[:, b, :], kb[:, b, :], ACT.Relu)
                a.activation(kb[:, b, :], kb[:, b, :], ACT.Exp).then_inc(S["ke_ok"], 1)

            def batch(i, nb, nb2):
                for j in range(NB):
                    if j == NB - 1 and nb2:
                        std_(i + 2, nb2)
                    features(i * NB + j, j % 2)
                    if j == 0:
                        low(i, NB - 1)
                    elif j <= nb:
                        low(i + 1, j - 1)
                    if j < nb:
                        high(i + 1, j)

            std_(0, NB)
            for j in range(NB):
                if j == NB - 1:
                    std_(1, NB)
                high(0, j, True)
                if j > 0:
                    low(0, j - 1)
            skip = NT // NB - 2 - NX
            with a.Fori(0, skip) as i:
                batch(i, NB, NB)
            with a.Fori(skip, skip + NX) as i:
                batch(i, NB, NB)
                load_expert(i - skip)
            batch(NT // NB - 2, NB, 1)
            batch(NT // NB - 1, 1, 0)
            features(NT - 1, 0)

            def query(t):
                a.wait_ge(S["q_ps"], t + 1)
                for out_, f in ((qr, ACT.Relu), (qe, ACT.Exp)):
                    for k in range(DK):
                        ins = a.activation(out_[:, k * P:(k + 1) * P], pQ[:, k * P:(k + 1) * P], f, bias=bqs[:, k:k + 1])
                ins.then_inc(S["qe_ok"], 1)

            def gate_in(t):
                a.wait_ge(S["x2t_ps"], t + 1)
                a.activation(x2t, pH0[:, 0:D], ACT.Copy).then_inc(S["x2t_sb"], 1)

            def softmax(t):
                a.wait_ge(S["nmx_ok"], t + 1)
                a.activation(lg[:, 1, :], lg[:, 0, :], ACT.Exp, bias=sc[:, 4:5], accum_out=sc[:, 5:6]).then_inc(S["ex_ok"], 1)

            def node(t, first=False, final=False):
                a.wait_ge(S["dg_ok"], t + 1)
                a.activation(ahi, pA[:, 0:D], ACT.Copy, scale=rdeg[:, 0:1]).then_inc(S["ahi_ok"], 1)
                a.activation(gb, bgs[:, :], ACT.Copy, scale=deg[:, 2:3]).then_inc(S["gb_ok"], 1)
                a.wait_ge(S["ot_ps"], t + 1)
                a.activation(ot, pH1[:, 0:D], ACT.Copy).then_inc(S["ot_sb"], 1)
                if not first:
                    gate_in(t - 1)
                if not final:
                    query(t + 1)
                a.wait_ge(S["agt_ps"], t + 1)
                a.activation(agt, pT[:, 0:D], ACT.Copy).then_inc(S["agt_sb"], 1)
                if not first:
                    softmax(t - 1)
                a.wait_ge(S["st_ok"], t + 1)
                a.activation(sc[:, 2:3], sc[:, 1:2], ACT.Sqrt, bias=eps[:, 0:1]).then_inc(S["sd_ok"], 1)
                a.wait_ge(S["nm_ok"], t + 1)
                a.sem_inc(S["act_hold"], 1)
                a.activation(x2, rows_sb[:, t % RB, 0:D], ACT.Identity, scale=rn[:, 0:1], bias=rn[:, 1:2]).then_inc(S["x2_ok"], 1)
                a.activation(spare[:, :], eps[:, 0:1], ACT.Exp)

            query(0)
            node(0, first=True)
            with a.Fori(1, NT - 1) as t:
                node(t)
            node(NT - 1, final=True)
            gate_in(NT - 1)
            softmax(NT - 1)

            def columns(j):
                a.wait_ge(S["xjt_ps"], j + 1)
                a.activation(xjt, pT[:, 0:D], ACT.Copy).then_inc(S["xjt_sb"], 1)
            columns(0)

            def job(e, j):
                a.wait_ge(S["h0_ps"], j + 1)
                for c in range(FC // 2):
                    ins = a.activation(hs[:, c, :], pH0[:, c * P:(c + 1) * P], ACT.Relu, bias=b1s[:, bass.ds(e * FC + c, 1)])
                ins.then_inc(S["h0_sb"], 1)
                columns(j + 1)
            a.wait_ge(S["plan_ok"], 1)
            with a.Fori(0, NX) as e:
                base, n = expert_jobs(a, e)
                with a.Fori(0, n) as i:
                    job(e, base + i)
                a.sem_inc(S["act_hold"], 1)

        @block.tensor
        def _(pe):
            pe.wait_ge(S["ident_ok"], 2)
            for a, (b0, b1_) in enumerate(((pT, pQ), (pS, pY))):
                pe.wait_ge(S["e_f32"], a + 1)
                for b in range(EBLK):
                    o = (b0, b1_)[b // 4][:, (b % 4) * P:(b % 4 + 1) * P]
                    ins = pe.transpose(o, xin_f(a)[:, b, :], ident[:, :])
                ins.then_inc(S["e_ps"], 1)
            pe.wait_ge(S["e_copied"], 2)
            pe.wait_ge(S["e_bound"], 1)
            for a in range(2):
                ins = pe.transpose(pS[0:NT, a * P:(a + 1) * P], bounds[:, a, :], ident[:, :])
            ins.then_inc(S["e_bt"], 1)
            pe.wait_ge(S["e_lohi"], 1)
            for a in range(2):
                ins = pe.matmul(pT[0:1, a * 64:a * 64 + NT], lohi[:, a:a + 1], ident[0:NT, 0:NT], start=True, stop=True)
            ins.then_inc(S["e_rowps"], 1)
            pe.wait_ge(S["e_row"], 1)
            pe.matmul(pS[0:NT, 0:1], new_row[0:1, 0:NT], ident[0:1, 0:1], start=True, stop=True).then_inc(S["e_newps"], 1)
            pe.wait_ge(S["e_new"], 1)
            pe.matmul(pT[0:1, 0:NT], new_col[:, :], tri[0:NT, 0:NT], start=True, stop=True).then_inc(S["e_baseps"], 1)

            kvp = (pH0, pH1)
            for k in range(DK):
                pe.matmul(kvp[k][:, 0:P + 1], zero16, any16[:, 0:P + 1], start=True, stop=False)
            pe.wait_ge(S["w_qkv"], 16 * 12)
            pe.wait_ge(S["spans_ok"], 1)

            def turn(t, j):
                pe.wait_ge(S["ln_xn"], t + 1)
                pe.sem_inc(S["pe_hold"], 1)
                for k in range(DK):
                    ins = pe.transpose(pTS(j % 2)[:, k * P:(k + 1) * P], xn[:, j, k * P:(k + 1) * P], ident[:, :])
                ins.then_inc(S["xt_ps"], 1)

            def project(t, j):
                pe.wait_ge(S["xt_sb"], t + 1)
                for k in range(DK):
                    ins = pe.matmul(pQY(j % 2)[:, :], xt[:, j, k * P:(k + 1) * P], wkv[:, k, :], start=(k == 0), stop=(k == DK - 1))
                ins.then_inc(S["kv_ps"], 1)

            def sum_kv(t, b, rows_n=P, last=False):
                pe.wait_ge(S["kk_ok"], t + 1)
                pe.sem_inc(S["pe_hold"], 1)
                pe.wait_ge(S["v_ok"], t + 1)
                for k in range(DK):
                    ins = pe.matmul(kvp[k][:, 0:P + 1], kr[0:rows_n, b, k * P:(k + 1) * P], vv[0:rows_n, b, k, :], start=False, stop=last)
                ins.then_inc(S["kv_used"], 1)

            pe.sem_inc(S["kv_used"], 2)

            def batch(i, first=False):
                for j in range(NB):
                    t = i * NB + j
                    turn(t + 1, (j + 1) % NB)
                    project(t, j)
                    if not (first and j == 0):
                        sum_kv(t - 1, (j + 1) % 2)
            turn(0, 0)
            batch(0, True)
            with pe.Fori(1, NT // NB) as i:
                batch(i)
            project(NT - 1, 0)
            sum_kv(NT - 2, 1)
            sum_kv(NT - 1, 0, LAST, True)

            pe.wait_ge(S["kvm_ok"], 1)
            pe.sem_inc(S["slots"], RQ)
            pe.sem_inc(S["oh_slots"], OQ)
            with pe.register("held") as at_r, pe.register("pair") as pair_r:
                pe.reg_mov(at_r, 0)
                pe.reg_mov(pair_r, 1)

                def query(t):
                    pe.wait_ge(S["xt_in"], t * 16 + 16)
                    for m in range(DK):
                        for k in range(DK):
                            ins = pe.matmul(pQ[:, m * P:(m + 1) * P], wqs[:, k, m * P:(m + 1) * P], xtin[:, t % 2, k * P:(k + 1) * P],
                                            start=(k == 0), stop=(k == DK - 1))
                    ins.then_inc(S["q_ps"], 1)

                def read_out(t):
                    pe.wait_ge(S["qt_ok"], t + 1)
                    for k in range(DK):
                        ins = pe.matmul(pQ[:, k * (P + HB):(k + 1) * (P + HB)], qt[:, k * P:(k + 1) * P], kvm[:, k, :], start=True, stop=True)
                    ins.then_inc(S["att_ps"], 1)

                def load_span(t):
                    return pe.value_load(words[0:1, bass.ds(t, 1)], min_val=1, max_val=EQ * NT * PACK)

                def sum_rows(t, w):
                    lo = pe.snap(w // PACK)
                    last = pe.snap(lo + w % PACK - 1)
                    at = pe.snap(at_r)
                    with pe.If(at < lo):
                        with pe.Fori(at, lo) as f:
                            pe.wait_ge(S["relayed"], f + 1)
                            pe.sem_inc(S["slots"], 1)
                        pe.sem_inc(S["pe_hold"], 1)
                    pe.matmul(pA[:, :], zero16, any16, start=True, stop=False)
                    pe.matmul(pD[:, 0:1], zero16, any16[:, 0:1], start=True, stop=False)

                    def add(f, final):
                        n = pe.snap(pair_r)
                        pe.wait_ge(S["relayed"], f + 1)
                        pe.sem_inc(S["pe_hold"], 1)
                        pe.wait_ge(S["oh_ready"], n + 1)
                        for j in range(G):
                            stop = final and j == G - 1
                            m = pe.matmul(pA[:, :], onehot[:, n % OQ, j, :], gathered[:, (f % RQ) * G + j, :], start=False, stop=stop)
                            if j == G - 1 and not final:
                                m.then_inc(S["slots"], 1)
                            m = pe.matmul(pD[:, 0:1], onehot[:, n % OQ, j, :], ones16[:, 0:1], start=False, stop=stop)
                        m.then_inc(S["oh_slots"], 1)
                        pe.reg_add(pair_r, pair_r, 1)

                    with pe.If(lo < last):
                        with pe.Fori(lo, last) as f:
                            add(f, False)
                        pe.sem_inc(S["pe_hold"], 1)
                    add(last, True)
                    pe.matmul(pD[:, 1:2], zero16, any16[:, 0:1], start=True, stop=True).then_inc(S["agg_done"], 1)
                    pe.reg_mov(at_r, last)

                def gate_in(t):
                    pe.wait_ge(S["x2_ok"], t + 1)
                    for k in range(DK):
                        ins = pe.transpose(pH0[:, k * P:(k + 1) * P], x2[:, k * P:(k + 1) * P], ident[:, :])
                    ins.then_inc(S["x2t_ps"], 1)

                def gate(t):
                    pe.wait_ge(S["x2t_sb"], t + 1)
                    for k in range(DK):
                        ins = pe.matmul(pS[:, 0:NX], x2t[:, k * P:(k + 1) * P], gws[:, k, :], start=(k == 0), stop=(k == DK - 1))
                    ins.then_inc(S["lg_ps"], 1)

                def count(t):
                    pe.wait_ge(S["oh_ok"], t + 1)
                    pe.matmul(pS[:, NX:2 * NX], tri16, oh16[:, :], start=True, stop=False)
                    pe.matmul(pS[:, NX:2 * NX], ones16, cnt16[:, :], start=False, stop=True).then_inc(S["pos_ps"], 1)

                def node(t, first=False, final=False):
                    pe.wait_ge(S["o_ok"], t + 1)
                    for k in range(DK):
                        ins = pe.transpose(pH1[:, k * P:(k + 1) * P], o_sb[:, k * P:(k + 1) * P], ident[:, :])
                    ins.then_inc(S["ot_ps"], 1)
                    if not first:
                        gate_in(t - 1)
                    if not final:
                        query(t + 1)
                    pe.wait_ge(S["agg_ok"], t + 1)
                    for k in range(DK):
                        ins = pe.transpose(pT[:, k * P:(k + 1) * P], agg[:, k * P:(k + 1) * P], ident[:, :])
                    ins.then_inc(S["agt_ps"], 1)
                    if not first:
                        gate(t - 1)
                    pe.matmul(pY[:, 0:D], tri[0:1, :], bos[0:1, :], start=True, stop=False)
                    pe.wait_ge(S["ot_sb"], t + 1)
                    for k in range(DK):
                        pe.matmul(pY[:, 0:D], ot[:, k * P:(k + 1) * P], wos[:, k, :], start=False, stop=False)
                    pe.wait_ge(S["agt_sb"], t + 1)
                    for k in range(DK):
                        ins = pe.matmul(pY[:, 0:D], agt[:, k * P:(k + 1) * P], wgs[:, k, :], start=False, stop=(k == DK - 1))
                    ins.then_inc(S["x1_ps"], 1)
                    if not final:
                        w = load_span(t + 1)
                        read_out(t + 1)
                    if not first:
                        count(t - 1)
                    if not final:
                        sum_rows(t + 1, w)

                query(0)
                w = load_span(0)
                read_out(0)
                sum_rows(0, w)
                node(0, first=True)
                with pe.Fori(1, NT - 1) as t:
                    node(t)
                node(NT - 1, final=True)
                gate_in(NT - 1)
                pe.wait_ge(S["row_ok"], NT - 1)
                pe.sem_inc(S["pe_hold"], 1)
                gate(NT - 1)
                count(NT - 1)
                pe.wait_ge(S["row_ok"], NT)
                pe.matmul(pS[:, 0:NX], ones16, cnt16[:, :], start=True, stop=True).then_inc(S["plan_ps"], 1)

            pe.wait_ge(S["w_big"], 16 * 18)

            def columns(j):
                pe.wait_ge(S["xj_ok"], j + 1)
                for k in range(DK):
                    ins = pe.transpose(pT[:, k * P:(k + 1) * P], xj[:, k * P:(k + 1) * P], ident[:, :])
                ins.then_inc(S["xjt_ps"], 1)
            columns(0)

            def job(e, job_r):
                n = pe.snap(job_r)
                pe.wait_ge(S["xjt_sb"], n)
                for c in range(FC):
                    ph = (pH0, pH1)[c // 4]
                    for k in range(DK):
                        ins = pe.matmul(ph[:, (c % 4) * P:(c % 4 + 1) * P], w1s[:, e, k, c * P:(c + 1) * P],
                                        xjt[:, k * P:(k + 1) * P], start=(k == 0), stop=(k == DK - 1))
                    if c % 4 == 3:
                        ins.then_inc(S["h0_ps" if c == 3 else "h1_ps"], 1)
                columns(n)
                pe.wait_ge(S["y_used"], n)
                pe.sem_inc(S["pe_hold"], 1)
                for c in range(FC):
                    if c % 4 == 0:
                        pe.wait_ge(S["h0_sb" if c == 0 else "h1_sb"], n)
                    ins = pe.matmul(pY[:, 0:D], hs[:, c, :], w2s[:, e, c, :], start=(c == 0), stop=(c == FC - 1))
                ins.then_inc(S["y_ps"], 1)
            pe.wait_ge(S["plan_ok"], 1)
            with ExitStack() as regs:
                job_r = regs.enter_context(pe.register("job"))
                n_r = [regs.enter_context(pe.register(f"jobs{e}")) for e in range(NX)]
                pe.reg_mov(job_r, 1)
                pe.load(n_r, counts)
                for e in range(NX):
                    with pe.Fori(0, pe.snap(n_r[e])):
                        job(e, job_r)
                        pe.reg_add(job_r, job_r, 1)
                    pe.sem_inc(S["pe_hold"], 1)

        @block.vector
        def _(v):
            c = Chain(v, S["dve_c"])
            v.wait_ge(S["iota_ok"], 2)
            c.mark(v.tensor_copy(iota_row[:, :], iota_i[:, :]))
            c.mark(v.tensor_scalar(expert_m8[:, :], iota_i[:, 0:NX], float(-NX), None, ALU.add))
            c.mark(v.tensor_copy(chunk_id[:, :], chunk_i[:, :]))
            c.mark(v.memset(cnt16[:, :], 0.0))
            v.wait_ge(S["ident_ok"], 2)
            c.mark(v.tensor_copy(tri16, tri[:, :]))
            c.mark(v.memset(kvm[:, :, :], 0.0))
            c.mark(v.memset(new_row[:, :], 0.0))
            c.mark(v.memset(spans[:, :, :], 1 << 30))
            edges = xin[:, :, :, :].rearrange("p a b c -> p (a b c)").bitcast(I32)
            for a, name in ((0, "e_dst"), (1, "e_src")):
                v.wait_ge(S[name], 48)
                v.tensor_copy(xin_f(a).rearrange("p b e -> p (b e)"), edges[:, a * 1024:a * 1024 + EBLK * P]).then_inc(S["e_f32"], 1)
            v.wait_ge(S["e_f32"], 2)
            c.mark(v.tensor_reduce(cmin[:, :], xin_f(0), AX, ALU.min))
            c(v.tensor_reduce(cmax[:, :], xin_f(0), AX, ALU.max))
            for a, (b0, b1_) in enumerate(((pT, pQ), (pS, pY))):
                v.wait_ge(S["e_ps"], a + 1)
                t = (dst_t, src_t)[a]
                v.tensor_copy(t[:, 0:512], b0[:, :])
                v.tensor_copy(t[:, 512:ECP], b1_[:, 0:ECP - 512]).then_inc(S["e_copied"], 1)
            sel = xn[:, :, :].rearrange("p a b -> p (a b)")
            m0 = sel[:, 0:NT * EBLK].rearrange("p (t b) -> p t b", b=EBLK)
            m1 = sel[:, 512:512 + NT * EBLK].rearrange("p (t b) -> p t b", b=EBLK)
            thr = kk[:, 0:NT]
            c(v.tensor_scalar(thr, iota_row[:, 0:NT], float(P), None, ALU.mult))

            def wide(ap):
                return ap.rearrange("p (a b) -> p a b", a=1).broadcast_to([P, NT, EBLK])
            thr_w = thr.rearrange("p (t a) -> p t a", a=1).broadcast_to([P, NT, EBLK])
            c(v.tensor_tensor(m0, wide(cmax[:, :]), thr_w, ALU.is_ge))
            ids_lo, ids_hi = lg[:, 0, 0:EBLK], lg[:, 1, 0:EBLK]
            c.mark(v.tensor_scalar(ids_lo, chunk_id[:, :], -BIG, None, ALU.add))
            c.mark(v.tensor_scalar(ids_hi, chunk_id[:, :], 1.0, None, ALU.add))
            c(v.tensor_scalar(thr, thr, float(P), None, ALU.add))
            c(v.tensor_tensor(m1, wide(cmin[:, :]), thr_w, ALU.is_lt))
            c(v.tensor_tensor(m0, m0, wide(ids_lo), ALU.mult))
            c(v.tensor_tensor(m1, m1, wide(ids_hi), ALU.mult))
            c.mark(v.tensor_reduce(bounds[:, 0, :], m0, AX, ALU.min))
            c(v.tensor_reduce(bounds[:, 1, :], m1, AX, ALU.max))
            v.sem_inc(S["e_bound"], 1)
            v.wait_ge(S["e_bt"], 1)
            c.mark(v.tensor_reduce(lohi[:, 0:1], pS[0:NT, 0:P], AX, ALU.min))
            c(v.tensor_reduce(lohi[:, 1:2], pS[0:NT, P:2 * P], AX, ALU.max))
            c(v.tensor_scalar(lohi[:, 0:1], lohi[:, 0:1], BIG, float(EC - 1), ALU.add, ALU.min))
            c(v.tensor_scalar(new_col[:, :], lohi[:, 0:1], 1.0, None, ALU.add))
            c(v.tensor_tensor(lohi[:, 1:2], lohi[:, 1:2], new_col[:, :], ALU.max))
            c.mark(v.tensor_scalar(lohi[:, 0:1], lohi[:, 0:1], 1.0 / G, -(G - 1) / (2.0 * G), ALU.mult, ALU.add))
            c(v.tensor_scalar(lohi[:, 1:2], lohi[:, 1:2], 1.0 / G, (G - 1) / (2.0 * G), ALU.mult, ALU.add))
            c(v.tensor_scalar(lohi[:, :], lohi[:, :], 1.5 * 2.0 ** 23, None, ALU.add))
            c(v.tensor_scalar(lohi[:, :], lohi[:, :], -1.5 * 2.0 ** 23, None, ALU.add))
            v.sem_inc(S["e_lohi"], 1)
            v.wait_ge(S["e_rowps"], 1)
            c(v.tensor_copy(lh_row[0:1, :, 0:NT], pT[0:1, 0:2 * 64].rearrange("p (a t) -> p a t", a=2)[:, :, 0:NT]))
            c(v.scalar_tensor_tensor(new_row[0:1, 1:NT], lh_row[0:1, 1, 0:NT - 1], -1.0, lh_row[0:1, 0, 1:NT], ALU.add, ALU.is_gt))
            v.sem_inc(S["e_row"], 1)
            v.wait_ge(S["e_newps"], 1)
            c(v.tensor_copy(new_col[:, :], pS[0:NT, 0:1]))
            v.sem_inc(S["e_new"], 1)
            v.wait_ge(S["e_baseps"], 1)
            c(v.tensor_scalar(base_row[0:1, 0:NT], pT[0:1, 0:NT], float(EQ), None, ALU.mult))
            c.mark(v.tensor_tensor(new_row[0:1, 0:NT], lh_row[0:1, 1, 0:NT], lh_row[0:1, 0, 0:NT], ALU.subtract))
            c(v.tensor_tensor(lh_row[0:1, 0, 0:NT], lh_row[0:1, 0, 0:NT], base_row[0:1, 0:NT], ALU.add))
            c.mark(v.scalar_tensor_tensor(words[0:1, 0:NT], lh_row[0:1, 0, 0:NT], float(PACK), new_row[0:1, 0:NT], ALU.mult, ALU.add))
            c.mark(v.tensor_copy(ends[0:1, 0, :], lh_row[0:1, 0, 0:NT]))
            c.mark(v.tensor_tensor(ends[0:1, 2, :], lh_row[0:1, 0, 0:NT], new_row[0:1, 0:NT], ALU.add))
            c.mark(v.scalar_tensor_tensor(ends[0:1, 1, :], new_row[0:1, 0:NT], float(EARLY), lh_row[0:1, 0, 0:NT], ALU.min, ALU.add))
            c(v.tensor_scalar(rounds, base_row[0:1, NT - 1:NT], 1.0 / RQ, float(EB), ALU.mult, ALU.add))
            v.sem_inc(S["spans_ok"], 1)
            c0 = c.n

            K1 = 3

            def stats_(i, js):
                if js[0] == 0:
                    v.wait_ge(S["x_in"], i * 16 + 16)
                    hold(v, "dve_hold")
                for j in js:
                    ins = v.bn_stats(stats[:, j, :], xin[:, i % 2, j, :])
                return ins

            def moments(i, nb, ins):
                Chain(v, S["dve_c"], c0 + i * K1)(ins)
                hold(v, "dve_hold")
                for j in range(nb):
                    ins = v.bn_aggr(mv[:, j, :], stats[:, j, :])
                ins.then_inc(S["ln_stats"], 1)

            def invert(i, nb):
                v.wait_ge(S["ln_std"], i + 1)
                c = Chain(v, S["dve_c"], c0 + i * K1 + 1)
                c.mark(v.reciprocal(rstd2[:, bass.ds(i % 2 * NB, nb)], std[:, 0:nb]))
                c(v.tensor_copy(mean2[:, bass.ds(i % 2 * NB, nb)], mv[:, 0:nb, 0]))

            def norm(i, j):
                v.tensor_scalar(xn[:, j, :], xin[:, i % 2, j, :], mean2[:, bass.ds(i % 2 * NB + j, 1)], rstd2[:, bass.ds(i % 2 * NB + j, 1)],
                                ALU.subtract, ALU.mult).then_inc(S["ln_xn"], 1)

            def columns_out(t, j):
                v.wait_ge(S["xt_ps"], t + 1)
                v.tensor_copy(xt[:, j, :], pTS(j % 2)[:, 0:D]).then_inc(S["xt_sb"], 1)

            def keys(t, b):
                v.wait_ge(S["kv_ps"], t + 1)
                v.tensor_tensor(kb[:, b, :], pQY(b)[:, 0:D], bks[:, :], ALU.add).then_inc(S["kb_ok"], 1)

            def features(t, b):
                v.wait_ge(S["ke_ok"], t + 1)
                v.scalar_tensor_tensor(kr[:, b, :], kb[:, b, :], 1.0, kr[:, b, :], ALU.min, ALU.add).then_inc(S["kk_ok"], 1)

            def batch(i, nb, nb2, first=False):
                for j in range(NB):
                    t = i * NB + j
                    if j < nb:
                        v.wait_ge(S["ln_dif"], t + 1)
                        v.sem_inc(S["dve_hold"], 1)
                        norm(i + 1, j)
                    if j < NB - 1 and not first:
                        v.wait_ge(xt_st[j + 1], i * 16)
                        v.sem_inc(S["dve_hold"], 1)
                    if j == NB - 1:
                        v.wait_ge(xt_st[0], i * 16 + 16)
                        v.sem_inc(S["dve_hold"], 1)
                    columns_out(t + 1, (j + 1) % NB)
                    if not (first and j == 0):
                        features(t - 1, (j + 1) % 2)
                    keys(t, j % 2)
                    js = ((), (0, 1), (2, 3), ())[j][:nb2]
                    if js and js[0] < nb2:
                        last = stats_(i + 2, js)
                    if nb2 and j == 2:
                        moments(i + 2, nb2, last)
                if nb2:
                    invert(i + 2, nb2)

            moments(0, NB, stats_(0, range(NB)))
            invert(0, NB)
            for j in range(NB):
                norm(0, j)
            moments(1, NB, stats_(1, range(NB)))
            invert(1, NB)
            columns_out(0, 0)
            batch(0, NB, NB, True)
            with v.Fori(1, NT // NB - 2) as i:
                batch(i, NB, NB)
            batch(NT // NB - 2, NB, 1)
            batch(NT // NB - 1, 1, 0)
            keys(NT - 1, 0)
            features(NT - 2, 1)
            features(NT - 1, 0)
            c1 = c0 + (NT // NB + 1) * K1

            c = Chain(v, S["dve_c"], c1)
            v.wait_ge(S["kv_used"], NT + 2)
            for k in range(DK):
                ps = (pH0, pH1)[k]
                for h in range(HB):
                    r = slice(h * HD, (h + 1) * HD)
                    c.mark(v.tensor_copy(kvm[r, k, P + h:P + h + 1], ps[r, P:P + 1]))
            c.wait()
            for k in range(DK):
                ps = (pH0, pH1)[k]
                for h in range(HB):
                    r = slice(h * HD, (h + 1) * HD)
                    c.mark(v.scalar_tensor_tensor(kvm[r, k, h * HD:(h + 1) * HD], bvs[r, k * P + h * HD:k * P + (h + 1) * HD],
                                                  kvm[r, k, P + h:P + h + 1], ps[r, h * HD:(h + 1) * HD], ALU.mult, ALU.add))
            c.mark(v.tensor_copy(tile_iota[:, :], iota_row[:, :]))
            c(v.tensor_copy(tok[:, :], chunk_id[:, 0:1]))
            v.sem_inc(S["kvm_ok"], 1)
            v.sem_inc(S["xb_ok"], 1)
            v.sem_inc(S["row_stored"], RB)
            v.sem_inc(S["row_free"], RB - 1)
            v.sem_inc(S["fin_free"], 2)
            c2 = c1 + c.n

            K = {"agg_c": 4, "att_c": 2, "x1_c": 1, "norm_c": 2, "route_c": 4, "route2_c": 10, "tile_c": 1}

            def part(name, t):
                return Chain(v, S[name], t * K[name])

            with v.register("pair_v") as pair_r, v.register("first") as first_r, v.register("early_end") as mid_r, v.register("end") as end_r:
                v.reg_mov(pair_r, 1)

                def one_hots(lo, hi, wait=True):
                    with v.Fori(lo, hi) as ch:
                        n = v.snap(pair_r)
                        if wait:
                            v.wait_ge(S["oh_slots"], n)
                        v.tensor_tensor(onehot[:, n % OQ, :, :],
                                        tile_iota[:, :].rearrange("p (a n) -> p a n", a=1).broadcast_to([P, G, P]),
                                        dst_t[:, bass.ds(ch % EQ * G, G)].rearrange("p (g a) -> p g a", a=1).broadcast_to([P, G, P]),
                                        ALU.is_equal).then_inc(S["oh_ready"], 1)
                        v.reg_add(pair_r, pair_r, 1)

                def load_ends(t):
                    v.load((first_r, mid_r, end_r), ends[0:1, :, bass.ds(t, 1)])

                def early():
                    one_hots(v.snap(first_r), v.snap(mid_r), wait=False)

                def late():
                    mid, end = v.snap(mid_r), v.snap(end_r)
                    with v.If(mid < end):
                        one_hots(mid, end)
                        v.sem_inc(S["dve_hold"], 1)

                def queries(t):
                    v.wait_ge(S["qe_ok"], t + 1)
                    v.scalar_tensor_tensor(qt, qe, 1.0, qr, ALU.min, ALU.add).then_inc(S["qt_ok"], 1)

                def attend(t):
                    k = part("att_c", t)
                    v.wait_ge(S["att_ps"], t + 1)
                    att = pQ[:, 0:DK * (P + HB)].rearrange("p (k n) -> p k n", k=DK)
                    k(v.tensor_scalar(rden[:, :].rearrange("p (k h) -> p k h", k=DK), att[:, :, P:P + HB], 1e-6, None, ALU.add))
                    k(v.reciprocal(rden[:, :], rden[:, :]))
                    for m in range(DK):
                        ins = v.tensor_tensor(o_sb[:, m * P:(m + 1) * P].rearrange("p (h d) -> p h d", d=HD),
                                              att[:, m, 0:P].rearrange("p (h d) -> p h d", d=HD),
                                              rden[:, m * HB:(m + 1) * HB].rearrange("p (h a) -> p h a", a=1).broadcast_to([P, HB, HD]), ALU.mult)
                    ins.then_inc(S["o_ok"], 1)
                    assert k.n == K["att_c"]

                def mean(t, more):
                    k = part("agg_c", t)
                    v.wait_ge(S["agg_done"], t + 1)
                    k.mark(v.tensor_scalar(deg[:, 2:3], pD[:, 0:1], 1.0, None, ALU.min))
                    k.mark(v.tensor_scalar(deg[:, 0:1], pD[:, 0:1], 1.0, None, ALU.max))
                    k(v.tensor_scalar(deg[:, 1:2], pD[:, 0:1], 1.0, LO, ALU.max, ALU.mult))
                    v.reciprocal(rdeg[:, :], deg[:, 0:2]).then_inc(S["dg_ok"], 1)
                    if more:
                        load_ends(t + 1)
                    v.wait_ge(S["ahi_ok"], t + 1)
                    v.scalar_tensor_tensor(agg, pA[:, D:2 * D], rdeg[:, 1:2], ahi, ALU.mult, ALU.add).then_inc(S["agg_ok"], 1)
                    v.wait_ge(S["gb_ok"], t + 1)
                    v.sem_inc(S["dve_hold"], 1)
                    v.wait_ge(S["xr_in"], t * 16 + 16)
                    k(v.tensor_tensor(xb, xres[:, t % 2, :], gb, ALU.add))
                    v.sem_inc(S["xb_ok"], 1)
                    assert k.n == K["agg_c"]

                def residual(t):
                    k = part("x1_c", t)
                    v.wait_ge(S["row_stored"], t + 1)
                    v.sem_inc(S["dve_hold"], 1)
                    v.wait_ge(S["row_free"], t + 1)
                    v.sem_inc(S["dve_hold"], 1)
                    v.wait_ge(S["x1_ps"], t + 1)
                    v.tensor_tensor(rows_sb[:, t % RB, 0:D], pY[:, 0:D], xb, ALU.add).then_inc(S["x1_ok"], 1)
                    v.wait_ge(S["x1_ok"], t + 1)
                    hold(v, "dve_hold")
                    k(v.bn_stats(stats[:, 0, :], rows_sb[:, t % RB, 0:D]))
                    hold(v, "dve_hold")
                    v.bn_aggr(sc[:, 0:2], stats[:, 0, :]).then_inc(S["st_ok"], 1)
                    assert k.n == K["x1_c"]

                def scale(t):
                    k = part("norm_c", t)
                    v.wait_ge(S["sd_ok"], t + 1)
                    k(v.reciprocal(rn[:, 0:1], sc[:, 2:3]))
                    v.scalar_tensor_tensor(rn[:, 1:2], sc[:, 0:1], -1.0, rn[:, 0:1], ALU.mult, ALU.mult).then_inc(S["nm_ok"], 1)
                    v.wait_ge(S["nm_ok"], t + 1)
                    hold(v, "dve_hold")
                    k.mark(v.tensor_copy(rows_sb[:, t % RB, C_RSTD:C_NMR + 1], rn[:, :]))
                    assert k.n == K["norm_c"]

                def route(t):
                    k = part("route_c", t)
                    v.wait_ge(S["lg_ps"], t + 1)
                    k(v.tensor_tensor(lg[:, 0, :], pS[:, 0:NX], gbs[:, :], ALU.add))
                    k(v.tensor_reduce(sc[:, 3:4], lg[:, 0, :], AX, ALU.max))
                    v.tensor_scalar(sc[:, 4:5], sc[:, 3:4], -1.0, None, ALU.mult).then_inc(S["nmx_ok"], 1)
                    k(v.scalar_tensor_tensor(lg[:, 2, :], lg[:, 0, :], sc[:, 3:4], expert_m8[:, :], ALU.is_ge, ALU.mult))
                    k(v.tensor_reduce(sc[:, 6:7], lg[:, 2, :], AX, ALU.min))
                    v.tensor_scalar(oh16[:, :], expert_m8[:, :], sc[:, 6:7], None, ALU.is_equal).then_inc(S["oh_ok"], 1)
                    assert k.n == K["route_c"]

                def place(t):
                    k = part("route2_c", t)
                    v.wait_ge(S["ex_ok"], t + 1)
                    k.mark(v.reciprocal(rows_sb[:, t % RB, C_PRB:C_PRB + 1], sc[:, 5:6]))
                    v.wait_ge(S["pos_ps"], t + 1)
                    k(v.tensor_tensor(lg[:, 3, :], pS[:, NX:2 * NX], oh16[:, :], ALU.mult))
                    k.mark(v.tensor_reduce(sc[:, 7:8], lg[:, 3, :], AX, ALU.add))
                    k.mark(v.tensor_tensor(cnt16[:, :], cnt16[:, :], oh16[:, :], ALU.add))
                    k(v.tensor_scalar(sc[:, 8:9], sc[:, 6:7], float(SLOTS), float(NX * SLOTS - 1), ALU.mult, ALU.add))
                    k.mark(v.tensor_copy(rows_sb[:, t % RB, C_TOK:C_TOK + 1].bitcast(I32), tok[:, :]))
                    k.mark(v.tensor_scalar(sc[:, 9:10], sc[:, 7:8], float(CAP), BIG, ALU.is_gt, ALU.mult))
                    k(v.tensor_tensor(sc[:, 8:9], sc[:, 8:9], sc[:, 7:8], ALU.add))
                    k.mark(v.tensor_scalar(tok[:, :], tok[:, :], float(P), None, ALU.add))
                    k(v.tensor_tensor(row_at[:, bass.ds(t % RB, 1)], sc[:, 8:9], sc[:, 9:10], ALU.add))
                    assert k.n == K["route2_c"], k.n
                    v.sem_inc(S["row_ok"], 1)

                def node(t, first=False, final=False):
                    late()
                    mean(t, not final)
                    if not final:
                        v.wait_ge(S["oh_ready"], v.snap(pair_r))
                        v.sem_inc(S["dve_hold"], 1)
                        p = part("tile_c", t)
                        p(v.tensor_scalar(tile_iota[:, :], tile_iota[:, :], float(P), None, ALU.add))
                        queries(t + 1)
                    if not first:
                        route(t - 1)
                    if not final:
                        early()
                    residual(t)
                    if not first:
                        place(t - 1)
                    scale(t)
                    if not final:
                        attend(t + 1)

                v.sem_inc(S["oh_ready"], 1)
                load_ends(0)
                early()
                queries(0)
                attend(0)
                node(0, first=True)
                with v.Fori(1, NT - 1) as t:
                    node(t)
                node(NT - 1, final=True)
                route(NT - 1)
                place(NT - 1)

            c = Chain(v, S["dve_c"], c2)
            njobs, s1, s2, s3 = (lg[0:1, k, :] for k in range(4))
            v.wait_ge(S["plan_ps"], 1)
            c(v.tensor_scalar(njobs, pS[0:1, 0:NX], float(CAP), 1.0 / P, ALU.min, ALU.mult))
            c(v.tensor_scalar(njobs, njobs, (P - 1) / (2.0 * P), 1.5 * 2.0 ** 23, ALU.add, ALU.add))
            c(v.tensor_scalar(njobs, njobs, -1.5 * 2.0 ** 23, 1.0, ALU.add, ALU.max))
            for a, b, step in ((njobs, s1, 1), (s1, s2, 2), (s2, s3, 4)):
                c.mark(v.tensor_copy(b[0:1, 0:step], a[0:1, 0:step]))
                c(v.tensor_tensor(b[0:1, step:NX], a[0:1, step:NX], a[0:1, 0:NX - step], ALU.add))
            c.mark(v.tensor_copy(total, s3[0:1, NX - 1:NX]))
            c.mark(v.tensor_copy(counts, njobs))
            c(v.tensor_tensor(s1, s3, njobs, ALU.subtract))
            c(v.scalar_tensor_tensor(plan, s1, float(PACK), njobs, ALU.mult, ALU.add))
            v.sem_inc(S["plan_ok"], 1)
            c2 += c.n

            K3 = 7

            def columns(j):
                v.wait_ge(S["j_in"], j * 16 + 16)
                v.sem_inc(S["dve_hold"], 1)
                v.tensor_scalar(xj, jrow[:, j % JB, 0:D], jrow[:, j % JB, C_RSTD:C_RSTD + 1], jrow[:, j % JB, C_NMR:C_NMR + 1],
                                ALU.mult, ALU.add).then_inc(S["xj_ok"], 1)

            def job(e, n):
                row, half = (n + JB - 1) % JB, (n + 1) % 2
                k = Chain(v, S["dve_c"], c2 - K3 + n * K3)
                v.wait_ge(S["h1_ps"], n)
                for q in range(FC // 2, FC):
                    ins = v.tensor_scalar(hs[:, q, :], pH1[:, (q - FC // 2) * P:(q - FC // 2 + 1) * P],
                                          b1s[:, e * FC + q:e * FC + q + 1], 0.0, ALU.add, ALU.max)
                ins.then_inc(S["h1_sb"], 1)
                v.wait_ge(S["xjt_ps"], n + 1)
                v.sem_inc(S["dve_hold"], 1)
                columns(n + 1)
                v.wait_ge(S["y_ps"], n)
                v.tensor_tensor(y[:, 0, :], pY[:, 0:D], b2s[:, e, :], ALU.add).then_inc(S["y_used"], 1)
                v.wait_ge(S["y_used"], n + 1)
                hold(v, "dve_hold")
                k(v.tensor_scalar(y[:, 1, :], y[:, 0, :], jrow[:, row, C_PRB:C_PRB + 1], None, ALU.mult))
                k.mark(v.tensor_scalar(y[:, 2, :].bitcast(I32), y[:, 1, :], 0.0, 0.0, ALU.mult, ALU.is_equal))
                v.wait_ge(S["fin_free"], n)
                v.sem_inc(S["dve_hold"], 1)
                k.mark(v.tensor_scalar(fin[:, half, :], y[:, 1, :], 1.0e4, -1.0e4, ALU.min, ALU.max))
                k(v.tensor_tensor(y[:, 0, :], y[:, 1, :], y[:, 1, :], ALU.is_equal))
                k(v.tensor_tensor(y[:, 0, :], fin[:, half, :], y[:, 0, :], ALU.mult))
                hold(v, "dve_hold")
                k(v.copy_predicated(y[:, 0, :], y[:, 2, :].bitcast(I32), y[:, 1, :]))
                v.tensor_copy(jtok[:, bass.ds(half, 1)], jrow[:, row, C_TOK:C_TOK + 1].bitcast(I32))
                k(v.tensor_tensor(fin[:, half, :], y[:, 0, :], jrow[:, row, 0:D], ALU.add))
                assert k.n == K3, k.n
                v.sem_inc(S["fin_ok"], 1)
                v.sem_inc(S["j_free"], 1)

            v.sem_inc(S["y_used"], 1)
            v.sem_inc(S["j_free"], JB)
            columns(0)
            v.wait_ge(S["xjt_ps"], 1)
            columns(1)
            with ExitStack() as regs:
                job_r = regs.enter_context(v.register("job_v"))
                n_r = [regs.enter_context(v.register(f"jobs_v{e}")) for e in range(NX)]
                v.reg_mov(job_r, 1)
                v.load(n_r, counts)
                for e in range(NX):
                    with v.Fori(0, v.snap(n_r[e])):
                        job(e, v.snap(job_r))
                        v.reg_add(job_r, job_r, 1)
                    v.sem_inc(S["dve_hold"], 1)


_INS = ["x", "src", "dst", "L0_gnn_W", "L0_gnn_b", "L0_mix_wq", "L0_mix_bq", "L0_mix_wk", "L0_mix_bk", "L0_mix_wv", "L0_mix_bv",
        "L0_mix_wo", "L0_mix_bo", "L0_ffn_gate_w", "L0_ffn_gate_b", "L0_ffn_w1", "L0_ffn_b1", "L0_ffn_w2", "L0_ffn_b2"]
_OUTS = [((N, D), "float32")]


def kernel(**inputs):
    import numpy as _np
    import concourse.bacc as _bacc
    from concourse import mybir as _mybir
    from concourse.bass_utils import run_bass_kernel_spmd as _run

    nc = _bacc.Bacc("TRN2", target_bir_lowering=False, num_devices=1)
    arrays, args = {}, []
    for name in _INS:
        a = _np.ascontiguousarray(inputs[name])
        arrays[f"in_{name}_dram"] = a
        args.append(nc.dram_tensor(f"in_{name}_dram", a.shape, _mybir.dt.from_np(a.dtype), kind="ExternalInput").ap())
    for i, (shape, dtype) in enumerate(_OUTS):
        dt = _mybir.dt.from_np(_np.dtype(dtype))
        args.append(nc.dram_tensor(f"out_{i}_dram", shape, dt, kind="ExternalOutput").ap())
    gps_block(nc, *args)
    r = _run(nc, [arrays], core_ids=[0])
    got = tuple(r.results[0][f"out_{i}_dram"] for i in range(len(_OUTS)))
    return got[0]
```
